# Optimizing a Trainium2 kernel written in Bass

```python
import numpy as np
import jax
import jax.numpy as jnp

def _softmax(x, axis=-1):
    return jax.nn.softmax(x, axis=axis)

def _gelu(x):
    return jax.nn.gelu(x, approximate=True)

def _silu(x):
    return jax.nn.silu(x)

def _sigmoid(x):
    return jax.nn.sigmoid(x)

def _layernorm(x, axis=-1, eps=1e-05):
    m = jnp.mean(x, axis=axis, keepdims=True)
    v = jnp.var(x, axis=axis, keepdims=True)
    return (x - m) / jnp.sqrt(v + eps)

def _scatter_add(tgt, idx, src, axis=0):
    return tgt.at[idx].add(src)

def _segment_sum(src, seg, n):
    return jax.ops.segment_sum(src, seg, n)
kernel_name = 'mk_macaron_d1_jaxref_r4_a06285'

def setup_inputs(seed: int=0):
    np.random.seed(seed)
    _w = jnp.asarray

    def _L0_attn_setup():
        import jax, jax.numpy as jnp
        import numpy as np
        B, N, D, H = (2, 512, 256, 8)
        HD = D // H
        EPS = 1e-06

        def _interleave(a, b):
            return jnp.stack([a, b], axis=2).reshape(a.shape[0], 2 * a.shape[1], a.shape[2], a.shape[3])

        def _l2norm(x):
            return x / jnp.sqrt(jnp.sum(x * x, axis=-1, keepdims=True) + EPS)

        def _dense_rnn(x, Wq, Wk, Wv, Wf1, Wf2, Wbeta, Wog1, Wog2, norm_w, Wo):
            b, n, d = x.shape
            q = jax.nn.silu(x @ Wq)
            k = jax.nn.silu(x @ Wk)
            v = jax.nn.silu(x @ Wv)
            f = x @ Wf1 @ Wf2
            log_f = jax.nn.log_sigmoid(f)
            beta = jax.nn.sigmoid(x @ Wbeta) * 2.0
            shp = (b, n, H, HD)
            q, k, v, log_f = (t.reshape(shp) for t in (q, k, v, log_f))
            k = _l2norm(k)
            k_ = -beta[..., None] * k
            zero = jnp.zeros(shp, x.dtype)
            gk = _interleave(log_f, zero)
            a = _interleave(k_ * jnp.exp(log_f), k_)
            bb = _interleave(k, k)
            kk = _interleave(zero, k)
            vv = _interleave(zero, v)
            qq = _interleave(zero, q)
            seq = tuple((jnp.moveaxis(t, 1, 0) for t in (gk, a, bb, kk, vv, qq)))
            S0 = jnp.zeros((b, H, HD, HD), x.dtype)

            def step(S, inp):
                g, a_t, b_t, k_t, v_t, q_t = inp
                bS = jnp.einsum('bhk,bhkv->bhv', b_t, S)
                S = jnp.exp(g)[..., None] * S + a_t[..., None] * bS[:, :, None, :] + k_t[..., None] * v_t[:, :, None, :]
                o = jnp.einsum('bhk,bhkv->bhv', q_t, S)
                return (S, o)
            _, o = jax.lax.scan(step, S0, seq)
            o = jnp.moveaxis(o, 0, 1)[:, 1::2]
            out = o.reshape(b, n, d)
            gate = x @ Wog1 @ Wog2
            y = out * jax.nn.sigmoid(gate)
            yh = y.reshape(b, n, H, HD)
            yh = yh / jnp.sqrt(jnp.mean(yh * yh, axis=-1, keepdims=True) + EPS)
            y = yh.reshape(b, n, d) * norm_w
            return y @ Wo
        key = jax.random.key(seed)
        ks = jax.random.split(key, 11)
        std = 0.02
        w = lambda k, shape: jax.random.normal(k, shape, dtype=jnp.float32) * std
        return {'x': jax.random.normal(ks[0], (B, N, D), dtype=jnp.float32), 'Wq': w(ks[1], (D, D)), 'Wk': w(ks[2], (D, D)), 'Wv': w(ks[3], (D, D)), 'Wf1': w(ks[4], (D, HD)), 'Wf2': w(ks[5], (HD, D)), 'Wbeta': w(ks[6], (D, H)), 'Wog1': w(ks[7], (D, HD)), 'Wog2': w(ks[8], (HD, D)), 'norm_w': jnp.ones((D,), dtype=jnp.float32), 'Wo': w(ks[9], (D, D))}
    _L0_attn_in = _L0_attn_setup()

    def _L0_ffn_setup():
        import jax, jax.numpy as jnp
        import numpy as np
        TOPK = 2
        key = jax.random.key(seed)
        k0, k1, k2, k3 = jax.random.split(key, 4)
        B, S, H, I, E = (4, 512, 256, 512, 8)
        return {'hidden_states': jax.random.normal(k0, (B, S, H), dtype=jnp.float32), 'w1': jax.random.normal(k1, (E, 2 * I, H), dtype=jnp.float32) * 0.02, 'w2': jax.random.normal(k2, (E, H, I), dtype=jnp.float32) * 0.02, 'router_w': jax.random.normal(k3, (E, H), dtype=jnp.float32) * 0.02}
    _L0_ffn_in = _L0_ffn_setup()
    _d = {'L0_attn_x': _L0_attn_in['x'], 'L0_attn_Wq': _L0_attn_in['Wq'], 'L0_attn_Wk': _L0_attn_in['Wk'], 'L0_attn_Wv': _L0_attn_in['Wv'], 'L0_attn_Wf1': _L0_attn_in['Wf1'], 'L0_attn_Wf2': _L0_attn_in['Wf2'], 'L0_attn_Wbeta': _L0_attn_in['Wbeta'], 'L0_attn_Wog1': _L0_attn_in['Wog1'], 'L0_attn_Wog2': _L0_attn_in['Wog2'], 'L0_attn_norm_w': _L0_attn_in['norm_w'], 'L0_attn_Wo': _L0_attn_in['Wo'], 'L0_ffn_w1': _L0_ffn_in['w1'], 'L0_ffn_w2': _L0_ffn_in['w2'], 'L0_ffn_router_w': _L0_ffn_in['router_w']}
    _x0 = _d['L0_attn_x']
    _d['L0_attn_x'] = jax.random.normal(jax.random.fold_in(jax.random.key(seed), 1), (4, 1024, 256), dtype=_x0.dtype)
    del _x0
    return _d

def reference(L0_attn_x, L0_attn_Wq, L0_attn_Wk, L0_attn_Wv, L0_attn_Wf1, L0_attn_Wf2, L0_attn_Wbeta, L0_attn_Wog1, L0_attn_Wog2, L0_attn_norm_w, L0_attn_Wo, L0_ffn_w1, L0_ffn_w2, L0_ffn_router_w):

    def _L0_attn_ref(x, Wq, Wk, Wv, Wf1, Wf2, Wbeta, Wog1, Wog2, norm_w, Wo):
        import jax, jax.numpy as jnp
        import numpy as np
        B, N, D, H = (2, 512, 256, 8)
        HD = D // H
        EPS = 1e-06

        def _interleave(a, b):
            return jnp.stack([a, b], axis=2).reshape(a.shape[0], 2 * a.shape[1], a.shape[2], a.shape[3])

        def _l2norm(x):
            return x / jnp.sqrt(jnp.sum(x * x, axis=-1, keepdims=True) + EPS)

        def _dense_rnn(x, Wq, Wk, Wv, Wf1, Wf2, Wbeta, Wog1, Wog2, norm_w, Wo):
            b, n, d = x.shape
            q = jax.nn.silu(x @ Wq)
            k = jax.nn.silu(x @ Wk)
            v = jax.nn.silu(x @ Wv)
            f = x @ Wf1 @ Wf2
            log_f = jax.nn.log_sigmoid(f)
            beta = jax.nn.sigmoid(x @ Wbeta) * 2.0
            shp = (b, n, H, HD)
            q, k, v, log_f = (t.reshape(shp) for t in (q, k, v, log_f))
            k = _l2norm(k)
            k_ = -beta[..., None] * k
            zero = jnp.zeros(shp, x.dtype)
            gk = _interleave(log_f, zero)
            a = _interleave(k_ * jnp.exp(log_f), k_)
            bb = _interleave(k, k)
            kk = _interleave(zero, k)
            vv = _interleave(zero, v)
            qq = _interleave(zero, q)
            seq = tuple((jnp.moveaxis(t, 1, 0) for t in (gk, a, bb, kk, vv, qq)))
            S0 = jnp.zeros((b, H, HD, HD), x.dtype)

            def step(S, inp):
                g, a_t, b_t, k_t, v_t, q_t = inp
                bS = jnp.einsum('bhk,bhkv->bhv', b_t, S)
                S = jnp.exp(g)[..., None] * S + a_t[..., None] * bS[:, :, None, :] + k_t[..., None] * v_t[:, :, None, :]
                o = jnp.einsum('bhk,bhkv->bhv', q_t, S)
                return (S, o)
            _, o = jax.lax.scan(step, S0, seq)
            o = jnp.moveaxis(o, 0, 1)[:, 1::2]
            out = o.reshape(b, n, d)
            gate = x @ Wog1 @ Wog2
            y = out * jax.nn.sigmoid(gate)
            yh = y.reshape(b, n, H, HD)
            yh = yh / jnp.sqrt(jnp.mean(yh * yh, axis=-1, keepdims=True) + EPS)
            y = yh.reshape(b, n, d) * norm_w
            return y @ Wo
        return _dense_rnn(x, Wq, Wk, Wv, Wf1, Wf2, Wbeta, Wog1, Wog2, norm_w, Wo)

    def _L0_ffn_ref(hidden_states, w1, w2, router_w):
        import jax, jax.numpy as jnp
        import numpy as np
        TOPK = 2
        orig_shape = hidden_states.shape
        H = orig_shape[-1]
        E = w1.shape[0]
        I = w2.shape[-1]
        dtype = hidden_states.dtype
        x = hidden_states.reshape(-1, H)
        gating = x @ router_w.T
        probs = jax.nn.softmax(gating.astype(jnp.float32), axis=-1)
        topk_weights, selected_experts = jax.lax.top_k(probs, TOPK)
        topk_weights = topk_weights.astype(dtype)
        out = jnp.zeros_like(x)
        for e in range(E):
            ew = jnp.sum(topk_weights * (selected_experts == e), axis=-1, keepdims=True)
            h = x @ w1[e].T
            gate = jax.nn.silu(h[:, :I])
            y = h[:, I:] * gate @ w2[e].T
            out = out + y * ew
        return out.reshape(orig_shape)
    x = L0_attn_x
    x = x + 0.5 * _L0_ffn_ref(_layernorm(x, axis=-1), L0_ffn_w1, L0_ffn_w2, L0_ffn_router_w)
    x = x + _L0_attn_ref(_layernorm(x, axis=-1), L0_attn_Wq, L0_attn_Wk, L0_attn_Wv, L0_attn_Wf1, L0_attn_Wf2, L0_attn_Wbeta, L0_attn_Wog1, L0_attn_Wog2, L0_attn_norm_w, L0_attn_Wo)
    x = x + 0.5 * _L0_ffn_ref(_layernorm(x, axis=-1), L0_ffn_w1, L0_ffn_w2, L0_ffn_router_w)
    return x

_drawn_inputs = setup_inputs


def setup_inputs(seed=0):
    import zlib

    import numpy as np

    out = dict(_drawn_inputs(seed))
    spreads = {'L0_attn_norm_w': (1.0, 0.2)}
    factors = {'L0_attn_Wf1': 8.0,
     'L0_attn_Wf2': 8.0,
     'L0_attn_Wbeta': 23.453,
     'L0_attn_Wog1': 8.0,
     'L0_attn_Wog2': 8.0,
     'L0_ffn_w1': 8.0,
     'L0_ffn_w2': 8.0,
     'L0_ffn_router_w': 8.0}
    for name, (base, spread) in spreads.items():
        noise = np.random.default_rng([zlib.crc32(name.encode()), seed]).standard_normal(out[name].shape)
        drawn = base * np.exp(spread * noise) if base else spread * noise
        out[name] = jnp.asarray(drawn.astype(out[name].dtype))
    for name, factor in factors.items():
        out[name] = (out[name] * factor).astype(out[name].dtype)
    return out
```

```python
import numpy as np
from contextlib import ExitStack
import concourse.bass as bass
from concourse import mybir

F32 = mybir.dt.float32
I32 = mybir.dt.int32
U32 = mybir.dt.uint32
ALU = mybir.AluOpType
ACT = mybir.ActivationFunctionType
AX = mybir.AxisListType
P = 128

BATCH, SEQ, DIM = 4, 1024, 256
TOKENS = BATCH * SEQ
KCH = DIM // P
EXPERTS, INNER, TOPK = 8, 512, 2
TILES = TOKENS // P
ICH = INNER // P
LN_EPS = 1e-5
SLOTS = TOKENS * TOPK // P + EXPERTS
ROWS = SLOTS * P
XS_ROWS = ROWS + EXPERTS * P

HEADS, HD = 8, 32
HQ = P // HD
CHAINS = (HEADS // HQ) * BATCH
RANK = 32
EPS = 1e-6
CT = 16
SUB = 2 * CT
UN = 16
PT = CT * UN
PASSES = SEQ // PT
GS = CT + 1
LEVELS = (8, 4, 2, 1)
LW, RW = 16, 24
E_OFF = [0]
for _T in LEVELS:
    E_OFF.append(E_OFF[-1] + UN * (8 // _T) * 2 * (_T + 1))
HS = 33 * SUB
FG = 2 * RANK + HEADS


def clear(nc, sems):
    with nc.Block() as block:

        @block.sync
        def _(sp):
            for s in sems:
                sp.sem_clear(s)


def ffn_constants():
    c = {}
    c["ident"] = np.eye(P, dtype=np.float32)
    c["lower"] = np.triu(np.ones((P, P), np.float32), 1)
    c["ones"] = np.ones((P, P), np.float32)
    e = np.arange(EXPERTS)
    row = np.zeros((1, EXPERTS * EXPERTS + EXPERTS + TILES + SLOTS), np.float32)
    row[0, 0:64] = (e[None, :] < e[:, None]).astype(np.float32).ravel()
    row[0, 64:72] = ROWS + e * P
    row[0, 72:104] = np.arange(TILES) * P
    row[0, 104:] = np.arange(SLOTS)
    c["row"] = np.repeat(row, P, 0)
    c["part"] = np.arange(P, dtype=np.float32)[:, None].copy()
    return c


GOT = 8


def pool_dma_semaphores(nc, ctx, tag):
    names = ["scat", "store0", "store1"] + [f"got{i}" for i in range(GOT)]
    return {n: ctx.enter_context(nc.semaphore(f"{tag}_{n}")) for n in names}


def ffn(nc, tag, x_in, x_out, w1t, w2t, rwt, cst, xs, ys, pool_sems):
    with ExitStack() as ctx:
        def sb(name, shape, dt=F32):
            return ctx.enter_context(nc.sbuf_tensor(f"{tag}_{name}", shape, dt))

        sems = []

        def sem(name):
            if name in pool_sems:
                return pool_sems[name]
            sems.append(ctx.enter_context(nc.semaphore(f"{tag}_{name}")))
            return sems[-1]

        psum = [ctx.enter_context(nc.psum_tensor(f"{tag}_bank{i}", [P, 512], F32)) for i in range(8)]

        w1 = sb("w1", [P, EXPERTS * KCH * 2 * INNER])
        w2 = sb("w2", [P, EXPERTS * ICH * DIM])
        rw = sb("rw", [P, KCH, EXPERTS])
        ident = sb("ident", [P, P])
        xr = sb("xr", [P, TILES, DIM])
        xn = sb("xn", [P, TILES, DIM])
        wtop = sb("wtop", [P, TOPK, TILES])
        slot_u = sb("slot_u", [P, TOPK, TILES], U32)
        tab_i = sb("tab_i", [1, SLOTS], I32)

        x_view = x_in.rearrange("(i p) d -> p i d", p=P)
        o_view = x_out.rearrange("(i p) d -> p i d", p=P)
        XG = 4
        TG = TILES // XG

        s_x = [sem(f"x{g}") for g in range(XG)]
        s_cst, s_w = sem("cst"), sem("w")

        with ExitStack() as rctx:
            def rb(name, shape, dt=F32):
                return rctx.enter_context(nc.sbuf_tensor(f"{tag}_{name}", shape, dt))

            lower, ones = rb("lower", [P, P]), rb("ones", [P, P])
            row, part = rb("row", [P, cst["row"].shape[1]]), rb("part", [P, 1])
            stats = rb("stats", [P, TILES, 6])
            mean, var, rstd = rb("mean", [P, TILES]), rb("var", [P, TILES]), rb("rstd", [P, TILES])
            dm = rb("dm", [P, TILES])
            xt = [rb(f"xt{i}", [P, KCH, P]) for i in range(2)]
            prob = rb("prob", [P, TILES, EXPERTS])
            tmax, tsum = rb("tmax", [P, TILES]), rb("tsum", [P, TILES])
            beats, ties = rb("beats", [P, TILES * 64]), rb("ties", [P, TILES * 64])
            rank = rb("rank", [P, TILES, EXPERTS])
            sel = rb("sel", [P, TOPK, TILES, EXPERTS])
            both = rb("both", [P, TILES, EXPERTS])
            slot = rb("slot", [P, TILES, EXPERTS])
            upto = rb("upto", [P, EXPERTS, TILES])
            pick = rb("pick", [P, TILES, EXPERTS])
            slot_f = rb("slot_f", [P, TOPK, TILES])
            need = rb("need", [P, EXPERTS, 32])
            ntile, tend, tbeg = rb("ntile", [P, EXPERTS]), rb("tend", [P, EXPERTS]), rb("tbeg", [P, EXPERTS])
            tail, tail_ok, tail_d = rb("tail", [P, EXPERTS]), rb("tail_ok", [P, EXPERTS]), rb("tail_d", [P, EXPERTS])
            tail_u = rb("tail_u", [P, EXPERTS], U32)
            base = rb("base", [P, EXPERTS])
            done, tab_f = rb("done", [1, SLOTS, EXPERTS]), rb("tab_f", [1, SLOTS])
            zeros = rb("zeros", [P, DIM])
            s_zero, s_spare = sem("zero"), sem("spare")

            s_stat, s_var, s_std = sem("stat"), sem("var"), sem("std")
            s_xn, s_tr, s_xt, s_gate = sem("xn"), sem("tr"), sem("xt"), sem("gate")
            s_dve = sem("dve")
            s_sub, s_exp = sem("sub"), sem("exp")
            s_both, s_cnt = sem("both"), sem("cnt")
            s_slots, s_tails, s_tab = sem("slots"), sem("tails"), sem("tab")
            s_scat = sem("scat")

            LT = row[:, 0:64]
            DUMPS, STEPS, COUNT = row[:, 64:72], row[:, 72:104], row[:, 104:]

            with nc.Block() as block:

                @block.sync
                def _(sp):
                    for g in range(XG):
                        sp.dma_start(xr[:, g * TG:(g + 1) * TG, :], x_view[:, g * TG:(g + 1) * TG, :]).then_inc(s_x[g], 16)
                    for dst, src in ((ident, "ident"), (lower, "lower"), (ones, "ones"), (row, "row"), (part, "part")):
                        sp.dma_start(dst[:, :], cst[src]).then_inc(s_cst, 16)
                    sp.dma_start(rw[:, :, :], rwt).then_inc(s_cst, 16)
                    sp.wait_ge(s_zero, 1)
                    for m in range(SLOTS - EXPERTS, SLOTS):
                        sp.dma_start(xs[m * P:(m + 1) * P, :], zeros[:, :]).then_inc(s_spare, 16)
                    for e in range(EXPERTS):
                        sp.dma_start(w1[:, e * 2048:(e + 1) * 2048].rearrange("p (k f) -> p k f", k=KCH), w1t[e]).then_inc(s_w, 16)
                        sp.dma_start(w2[:, e * 1024:(e + 1) * 1024].rearrange("p (k f) -> p k f", k=ICH), w2t[e]).then_inc(s_w, 16)

                @block.vector
                def _(dve):
                    n = [0]

                    def link(ins):
                        n[0] += 1
                        ins.then_inc(s_dve, 1)
                        dve.wait_ge(s_dve, n[0])

                    dve.memset(zeros[:, :], 0.0).then_inc(s_zero, 1)
                    for g in range(XG):
                        dve.wait_ge(s_x[g], 16)
                        with dve.Fori(g * TG, (g + 1) * TG) as i:
                            dve.bn_stats(stats[:, bass.ds(i, 1), :], xr[:, bass.ds(i, 1), :]).then_inc(s_stat, 1)
                    dve.wait_ge(s_stat, TILES)
                    link(dve.tensor_tensor(mean[:, :], stats[:, :, 1], stats[:, :, 4], ALU.add))
                    link(dve.tensor_tensor(dm[:, :], stats[:, :, 1], stats[:, :, 4], ALU.subtract))
                    link(dve.tensor_tensor(var[:, :], stats[:, :, 2], stats[:, :, 5], ALU.add))
                    link(dve.tensor_tensor(dm[:, :], dm[:, :], dm[:, :], ALU.mult))
                    link(dve.tensor_scalar(mean[:, :], mean[:, :], 0.5, None, ALU.mult))
                    link(dve.tensor_scalar(var[:, :], var[:, :], 1.0 / DIM, LN_EPS, ALU.mult, ALU.add))
                    dve.scalar_tensor_tensor(out=var[:, :], in0=dm[:, :], scalar=0.25, in1=var[:, :],
                                             op0=ALU.mult, op1=ALU.add).then_inc(s_var, 1)
                    dve.wait_ge(s_std, 1)
                    link(dve.reciprocal(rstd[:, :], rstd[:, :]))
                    with dve.Fori(0, TILES) as i:
                        dve.tensor_scalar(xn[:, bass.ds(i, 1), :], xr[:, bass.ds(i, 1), :], mean[:, bass.ds(i, 1)],
                                          rstd[:, bass.ds(i, 1)], ALU.subtract, ALU.mult).then_inc(s_xn, 1)
                    logits = psum[2][:, 0:TILES * EXPERTS].rearrange("p (i e) -> p i e", e=EXPERTS)
                    dve.wait_ge(s_gate, TILES)
                    link(dve.tensor_reduce(tmax[:, :], logits, AX.X, ALU.max))
                    dve.tensor_tensor(prob[:, :, :], logits, tmax[:, :].unsqueeze(2).to_broadcast([P, TILES, EXPERTS]),
                                      ALU.subtract).then_inc(s_sub, 1)
                    dve.wait_ge(s_exp, 1)
                    link(dve.tensor_reduce(tsum[:, :], prob[:, :, :], AX.X, ALU.add))
                    link(dve.reciprocal(tsum[:, :], tsum[:, :]))
                    link(dve.tensor_tensor(prob[:, :, :], prob[:, :, :],
                                           tsum[:, :].unsqueeze(2).to_broadcast([P, TILES, EXPERTS]), ALU.mult))
                    def cube(t):
                        return t[:, :].rearrange("p (i e f) -> p i e f", e=EXPERTS, f=EXPERTS)
                    other = prob[:, :, :].unsqueeze(2).to_broadcast([P, TILES, EXPERTS, EXPERTS])
                    mine = prob[:, :, :].unsqueeze(3).to_broadcast([P, TILES, EXPERTS, EXPERTS])
                    dve.tensor_tensor(cube(beats), other, mine, ALU.is_gt)
                    link(dve.tensor_tensor(cube(ties), other, mine, ALU.is_equal))
                    link(dve.tensor_tensor(ties[:, :].rearrange("p (i f) -> p i f", f=64), ties[:, :].rearrange("p (i f) -> p i f", f=64),
                                           LT.unsqueeze(1).to_broadcast([P, TILES, 64]), ALU.mult))
                    link(dve.tensor_tensor(beats[:, :], beats[:, :], ties[:, :], ALU.add))
                    link(dve.tensor_reduce(rank[:, :, :], cube(beats), AX.X, ALU.add))
                    for c in range(TOPK):
                        dve.tensor_scalar(sel[:, c, :, :], rank[:, :, :], float(c), None, ALU.is_equal)
                    dve.tensor_scalar(both[:, :, :], rank[:, :, :], float(TOPK), None, ALU.is_lt).then_inc(s_both, 1)
                    dve.wait_ge(s_cnt, 2)
                    totals = psum[4][:, 0:TILES * EXPERTS].rearrange("p (i e) -> p e i", e=EXPERTS)
                    before = psum[3][:, 0:TILES * EXPERTS].rearrange("p (i e) -> p i e", e=EXPERTS)
                    for e in range(EXPERTS):
                        last = dve.tensor_tensor_scan(upto[:, e, :], ones[:, 0:TILES], totals[:, e, :], 0.0, ALU.mult, ALU.add)
                    link(last)
                    cnt = upto[:, :, TILES - 1]
                    link(dve.tensor_tensor(need[:, :, :], cnt.unsqueeze(2).to_broadcast([P, EXPERTS, TILES]),
                                           STEPS.unsqueeze(1).to_broadcast([P, EXPERTS, TILES]), ALU.is_gt))
                    link(dve.tensor_reduce(ntile[:, :], need[:, :, :], AX.X, ALU.add))
                    link(dve.tensor_tensor_scan(tend[:, :], ones[:, 0:EXPERTS], ntile[:, :], 0.0, ALU.mult, ALU.add))
                    link(dve.tensor_tensor(tbeg[:, :], tend[:, :], ntile[:, :], ALU.subtract))
                    link(dve.tensor_scalar(base[:, :], tbeg[:, :], float(P), None, ALU.mult))
                    link(dve.tensor_tensor(slot[:, :, :], upto[:, :, :].rearrange("p e i -> p i e"), totals.rearrange("p e i -> p i e"), ALU.subtract))
                    link(dve.tensor_tensor(slot[:, :, :], slot[:, :, :], before, ALU.add))
                    link(dve.tensor_tensor(slot[:, :, :], slot[:, :, :], base[:, :].unsqueeze(1).to_broadcast([P, TILES, EXPERTS]), ALU.add))
                    for c in range(TOPK):
                        link(dve.tensor_tensor(pick[:, :, :], sel[:, c, :, :], slot[:, :, :], ALU.mult))
                        link(dve.tensor_reduce(slot_f[:, c, :], pick[:, :, :], AX.X, ALU.add))
                    link(dve.tensor_copy(slot_u[:, :, :], slot_f[:, :, :]))
                    link(dve.tensor_scalar(tail[:, :], cnt, part[:, 0:1], None, ALU.add))
                    link(dve.scalar_tensor_tensor(out=tail_ok[:, :], in0=ntile[:, :], scalar=float(P), in1=tail[:, :],
                                                  op0=ALU.mult, op1=ALU.is_gt))
                    link(dve.tensor_tensor(tail[:, :], tail[:, :], base[:, :], ALU.add))
                    link(dve.tensor_scalar(tail_d[:, :], DUMPS, part[:, 0:1], None, ALU.add))
                    link(dve.tensor_tensor(tail[:, :], tail[:, :], tail_d[:, :], ALU.subtract))
                    link(dve.tensor_tensor(tail[:, :], tail[:, :], tail_ok[:, :], ALU.mult))
                    link(dve.tensor_tensor(tail[:, :], tail[:, :], tail_d[:, :], ALU.add))
                    dve.tensor_copy(tail_u[:, :], tail[:, :]).then_inc(s_slots, 1)
                    big = [1, SLOTS, EXPERTS]
                    link(dve.tensor_tensor(done[:, :, :], COUNT[0:1, :].unsqueeze(2).to_broadcast(big),
                                           tend[0:1, :].unsqueeze(1).to_broadcast(big), ALU.is_ge))
                    link(dve.tensor_reduce(tab_f[:, :], done[:, :, :], AX.X, ALU.add))
                    link(dve.tensor_scalar(tab_f[:, :], tab_f[:, :], float(EXPERTS - 1), None, ALU.min))
                    dve.tensor_copy(tab_i[:, :], tab_f[:, :]).then_inc(s_tab, 1)
                    for c in range(TOPK):
                        link(dve.tensor_tensor(pick[:, :, :], sel[:, c, :, :], prob[:, :, :], ALU.mult))
                        link(dve.tensor_reduce(wtop[:, c, :], pick[:, :, :], AX.X, ALU.add))
                    link(dve.tensor_scalar(wtop[:, :, :], wtop[:, :, :], 0.5, None, ALU.mult))

                @block.scalar
                def _(act):
                    act.wait_ge(s_var, 1)
                    act.activation(rstd[:, :], var[:, :], ACT.Sqrt).then_inc(s_std, 1)
                    with act.Fori(0, TILES // 2) as j:
                        for b in range(2):
                            act.wait_ge(s_tr, 2 * j + b + 1)
                            act.copy(xt[b][:, :, :].rearrange("p k t -> p (k t)"), psum[b][:, 0:DIM]).then_inc(s_xt, 1)
                    act.wait_ge(s_sub, 1)
                    act.activation(prob[:, :, :], prob[:, :, :], ACT.Exp).then_inc(s_exp, 1)

                @block.tensor
                def _(pe):
                    pe.wait_ge(s_cst, 96)
                    def turn(i, b):
                        pe.wait_ge(s_xn, i + 1)
                        for k in range(KCH):
                            t = pe.transpose(psum[b][:, k * P:(k + 1) * P], xn[:, bass.ds(i, 1), k * P:(k + 1) * P].rearrange("p a t -> p (a t)")
                                             if not isinstance(i, int) else xn[:, i, k * P:(k + 1) * P], ident[:, :])
                        t.then_inc(s_tr, 1)

                    def gate(i, b):
                        pe.wait_ge(s_xt, i + 1)
                        for k in range(KCH):
                            g = pe.matmul(psum[2][:, bass.ds(i * EXPERTS, EXPERTS)], xt[b][:, k, :], rw[:, k, :],
                                          start=(k == 0), stop=(k == KCH - 1))
                        g.then_inc(s_gate, 1)
                    for i in range(TILES):
                        turn(i, i % 2)
                        if i > 0:
                            gate(i - 1, (i - 1) % 2)
                    gate(TILES - 1, (TILES - 1) % 2)
                    pe.wait_ge(s_both, 1)
                    flat = both[:, :, :].rearrange("p i e -> p (i e)")
                    pe.matmul(psum[3][:, 0:TILES * EXPERTS], lower[:, :], flat, start=True, stop=True).then_inc(s_cnt, 1)
                    pe.matmul(psum[4][:, 0:TILES * EXPERTS], ones[:, :], flat, start=True, stop=True).then_inc(s_cnt, 1)

                @block.gpsimd
                def _(pool):
                    pool.wait_ge(s_slots, 1)
                    pool.wait_ge(s_spare, 16 * EXPERTS)
                    for e in range(EXPERTS):
                        pool.indirect_dma_start(xs, bass.IndirectOffsetOnAxis(ap=tail_u[:, e:e + 1], axis=0), zeros[:, :], None).then_inc(s_scat, 16)
                    pool.wait_ge(s_xn, TILES)
                    for i in range(TILES):
                        for c in range(TOPK):
                            pool.indirect_dma_start(xs, bass.IndirectOffsetOnAxis(ap=slot_u[:, c, i:i + 1], axis=0),
                                                    xn[:, i, :], None).then_inc(s_scat, 16)
                    pool.wait_ge(s_scat, 16 * (EXPERTS + TOPK * TILES))

        with ExitStack() as ectx:
            def eb(name, shape, dt=F32):
                return ectx.enter_context(nc.sbuf_tensor(f"{tag}_{name}", shape, dt))

            rows = [eb(f"rows{i}", [P, DIM]) for i in range(2)]
            rowsT = [eb(f"rowsT{i}", [P, KCH * P]) for i in range(2)]
            gate = [eb(f"gate{i}", [P, INNER]) for i in range(2)]
            actT = [eb(f"actT{i}", [P, ICH * P]) for i in range(2)]
            yout = [eb(f"yout{i}", [P, DIM]) for i in range(2)]
            p_x = [psum[0][:, 0:DIM], psum[1][:, 0:DIM]]
            p_g, p_u = [psum[2], psum[3]], [psum[4], psum[5]]
            p_t = p_g
            p_y = [psum[6][:, 0:DIM], psum[7][:, 0:DIM]]

            s_in = [sem(f"in{i}") for i in range(2)]
            s_store = [sem(f"store{i}") for i in range(2)]
            s_xT, s_xTs = sem("xT"), sem("xTs")
            s_g, s_u, s_silu, s_act = sem("g"), sem("u"), sem("silu"), sem("act")
            s_aT, s_aTs, s_y, s_ys = sem("aT"), sem("aTs"), sem("y"), sem("ys")

            with nc.Block() as block:

                @block.sync
                def _(sp):
                    def load(m, j, b):
                        if j is not None:
                            sp.wait_ge(s_xT, m - 1)
                        sp.dma_start(rows[b][:, :], xs[bass.ds(m * P, P), :]).then_inc(s_in[b], 16)
                    for b in range(2):
                        load(b, None, b)
                    with sp.Fori(1, SLOTS // 2) as j:
                        for b in range(2):
                            load(2 * j + b, j, b)

                @block.tensor
                def _(pe):
                    pe.wait_ge(s_w, 16 * 2 * EXPERTS)

                    def turn_rows(m, j, b):
                        pe.wait_ge(s_in[b], 16 * j + 16)
                        if not (isinstance(m, int) and m < 2):
                            pe.wait_ge(s_xTs, m - 1)
                        for k in range(KCH):
                            t = pe.transpose(p_x[b][:, k * P:(k + 1) * P], rows[b][:, k * P:(k + 1) * P], ident[:, :])
                        t.then_inc(s_xT, 1)

                    def up(m, b, e, half):
                        if half == 0:
                            pe.wait_ge(s_xTs, m + 1)
                            if not (isinstance(m, int) and m < 2):
                                pe.wait_ge(s_aTs, m - 1)
                        bank = (p_g if half == 0 else p_u)[b]
                        for k in range(KCH):
                            t = pe.matmul(bank[:, :], rowsT[b][:, k * P:(k + 1) * P],
                                          w1[:, bass.ds(e * 2048 + (k * 1024 + half * INNER), INNER)],
                                          start=(k == 0), stop=(k == KCH - 1))
                        t.then_inc(s_g if half == 0 else s_u, 1)

                    def turn_act(m, b):
                        pe.wait_ge(s_act, m + 1)
                        for k in range(ICH):
                            t = pe.transpose(p_t[b][:, k * P:(k + 1) * P], gate[b][:, k * P:(k + 1) * P], ident[:, :])
                        t.then_inc(s_aT, 1)

                    def down(m, b, e):
                        pe.wait_ge(s_aTs, m + 1)
                        if not (isinstance(m, int) and m < 2):
                            pe.wait_ge(s_ys, m - 1)
                        for k in range(ICH):
                            t = pe.matmul(p_y[b], actT[b][:, k * P:(k + 1) * P],
                                          w2[:, bass.ds(e * 1024 + k * DIM, DIM)],
                                          start=(k == 0), stop=(k == ICH - 1))
                        t.then_inc(s_y, 1)

                    def expert(m):
                        return pe.value_load(tab_i[0:1, bass.ds(m, 1)], min_val=0, max_val=EXPERTS - 1)

                    def step(j, b, last=False):
                        m = 2 * j + b
                        first = isinstance(m, int) and m == 0
                        if not last:
                            turn_rows(m + 1, j + (b == 1), 1 - b)
                        e = expert(m)
                        up(m, b, e, 0)
                        if not first:
                            turn_act(m - 1, 1 - b)
                        up(m, b, e, 1)
                        if not first:
                            down(m - 1, 1 - b, expert(m - 1))

                    turn_rows(0, 0, 0)
                    step(0, 0)
                    step(0, 1)
                    with pe.Fori(1, SLOTS // 2 - 1) as j:
                        step(j, 0)
                        step(j, 1)
                    step(SLOTS // 2 - 1, 0)
                    step(SLOTS // 2 - 1, 1, last=True)
                    turn_act(SLOTS - 1, 1)
                    down(SLOTS - 1, 1, expert(SLOTS - 1))

                @block.scalar
                def _(act):
                    def step(j, b, lag):
                        m = 2 * j + b
                        first = isinstance(m, int) and m < 2
                        act.wait_ge(s_xT, m + 1)
                        if not first:
                            act.wait_ge(s_u, m - 1)
                        act.copy(rowsT[b][:, :], p_x[b]).then_inc(s_xTs, 1)
                        act.wait_ge(s_g, m + 1)
                        if not first:
                            act.wait_ge(s_aT, m - 1)
                        act.activation(gate[b][:, :], p_g[b][:, :], ACT.Silu).then_inc(s_silu, 1)
                    for b in range(2):
                        step(0, b, None)
                    with act.Fori(1, SLOTS // 2) as j:
                        for b in range(2):
                            step(j, b, None)

                @block.vector
                def _(dve):
                    def step(j, b):
                        m = 2 * j + b
                        first = isinstance(m, int) and m < 2
                        dve.wait_ge(s_silu, m + 1)
                        dve.wait_ge(s_u, m + 1)
                        dve.tensor_tensor(gate[b][:, :], gate[b][:, :], p_u[b][:, :], ALU.mult).then_inc(s_act, 1)
                        dve.wait_ge(s_aT, m + 1)
                        if not first:
                            dve.wait_ge(s_y, m - 1)
                        dve.tensor_copy(actT[b][:, :], p_t[b][:, :]).then_inc(s_aTs, 1)
                        dve.wait_ge(s_y, m + 1)
                        if not first:
                            dve.wait_ge(s_store[b], 16 * j)
                        dve.tensor_copy(yout[b][:, :], p_y[b]).then_inc(s_ys, 1)
                    for b in range(2):
                        step(0, b)
                    with dve.Fori(1, SLOTS // 2) as j:
                        for b in range(2):
                            step(j, b)

                @block.gpsimd
                def _(pool):
                    with pool.Fori(0, SLOTS // 2) as j:
                        for b in range(2):
                            m = 2 * j + b
                            pool.wait_ge(s_ys, m + 1)
                            pool.dma_start(ys[bass.ds(m * P, P), :], yout[b][:, :]).then_inc(s_store[b], 16)
                    for b in range(2):
                        pool.wait_ge(s_store[b], 16 * (SLOTS // 2))

            s_got = [sem(f"got{i}") for i in range(GOT)]
            s_sum, s_o = sem("sum"), sem("o")
            got2 = eb("got2", [P, GOT, DIM])
            with nc.Block() as block:

                @block.gpsimd
                def _(pool):
                    for i in range(TILES):
                        if i >= GOT:
                            pool.wait_ge(s_sum, 2 * (i - GOT) + 2)
                        for c, dst in enumerate((xn[:, i, :], got2[:, i % GOT, :])):
                            pool.indirect_dma_start(dst, None, ys, bass.IndirectOffsetOnAxis(ap=slot_u[:, c, i:i + 1], axis=0)).then_inc(s_got[i % GOT], 16)

                @block.vector
                def _(dve):
                    for i in range(TILES):
                        dve.wait_ge(s_got[i % GOT], 32 * (i // GOT + 1))
                        for c, src in enumerate((xn[:, i, :], got2[:, i % GOT, :])):
                            dve.scalar_tensor_tensor(out=xr[:, i, :], in0=src, scalar=wtop[:, c, i:i + 1], in1=xr[:, i, :],
                                                     op0=ALU.mult, op1=ALU.add).then_inc(s_sum, 1)
                            if c == 0:
                                dve.wait_ge(s_sum, 2 * i + 1)

                @block.sync
                def _(sp):
                    for g in range(TILES // 2):
                        sp.wait_ge(s_sum, 4 * (g + 1))
                        sp.dma_start(o_view[:, 2 * g:2 * g + 2, :], xr[:, 2 * g:2 * g + 2, :]).then_inc(s_o, 16)
                    sp.wait_ge(s_o, 16 * (TILES // 2))
        clear(nc, sems)


def attn_constants():
    c = {}
    p = np.arange(P)
    c["headsum"] = (p[:, None] // HD == p[None, :] // HD).astype(np.float32)
    hc = np.zeros((P, HD), np.float32)
    hc[p, p // HD] = 1.0
    c["headcol"] = hc
    sel = np.zeros((HEADS, 2, P), np.float32)
    for g in range(2):
        sel[g * HQ + p // HD, g, p] = -1.0
    c["negsel"] = sel.reshape(HEADS, 2 * P)
    return c


def attn(nc, x_in, x_out, w, cst, v_scr, g_scr, o_scr, t_scr):
    with ExitStack() as ctx:
        def sb(name, shape, dt=F32, at=ctx):
            return at.enter_context(nc.sbuf_tensor(f"at_{name}", shape, dt))

        sems, kept = [], []

        def sem(name, keep=False):
            s = ctx.enter_context(nc.semaphore(f"at_{name}"))
            (kept if keep else sems).append(s)
            return s

        psum = [ctx.enter_context(nc.psum_tensor(f"at_bank{i}", [P, 512], F32)) for i in range(8)]

        wq, wk, wv = (sb(n, [P, KCH, DIM]) for n in ("wq", "wk", "wv"))
        wcat = sb("wcat", [P, KCH, FG])
        wrank = sb("wrank", [P, DIM])
        ident, headsum, headcol = sb("ident", [P, P]), sb("headsum", [P, P]), sb("headcol", [P, HD])
        epsk = sb("epsk", [P, 1])
        mask = sb("mask", [P, UN * GS])
        k, q, kb = (sb(n, [P, CHAINS, PT]) for n in ("k", "q", "kb"))
        lf, gx = sb("lf", [P, CHAINS, UN * GS]), sb("gx", [P, CHAINS, UN * GS])
        eg, ek = sb("eg", [P, CHAINS, UN * GS]), sb("ek", [P, CHAINS, UN * GS])
        S = sb("S", [P, CHAINS, HD])
        ta = sb("ta", [P, UN, CHAINS, SUB + CT])

        s_w, s_init = sem("w", True), sem("init", True)
        with nc.Block() as block:

            @block.sync
            def _(sp):
                for dst, src in ((wq, "wq"), (wk, "wk"), (wv, "wv"), (wcat, "wcat")):
                    sp.dma_start(dst[:, :, :], w[src]).then_inc(s_w, 16)
                sp.dma_start(wrank[0:RANK, :], w["wf2"]).then_inc(s_w, 16)
                sp.dma_start(wrank[RANK:2 * RANK, :], w["wog2"]).then_inc(s_w, 16)
                sp.dma_start(wrank[2 * RANK:FG, :], cst["negsel"]).then_inc(s_w, 16)
                for dst, src in ((ident, "ident"), (headsum, "headsum"), (headcol, "headcol")):
                    sp.dma_start(dst[:, :], cst[src]).then_inc(s_w, 16)

            @block.vector
            def _(dve):
                dve.memset(epsk[:, :], EPS)
                dve.memset(mask[:, :], 1.0).then_inc(s_init, 1)
                dve.wait_ge(s_init, 1)
                dve.memset(mask[:, :].rearrange("p (u s) -> p u s", s=GS)[:, :, 0:1], 0.0)
                dve.memset(lf[:, :, :], 0.0)
                dve.memset(S[:, :, :], 0.0)
                dve.wait_ge(s_w, 160)
                for t in (wq, wk, wv):
                    dve.tensor_scalar(t[:, :, :], t[:, :, :], 0.5, None, ALU.mult)

        loop = ctx.enter_context(ExitStack())
        s = loop.enter_context(nc.Fori(0, PASSES))
        project(nc, ctx, sb, sem, psum, s, locals())
        decays_and_triangles(nc, ctx, sb, sem, psum, s, locals())
        scan(nc, ctx, sb, sem, psum, s, locals())
        clear(nc, sems)
        loop.close()
        epilogue(nc, sb, sem, psum, ident, x_in, x_out, w, g_scr, o_scr)
        clear(nc, kept)


def project(nc, ctx, sb, sem, psum, s, env):
    (x_in, wq, wk, wv, wcat, wrank, ident, headsum, epsk, k, q, kb, lf, v_scr, g_scr) = (
        env[n] for n in "x_in wq wk wv wcat wrank ident headsum epsk k q kb lf v_scr g_scr".split())
    NT = BATCH * PT // P
    with ExitStack() as scope:
        def tb(name, shape):
            return sb(name, shape, at=scope)

        x = tb("x", [P, NT, DIM])
        stats = tb("stats", [P, NT, 6])
        mean, var, rstd, dm = (tb(n, [P, NT]) for n in ("mean", "var", "rstd", "dm"))
        xT = tb("xT", [P, KCH, BATCH * PT])
        fg = tb("fg", [FG, BATCH * PT])
        th = [tb(f"th{i}", [P, 512]) for i in range(2)]
        vt, gt = tb("vt", [P, NT, DIM]), tb("gt", [P, NT, DIM])
        sq = [tb(f"sq{i}", [P, 512]) for i in range(2)]
        lg = [tb(f"lg{i}", [P, 512]) for i in range(2)]
        rn = [tb(f"rn{i}", [P, 512]) for i in range(2)]

        s_x = [sem(f"x{b}") for b in range(BATCH)]
        s_stat, s_var, s_std, s_xn = sem("stat"), sem("var"), sem("std"), sem("xn")
        s_dve, s_tr, s_xt = sem("dve"), sem("tr"), sem("xt")
        s_fg, s_fgc, s_bt, s_beta = sem("fg"), sem("fgc"), sem("bt"), sem("beta")
        s_mm, s_th, s_ev, s_gt, s_st = sem("mm"), sem("th"), sem("ev"), sem("gt"), sem("st")

        KQ = [(wh, g, c) for wh in range(2) for g in range(2) for c in range(2)]
        NKQ, NV = len(KQ), NT

        def rows(t, i):
            return t.rearrange("(b q i p) d -> p b q i d", b=BATCH, q=PASSES, p=P)

        with nc.Block() as block:

            @block.sync
            def _(sp):
                for b in range(BATCH):
                    sp.dma_start(x[:, 2 * b:2 * b + 2, :], x_in[bass.ds(b * SEQ + s * PT, PT), :].rearrange("(i p) d -> p i d", p=P)).then_inc(s_x[b], 16)
                for b in range(BATCH):
                    sp.wait_ge(s_ev, NKQ + 2 * b + 2)
                    for g in range(2):
                        sp.dma_start(v_scr[bass.ds((g * BATCH + b) * SEQ + s * PT, PT), :].rearrange("(i p) d -> p i d", p=P),
                                     vt[:, 2 * b:2 * b + 2, g * P:(g + 1) * P]).then_inc(s_st, 16)
                for b in range(BATCH):
                    sp.wait_ge(s_gt, 2 * b + 2)
                    sp.dma_start(g_scr[bass.ds(b * SEQ + s * PT, PT), :].rearrange("(i p) d -> p i d", p=P), gt[:, 2 * b:2 * b + 2, :]).then_inc(s_st, 16)

            @block.vector
            def _(dve):
                n = [0]

                def link(ins):
                    n[0] += 1
                    ins.then_inc(s_dve, 1)
                    dve.wait_ge(s_dve, n[0])

                for i in range(NT):
                    if i % 2 == 0:
                        dve.wait_ge(s_x[i // 2], 16)
                    dve.bn_stats(stats[:, i, :], x[:, i, :]).then_inc(s_stat, 1)
                dve.wait_ge(s_stat, NT)
                link(dve.tensor_tensor(mean[:, :], stats[:, :, 1], stats[:, :, 4], ALU.add))
                link(dve.tensor_tensor(dm[:, :], stats[:, :, 1], stats[:, :, 4], ALU.subtract))
                link(dve.tensor_tensor(var[:, :], stats[:, :, 2], stats[:, :, 5], ALU.add))
                link(dve.tensor_tensor(dm[:, :], dm[:, :], dm[:, :], ALU.mult))
                link(dve.tensor_scalar(mean[:, :], mean[:, :], 0.5, None, ALU.mult))
                link(dve.tensor_scalar(var[:, :], var[:, :], 1.0 / DIM, LN_EPS, ALU.mult, ALU.add))
                dve.scalar_tensor_tensor(out=var[:, :], in0=dm[:, :], scalar=0.25, in1=var[:, :],
                                         op0=ALU.mult, op1=ALU.add).then_inc(s_var, 1)
                dve.wait_ge(s_std, 1)
                link(dve.reciprocal(rstd[:, :], rstd[:, :]))
                for i in range(NT):
                    dve.tensor_scalar(x[:, i, :], x[:, i, :], mean[:, i:i + 1], rstd[:, i:i + 1],
                                      ALU.subtract, ALU.mult).then_inc(s_xn, 1)
                for c in range(2):
                    dve.wait_ge(s_fg, c + 1)
                    dve.tensor_copy(fg[0:2 * RANK, c * 512:(c + 1) * 512], psum[2 + c][0:2 * RANK, :]).then_inc(s_fgc, 1)
                dve.wait_ge(s_bt, 2)
                dve.tensor_scalar(fg[2 * RANK:FG, :], fg[2 * RANK:FG, :], 1.0, None, ALU.add).then_inc(s_beta, 1)
                for j in range(NKQ + NV):
                    if j < NKQ:
                        wh, g, c = KQ[j]
                        cols = 512
                        out = (k, q)[wh][:, g * BATCH + 2 * c:g * BATCH + 2 * c + 2, :].rearrange("p c t -> p (c t)")
                    else:
                        cols, out = DIM, vt[:, j - NKQ, :]
                    dve.wait_ge(s_th, j + 1)
                    dve.scalar_tensor_tensor(out=out, in0=th[j % 2][:, 0:cols], scalar=1.0, in1=psum[4 + j % 4][:, 0:cols],
                                             op0=ALU.add, op1=ALU.mult).then_inc(s_ev, 1)

            @block.scalar
            def _(act):
                act.wait_ge(s_var, 1)
                act.activation(rstd[:, :], var[:, :], ACT.Sqrt).then_inc(s_std, 1)
                for i in range(NT):
                    act.wait_ge(s_tr, i + 1)
                    act.copy(xT[:, :, i * P:(i + 1) * P], psum[i % 2][:, 0:DIM].rearrange("p (k t) -> p k t", k=KCH)).then_inc(s_xt, 1)
                for c in range(2):
                    act.wait_ge(s_fg, c + 1)
                    act.activation(fg[2 * RANK:FG, c * 512:(c + 1) * 512], psum[2 + c][2 * RANK:FG, :], ACT.Tanh, scale=0.5).then_inc(s_bt, 1)
                for j in range(NKQ + NV):
                    cols = 512 if j < NKQ else DIM
                    act.wait_ge(s_mm, j + 1)
                    if j >= 2:
                        act.wait_ge(s_ev, j - 1)
                    act.activation(th[j % 2][:, 0:cols], psum[4 + j % 4][:, 0:cols], ACT.Tanh).then_inc(s_th, 1)
                for i in range(NT):
                    j = NKQ + NV + i
                    act.wait_ge(s_mm, j + 1)
                    act.activation(gt[:, i, :], psum[4 + j % 4][:, 0:DIM], ACT.Tanh, scale=0.5).then_inc(s_gt, 1)

            @block.tensor
            def _(pe):
                for i in range(NT):
                    pe.wait_ge(s_xn, i + 1)
                    if i >= 2:
                        pe.wait_ge(s_xt, i - 1)
                    for c in range(KCH):
                        t = pe.transpose(psum[i % 2][:, c * P:(c + 1) * P], x[:, i, c * P:(c + 1) * P], ident[:, :])
                    t.then_inc(s_tr, 1)
                pe.wait_ge(s_xt, NT)
                for c in range(2):
                    for kc in range(KCH):
                        t = pe.matmul(psum[2 + c][0:FG, :], wcat[:, kc, :], xT[:, kc, c * 512:(c + 1) * 512],
                                      start=(kc == 0), stop=(kc == KCH - 1))
                    t.then_inc(s_fg, 1)
                for j in range(NKQ + NV + NT):
                    bank = psum[4 + j % 4]
                    if j >= 4:
                        if j - 4 < NKQ + NV:
                            pe.wait_ge(s_ev, j - 3)
                        else:
                            pe.wait_ge(s_gt, j - 3 - NKQ - NV)
                    if j < NKQ:
                        wh, g, c = KQ[j]
                        for kc in range(KCH):
                            t = pe.matmul(bank[:, :], (wk, wq)[wh][:, kc, g * P:(g + 1) * P], xT[:, kc, c * 512:(c + 1) * 512],
                                          start=(kc == 0), stop=(kc == KCH - 1))
                    elif j < NKQ + NV:
                        i = j - NKQ
                        for kc in range(KCH):
                            t = pe.matmul(bank[:, 0:DIM], xT[:, kc, i * P:(i + 1) * P], wv[:, kc, :],
                                          start=(kc == 0), stop=(kc == KCH - 1))
                    else:
                        i = j - NKQ - NV
                        if i == 0:
                            pe.wait_ge(s_fgc, 2)
                        t = pe.matmul(bank[:, 0:DIM], fg[RANK:2 * RANK, i * P:(i + 1) * P], wrank[RANK:2 * RANK, :], start=True, stop=True)
                    t.then_inc(s_mm, 1)

        s_f, s_a, s_e, s_l, s_lf = sem("f"), sem("a"), sem("e"), sem("l"), sem("lf")
        s_sq, s_ss, s_n1, s_n2, s_kn, s_bb, s_kb = (sem(n) for n in ("sq", "ss", "n1", "n2", "kn", "bb", "kb"))
        JB = [(g, c) for g in range(2) for c in range(2)]

        def pair(t, j):
            g, c = JB[j]
            return t[:, g * BATCH + 2 * c:g * BATCH + 2 * c + 2, :]

        with nc.Block() as block:

            @block.gpsimd
            def _(pool):
                for j in range(4):
                    if j >= 2:
                        pool.wait_ge(s_ss, j - 1)
                    kk = pair(k, j).rearrange("p c t -> p (c t)")
                    pool.tensor_tensor(sq[j % 2][:, :], kk, kk, ALU.mult).then_inc(s_sq, 1)

            @block.tensor
            def _(pe):
                for j, (g, c) in enumerate(JB):
                    pe.matmul(psum[j][:, :], wrank[0:RANK, g * P:(g + 1) * P], fg[0:RANK, c * 512:(c + 1) * 512],
                              start=True, stop=True).then_inc(s_f, 1)
                for j in range(4):
                    pe.wait_ge(s_sq, j + 1)
                    pe.matmul(psum[4 + j][:, :], headsum[:, :], sq[j % 2][:, :], start=True, stop=True).then_inc(s_ss, 1)
                for j, (g, c) in enumerate(JB):
                    pe.wait_ge(s_lf, j + 1)
                    pe.matmul(psum[j][:, :], wrank[2 * RANK:FG, g * P:(g + 1) * P], fg[2 * RANK:FG, c * 512:(c + 1) * 512],
                              start=True, stop=True).then_inc(s_bb, 1)

            @block.scalar
            def _(act):
                act.preload_act_table_set("natural_log_exp_and_others")
                for j in range(4):
                    act.wait_ge(s_f, j + 1)
                    if j >= 2:
                        act.wait_ge(s_lf, j - 1)
                    act.activation(lg[j % 2][:, :], psum[j][:, :], ACT.Abs).then_inc(s_a, 1)
                    act.wait_ge(s_a, j + 1)
                    act.activation(lg[j % 2][:, :], lg[j % 2][:, :], ACT.Exp, scale=-1.0).then_inc(s_e, 1)
                    act.wait_ge(s_e, j + 1)
                    act.activation(lg[j % 2][:, :], lg[j % 2][:, :], ACT.Ln, bias=1.0).then_inc(s_l, 1)
                for j in range(4):
                    act.wait_ge(s_ss, j + 1)
                    if j >= 2:
                        act.wait_ge(s_kn, j - 1)
                    act.activation(rn[j % 2][:, :], psum[4 + j][:, :], ACT.Ln, bias=epsk[:, 0:1]).then_inc(s_n1, 1)
                    act.wait_ge(s_n1, j + 1)
                    act.activation(rn[j % 2][:, :], rn[j % 2][:, :], ACT.Exp, scale=-0.5).then_inc(s_n2, 1)

            @block.vector
            def _(dve):
                for j in range(4):
                    dve.wait_ge(s_l, j + 1)
                    dve.scalar_tensor_tensor(
                        out=pair(lf, j).rearrange("p c (u s) -> p (c u) s", s=GS)[:, :, 1:GS],
                        in0=psum[j][:, :].rearrange("p (u t) -> p u t", t=CT), scalar=0.0,
                        in1=lg[j % 2][:, :].rearrange("p (u t) -> p u t", t=CT), op0=ALU.min, op1=ALU.subtract).then_inc(s_lf, 1)
                for j in range(4):
                    kk = pair(k, j).rearrange("p c t -> p (c t)")
                    dve.wait_ge(s_n2, j + 1)
                    dve.tensor_tensor(kk, kk, rn[j % 2][:, :], ALU.mult).then_inc(s_kn, 1)
                    dve.wait_ge(s_kn, j + 1)
                    dve.wait_ge(s_bb, j + 1)
                    dve.tensor_tensor(pair(kb, j).rearrange("p c t -> p (c t)"), kk, psum[j][:, :], ALU.mult).then_inc(s_kb, 1)

            @block.sync
            def _(sp):
                sp.wait_ge(s_st, 16 * 3 * BATCH)


def decays_and_triangles(nc, ctx, sb, sem, psum, s, env):
    (k, q, kb, lf, gx, eg, ek, ta, mask, ident, headcol, t_scr) = (
        env[n] for n in "k q kb lf gx eg ek ta mask ident headcol t_scr".split())
    NG = CHAINS * UN
    with ExitStack() as outer:
        a_sb = sb("a_sb", [P, NG, 4 * RW], at=outer)
        with ExitStack() as scope:
            def tb(name, shape):
                return sb(name, shape, at=scope)

            E = [tb(f"E{i}", [P, E_OFF[-1]]) for i in range(2)]
            fd = [tb(f"fd{i}", [P, PT]) for i in range(2)]
            left = [tb(f"left{i}", [P, UN, 4, LW]) for i in range(2)]
            right = [tb(f"right{i}", [P, UN, 4, RW]) for i in range(2)]
            prod = [tb(f"prod{i}", [P, 3, PT]) for i in range(2)]
            tsum = [tb(f"tsum{i}", [3 * HD, PT]) for i in range(2)]

            s_gx, s_sub, s_exp, s_f = sem("gx"), sem("sub"), sem("exp"), sem("fd")
            s_lr, s_qr, s_kf, s_pr = sem("lr"), sem("qr"), sem("kf"), sem("pr")
            s_A, s_ts, s_tse, s_go = sem("A"), sem("ts"), sem("tse"), sem("ago")
            s_Ae = [sem(f"Ae{i}") for i in range(4)]
            s_tst = [sem(f"tst{i}") for i in range(2)]

            def one(t, c):
                return t[:, bass.ds(c, 1), :]

            def gview(t, c, lo, T, a, b):
                v = one(t, c).rearrange("p a (u s) -> p (a u) s", s=GS)[:, :, lo:lo + CT]
                return v.rearrange("p u (m x) -> p u m x", x=2 * T)[:, :, :, a:b]

            def e_out(b, l, side):
                T = LEVELS[l]
                v = E[b][:, E_OFF[l]:E_OFF[l + 1]].rearrange("p (u m z e) -> p u m z e", m=8 // T, z=2, e=T + 1)
                return v[:, :, :, side, :]

            def e_keys(b, l, side):
                T = LEVELS[l]
                nb = 8 // T
                row = 2 * (T + 1)
                return bass.AP(tensor=E[b], offset=E_OFF[l] + side * (T + 1),
                               ap=[[E_OFF[-1], P], [nb * row, UN], [row, nb], [1, T], [1, 2]])

            def tok(t, c, T, half):
                return one(t, c).rearrange("p a (u m x) -> p (a u) m x", u=UN, x=2 * T)[:, :, :, half * T:half * T + T]

            with nc.Block() as block:

                @block.vector
                def _(dve):
                    def decay(c, b, first):
                        dve.tensor_tensor_scan(one(gx, c).rearrange("p a t -> p (a t)"), mask[:, :],
                                               one(lf, c).rearrange("p a t -> p (a t)"), 0.0, ALU.mult, ALU.add).then_inc(s_gx, 1)
                        dve.wait_ge(s_gx, c + 1)
                        g17 = one(gx, c).rearrange("p a (u s) -> p (a u) s", s=GS)
                        dve.tensor_tensor(one(ek, c).rearrange("p a (u s) -> p (a u) s", s=GS),
                                          g17[:, :, CT:GS].to_broadcast([P, UN, GS]), g17, ALU.subtract)
                        if not first:
                            dve.wait_ge(s_qr, c - 1)
                        for l, T in enumerate(LEVELS):
                            nb = 8 // T
                            mid = gview(gx, c, 0, T, T, T + 1).to_broadcast([P, UN, nb, T + 1])
                            dve.tensor_tensor(e_out(b, l, 0), mid, gview(gx, c, 0, T, 0, T + 1), ALU.subtract)
                            i = dve.tensor_tensor(e_out(b, l, 1), gview(gx, c, 1, T, T - 1, 2 * T), mid, ALU.subtract)
                        i.then_inc(s_sub, 1)

                    def keys(c, b, first):
                        dve.wait_ge(s_exp, c + 1)
                        if not first:
                            dve.wait_ge(s_A, 4 * c - 4)
                        for l, T in enumerate(LEVELS):
                            nb = 8 // T
                            for dst, t, half in ((left[b][:, :, l, :], k, 0), (right[b][:, :, l, 0:LW], kb, 1)):
                                i = dve.tensor_tensor(dst.rearrange("p u (m t r) -> p u m t r", m=nb, r=2),
                                                      tok(t, c, T, half).unsqueeze(4).to_broadcast([P, UN, nb, T, 2]),
                                                      e_keys(b, l, half), ALU.mult)
                        i.then_inc(s_lr, 1)

                    for b in range(2):
                        decay(b, b, True)
                    for b in range(2):
                        keys(b, b, True)
                    with dve.Fori(1, CHAINS // 2) as j:
                        for b in range(2):
                            decay(2 * j + b, b, False)
                        for b in range(2):
                            keys(2 * j + b, b, False)

                @block.gpsimd
                def _(pool):
                    def step(c, b, first):
                        pool.wait_ge(s_f, c + 1)
                        if not first:
                            pool.wait_ge(s_ts, c - 1)
                        kf, kt, qt = fd[b][:, :], one(k, c).rearrange("p a t -> p (a t)"), one(q, c).rearrange("p a t -> p (a t)")
                        pool.tensor_tensor(kf, kf, kt, ALU.mult).then_inc(s_kf, 1)
                        pool.tensor_tensor(prod[b][:, 2, :], kt, qt, ALU.mult)
                        pool.wait_ge(s_kf, c + 1)
                        pool.tensor_tensor(prod[b][:, 0, :], kf, one(kb, c).rearrange("p a t -> p (a t)"), ALU.mult)
                        pool.tensor_tensor(prod[b][:, 1, :], kf, qt, ALU.mult).then_inc(s_pr, 1)
                        pool.wait_ge(s_exp, c + 1)
                        if not first:
                            pool.wait_ge(s_A, 4 * c - 4)
                        for l, T in enumerate(LEVELS):
                            nb = 8 // T
                            i = pool.tensor_tensor(right[b][:, :, l, LW:RW].rearrange("p u (m t) -> p u m t", m=nb),
                                                   tok(q, c, T, 1), e_out(b, l, 1)[:, :, :, 1:T + 1], ALU.mult)
                        i.then_inc(s_qr, 1)
                    for b in range(2):
                        step(b, b, True)
                    with pool.Fori(1, CHAINS // 2) as j:
                        for b in range(2):
                            step(2 * j + b, b, False)

                @block.scalar
                def _(act):
                    def exps(c, b, first):
                        if not first:
                            act.wait_ge(s_pr, c - 1)
                        act.activation(fd[b][:, :].rearrange("p (u t) -> p u t", t=CT),
                                       one(lf, c).rearrange("p a (u s) -> p (a u) s", s=GS)[:, :, 1:GS], ACT.Exp).then_inc(s_f, 1)
                        act.wait_ge(s_sub, c + 1)
                        act.activation(one(eg, c), one(gx, c), ACT.Exp)
                        act.activation(one(ek, c), one(ek, c), ACT.Exp)
                        act.activation(E[b][:, :], E[b][:, :], ACT.Exp).then_inc(s_exp, 1)

                    def evac(c, b, first):
                        for u4 in range(4):
                            act.wait_ge(s_A, 4 * c + u4 + 1)
                            act.copy(a_sb[:, bass.ds(c * UN + 4 * u4, 4), :].rearrange("p u c -> p (u c)"), psum[u4][:, 0:16 * RW]).then_inc(s_Ae[u4], 1)
                        act.wait_ge(s_ts, c + 1)
                        if not first:
                            act.wait_ge(s_tst[b], 48 * ((c - b) // 2) if isinstance(c, int) else 48 * cj[0])
                        act.copy(tsum[b][:, :], psum[4 + b][0:3 * HD, 0:PT]).then_inc(s_tse, 1)
                    cj = [None]
                    for b in range(2):
                        exps(b, b, True)
                    for b in range(2):
                        evac(b, b, True)
                    with act.Fori(1, CHAINS // 2) as j:
                        cj[0] = j
                        for b in range(2):
                            exps(2 * j + b, b, False)
                        for b in range(2):
                            evac(2 * j + b, b, False)

                @block.tensor
                def _(pe):
                    def step(c, b, first):
                        pe.wait_ge(s_pr, c + 1)
                        if not first:
                            pe.wait_ge(s_tse, c - 1)
                        pe.wait_ge(s_lr, c + 1)
                        pe.wait_ge(s_qr, c + 1)
                        if not (isinstance(c, int) and c == 0):
                            pe.wait_ge(s_Ae[0], c)
                        for kind in range(3):
                            t = pe.matmul(psum[4 + b][kind * HD:kind * HD + HD, 0:PT], headcol[:, :], prod[b][:, kind, :], start=True, stop=True)
                        t.then_inc(s_ts, 1)
                        for u4 in range(4):
                            if u4 > 0 and not (isinstance(c, int) and c == 0):
                                pe.wait_ge(s_Ae[u4], c)
                                pe.sem_inc(s_go, 1)
                            for uu in range(4):
                                u = 4 * u4 + uu
                                for pk in range(2):
                                    for h in range(HQ):
                                        r = slice(HD * h, HD * h + HD)
                                        o = uu * 4 * RW + pk * 2 * RW
                                        t = pe.matmul(psum[u4][r, o:o + 2 * RW],
                                                      left[b][r, u, 2 * pk:2 * pk + 2, :].rearrange("p l c -> p (l c)"),
                                                      right[b][r, u, 2 * pk:2 * pk + 2, :].rearrange("p l c -> p (l c)"), start=True, stop=True)
                            t.then_inc(s_A, 1)
                    for b in range(2):
                        step(b, b, True)
                    with pe.Fori(1, CHAINS // 2) as j:
                        for b in range(2):
                            step(2 * j + b, b, False)

                @block.sync
                def _(sp):
                    def step(c, b):
                        sp.wait_ge(s_tse, c + 1)
                        for kind in range(3):
                            sp.dma_start(t_scr[bass.ds(c, 1), HQ * kind:HQ * kind + HQ, bass.ds(s * PT, PT)].rearrange("a h t -> (a h) t"),
                                         tsum[b][kind * HD:kind * HD + HQ, :]).then_inc(s_tst[b], 16)
                    with sp.Fori(0, CHAINS // 2) as j:
                        for b in range(2):
                            step(2 * j + b, b)
                    for b in range(2):
                        sp.wait_ge(s_tst[b], 48 * (CHAINS // 2))

        invert(nc, outer, sb, sem, psum, s, env, a_sb)


def invert(nc, scope, sb, sem, psum, s, env, a_sb):
    ident, ta, t_scr = (env[n] for n in ("ident", "ta", "t_scr"))

    def tb(name, shape):
        return sb(name, shape, at=scope)

    ng, tm = tb("ng", [P, HQ * HS]), tb("tm", [P, HQ * HS])
    aq = tb("aq", [P, CT, HQ, SUB])
    zz, pr = tb("zz", [P, HQ * 256]), tb("pr", [P, HQ * 256])
    tk = tb("tk", [P, 3 * HQ, CT])

    s_tk, s_zero, s_one, s_tp = sem("tk"), sem("zero"), sem("one"), sem("tp")
    s_ev = [sem("evA"), sem("evD")]
    s_diag, s_inv, s_tc, s_bk, s_bke = sem("diag"), sem("inv"), sem("tc"), sem("bk"), sem("bke")

    def square(t):
        return t[:, :].rearrange("p (h x) -> p h x", h=HQ)[:, :, 0:SUB * SUB].rearrange("p h (j i) -> p h j i", i=SUB)

    ngv, tmv = square(ng), square(tm)
    tc = a_sb[:, :, :].rearrange("p g c -> p (g c)")[:, 0:SUB * HQ * SUB].rearrange("p (j h i) -> p j h i", j=SUB, h=HQ)

    def runs(n):
        l, gq = n // 6, n % 6
        T = LEVELS[l]
        out = []
        per = 2 * T if gq < 4 else T
        base = 4 * (gq if gq < 4 else gq - 4)
        cc = 0
        while cc < 4:
            m, xx = (base + cc) // per, (base + cc) % per
            cnt = min(4 - cc, per - xx)
            row0 = 4 * T * m + 2 * T + xx if gq < 4 else 2 * T * m + T + xx
            out.append((cc, cnt, gq >= 4, row0, 4 * T * m, 2 * T * m, 2 * T))
            cc += cnt
        return l % 2, out

    def collect(eng, n, which):
        lev, rr = runs(n)
        bank = psum[n % 8][:, :].rearrange("p (c h l i) -> p h c l i", c=4, h=HQ, l=2)
        for cc, cnt, isq, row0, i0, l0, width in rr:
            src = bank[:, :, cc:cc + cnt, lev, l0:l0 + width]
            dst = (aq[:, :, :, :].rearrange("p t h i -> p h t i") if isq else ngv)[:, :, row0:row0 + cnt, i0:i0 + width]
            i = eng.copy(dst, src) if which == 0 else eng.tensor_copy(dst, src)
        i.then_inc(s_ev[which], 1)

    GROUPS = 24
    INV_STEPS = sum(2 * (2 * m - 1) for m in (2, 4, 8, 16))

    with nc.Block() as block:

        @block.sync
        def _(sp):
            for c in range(CHAINS):
                sp.dma_start(tk[c * UN:(c + 1) * UN, :, :],
                             t_scr[c, :, bass.ds(s * PT, PT)].rearrange("k (u t) -> u k t", t=CT)).then_inc(s_tk, 16)

        @block.gpsimd
        def _(pool):
            pool.memset(aq[:, :, :, :], 0.0).then_inc(s_zero, 1)
            pool.memset(tm[:, :], 0.0).then_inc(s_zero, 1)
            pool.wait_ge(s_zero, 2)
            dg = tm[:, :].rearrange("p (h j s) -> p h j s", h=HQ, s=SUB + 1)[:, :, :, 0:1]
            pool.memset(dg, 1.0).then_inc(s_one, 1)

        @block.tensor
        def _(pe):
            for n in range(GROUPS):
                if n >= 8:
                    pe.wait_ge(s_ev[n % 2], (n - 8) // 2 + 1)
                l, gq = n // 6, n % 6
                for cc in range(4):
                    col = l * RW + 4 * gq + cc
                    t = pe.transpose(psum[n % 8][:, cc * P:(cc + 1) * P], a_sb[:, :, col], ident[:, :])
                t.then_inc(s_tp, 1)
            for n in range(12):
                if n == 0:
                    for e in range(2):
                        pe.wait_ge(s_ev[e], GROUPS // 2)
                    pe.wait_ge(s_diag, 3)
                if n == 4:
                    pe.wait_ge(s_tc, 1)
                if n == 8:
                    pe.wait_ge(s_tc, 3)
                if n >= 8:
                    pe.wait_ge(s_bke, n - 7)
                for cc in range(4):
                    src = aq[:, 4 * n + cc, :, :] if n < 4 else tc[:, 4 * (n - 4) + cc, :, :]
                    t = pe.transpose(psum[n % 8][:, cc * P:(cc + 1) * P], src.rearrange("p h i -> p (h i)"), ident[:, :])
                t.then_inc(s_bk, 1)

        @block.scalar
        def _(act):
            for n in range(0, GROUPS, 2):
                if n == 0:
                    act.wait_ge(s_zero, 1)
                act.wait_ge(s_tp, n + 1)
                collect(act, n, 0)
            def compact(rows, cols):
                act.copy(tc[:, rows, :, cols], tmv[:, :, rows, cols].rearrange("p h j i -> p j h i")).then_inc(s_tc, 1)
            act.wait_ge(s_tp, GROUPS)
            act.wait_ge(s_inv, INV_STEPS - 2 * (2 * CT - 1))
            compact(slice(0, CT), slice(0, SUB))
            compact(slice(CT, SUB), slice(CT, SUB))
            for n in range(12):
                if n == 8:
                    act.wait_ge(s_inv, INV_STEPS)
                    compact(slice(CT, SUB), slice(0, CT))
                act.wait_ge(s_bk, n + 1)
                col = SUB + 4 * n if n < 4 else 4 * (n - 4)
                act.copy(ta[:, :, :, col:col + 4].rearrange("p u c j -> p c u j"),
                         psum[n % 8][:, :].rearrange("p (j c u) -> p c u j", j=4, c=CHAINS)).then_inc(s_bke, 1)

        @block.vector
        def _(dve):
            dve.wait_ge(s_zero, 1)
            for n in range(1, GROUPS, 2):
                dve.wait_ge(s_tp, n + 1)
                collect(dve, n, 1)
            dve.wait_ge(s_tk, 16 * CHAINS)
            dve.wait_ge(s_ev[0], GROUPS // 2)
            dve.wait_ge(s_one, 1)
            def kind(x):
                return tk[:, x * HQ:(x + 1) * HQ, :]
            for x in range(2):
                dst = bass.AP(tensor=aq, offset=x, ap=[[HQ * CT * SUB, P], [SUB, HQ], [HQ * SUB + 2, CT]])
                dve.tensor_copy(dst, kind(1 + x)).then_inc(s_diag, 1)
            dst = bass.AP(tensor=tm, offset=SUB, ap=[[HQ * HS, P], [HS, HQ], [2 * (SUB + 1), CT]])
            dve.tensor_copy(dst, kind(0)).then_inc(s_diag, 1)
            dve.wait_ge(s_diag, 3)
            dve.wait_ge(s_ev[1], GROUPS // 2)
            n = [0]

            def link(ins):
                n[0] += 1
                ins.then_inc(s_inv, 1)
                dve.wait_ge(s_inv, n[0])

            m = 2
            while m < SUB:
                blocks = HQ * SUB // (2 * m)

                def blk(t, j0, nj, i0, ni, dj=SUB, di=1):
                    return bass.AP(tensor=t, offset=j0 * SUB + i0, ap=[[HQ * HS, P], [2 * m * (SUB + 1), blocks], [dj, nj], [di, ni]])

                z = zz[:, 0:blocks * m * m].rearrange("p (b j i) -> p b j i", b=blocks, j=m)
                pv = pr[:, 0:blocks * m * m].rearrange("p (b j i) -> p b j i", b=blocks, j=m)
                for kk in range(m - 1, -1, -1):
                    dst = z if kk == m - 1 else pv
                    link(dve.tensor_tensor(dst[:, :, :, 0:kk + 1], blk(ng, m, m, kk, kk + 1, di=0), blk(tm, kk, m, 0, kk + 1, dj=0), ALU.mult))
                    if kk < m - 1:
                        link(dve.tensor_tensor(z[:, :, :, 0:kk + 1], z[:, :, :, 0:kk + 1], pv[:, :, :, 0:kk + 1], ALU.add))
                for kk in range(m):
                    rows = m - kk
                    zk = z[:, :, kk:kk + 1, :].to_broadcast([P, blocks, rows, m])
                    xk = blk(tm, m + kk, rows, m + kk, m, di=0)
                    out = blk(tm, m + kk, rows, 0, m)
                    if kk == 0:
                        link(dve.tensor_tensor(out, xk, zk, ALU.mult))
                    else:
                        link(dve.tensor_tensor(pv[:, :, 0:rows, :], xk, zk, ALU.mult))
                        link(dve.tensor_tensor(out, out, pv[:, :, 0:rows, :], ALU.add))
                m *= 2
            assert n[0] == INV_STEPS


def scan(nc, ctx, sb, sem, psum, s, env):
    k, q, kb, eg, ek, ta, S, v_scr, o_scr = (env[n] for n in "k q kb eg ek ta S v_scr o_scr".split())
    HC = CHAINS // 2
    with ExitStack() as scope:
        def tb(name, shape):
            return sb(name, shape, at=scope)

        v = tb("v", [P, UN, CHAINS, HD])
        o = tb("o", [P, UN, CHAINS, HD])
        kg = [tb(f"kg{i}", [P, CHAINS, CT, 2]) for i in range(2)]
        kd = [tb(f"kd{i}", [P, CHAINS, CT, 2]) for i in range(2)]
        kr = [tb(f"kr{i}", [P, CHAINS, HD]) for i in range(2)]
        qg = [tb(f"qg{i}", [P, CHAINS, SUB]) for i in range(2)]
        tu = [tb(f"tu{i}", [P, CHAINS, 2 * SUB]) for i in range(2)]
        R = [tb(f"R{i}", [P, HC, HD]) for i in range(2)]
        U = [tb(f"U{i}", [P, HC, HD]) for i in range(2)]
        D = [tb(f"D{i}", [P, HC, HD]) for i in range(2)]
        b_r, b_u, b_d, b_o = ([psum[4 * h + i][:, 0:HC * HD] for h in range(2)] for i in range(4))

        s_vz, s_pad, s_go = sem("vz"), sem("pad"), sem("go")
        s_v = [sem(f"v{i}") for i in range(2)]
        s_ost = sem("ost")
        s_kg, s_kd, s_kr, s_ta = sem("kg"), sem("kd"), sem("kr"), sem("ta")
        s_r, s_u, s_d, s_o, s_R, s_S, s_D, s_U, s_O = ([sem(f"{n}{h}") for h in range(2)] for n in
                                                         ("r", "u", "d", "o", "Rs", "Ss", "Ds", "Us", "Os"))

        def scr(t, c, h, half):
            return t[bass.ds(c * SEQ + s * PT + half * (PT // 2), PT // 2), h * HD:(h + 1) * HD].rearrange("(u t) v -> t u v", t=CT)

        H2 = UN // 2
        with nc.Block() as block:

            @block.sync
            def _(sp):
                sp.wait_ge(s_vz, 1)
                for half in range(2):
                    with sp.Fori(0, CHAINS) as c:
                        for h in range(HQ):
                            sp.dma_start(v[HD * h + 1:HD * h + HD:2, half * H2:(half + 1) * H2, bass.ds(c, 1), :].rearrange("p u a v -> p u (a v)"), scr(v_scr, c, h, half)).then_inc(s_v[half], 16)
                for half in range(2):
                    for i in range(2):
                        sp.wait_ge(s_O[i], (half + 1) * H2)
                    with sp.Fori(0, CHAINS) as c:
                        for h in range(HQ):
                            sp.dma_start(scr(o_scr, c, h, half), o[HD * h:HD * h + CT, half * H2:(half + 1) * H2, bass.ds(c, 1), :].rearrange("p u a v -> p u (a v)")).then_inc(s_ost, 16)
                sp.wait_ge(s_ost, 16 * 2 * CHAINS * HQ)

            @block.gpsimd
            def _(pool):
                for i in range(2):
                    pool.memset(qg[i][:, :, CT:SUB], 0.0).then_inc(s_pad, 1)
                    pool.memset(tu[i][:, :, SUB + CT:2 * SUB], 0.0).then_inc(s_pad, 1)

                def stage(u, b, first):
                    def t(x, width=CT, at=0, step=CT):
                        return x[:, :, bass.ds(u * step + at, width)]
                    if not first:
                        pool.wait_ge(s_o[1], u - 1)
                        pool.wait_ge(s_kr, u - 1)
                    for r in range(2):
                        pool.tensor_tensor(kg[b][:, :, :, r], t(kb), t(eg, at=r, step=GS), ALU.mult)
                    pool.tensor_tensor(qg[b][:, :, 0:CT], t(q), t(eg, at=1, step=GS), ALU.mult).then_inc(s_kg, 1)
                    for r in range(2):
                        i = pool.tensor_tensor(kd[b][:, :, :, r], t(k), t(ek, at=r, step=GS), ALU.mult)
                    i.then_inc(s_kd, 1)
                for b in range(2):
                    stage(b, b, True)
                with pool.Fori(1, UN // 2) as j:
                    for b in range(2):
                        stage(2 * j + b, b, False)

            @block.tensor
            def _(pe):
                def tiles(out, lhsT, rhs, cols, start, stop, open_=False):
                    for c in range(HC):
                        for h in range(HQ):
                            r = slice(HD * h, HD * h + HD)
                            i = pe.matmul(out[r, c * HD:(c + 1) * HD], lhsT(c)[r, cols], rhs[r, c, :],
                                          start=start and (not open_ or c == 0), stop=stop and (not open_ or c == HC - 1))
                    return i

                def step(u, b, first):
                    full = slice(0, SUB)
                    for f in range(2):
                        if f == 0:
                            pe.wait_ge(s_kg, u + 1)
                        if not (isinstance(u, int) and u == 0):
                            pe.wait_ge(s_S[f], u)
                            pe.wait_ge(s_O[f], u)
                        pe.sem_inc(s_go, 1)
                        St = S[:, HC * f:HC * f + HC, :]
                        tiles(b_r[f], lambda c: kg[b][:, HC * f + c, :, :].rearrange("p t r -> p (t r)"), St, full, start=True, stop=True).then_inc(s_r[f], 1)
                        tiles(b_o[f], lambda c: qg[b][:, HC * f + c, :], St, full, start=True, stop=False, open_=True)
                    for f in range(2):
                        if f == 0:
                            pe.wait_ge(s_ta, u + 1)
                        pe.wait_ge(s_R[f], u + 1)
                        pe.sem_inc(s_go, 1)
                        tiles(b_u[f], lambda c: tu[b][:, HC * f + c, 0:SUB], R[f], full, start=True, stop=True).then_inc(s_u[f], 1)
                    for f in range(2):
                        if f == 0:
                            pe.wait_ge(s_kr, u + 1)
                        pe.wait_ge(s_U[f], u + 1)
                        pe.sem_inc(s_go, 1)
                        tiles(b_d[f], lambda c: kr[b][:, HC * f + c, :], U[f], full, start=True, stop=True).then_inc(s_d[f], 1)
                        tiles(b_o[f], lambda c: tu[b][:, HC * f + c, SUB:2 * SUB], U[f], full, start=False, stop=True, open_=True).then_inc(s_o[f], 1)
                pe.wait_ge(s_pad, 4)
                for b in range(2):
                    step(b, b, True)
                with pe.Fori(1, UN // 2) as j:
                    for b in range(2):
                        step(2 * j + b, b, False)

            @block.scalar
            def _(act):
                def stage(u, b, first):
                    if not first:
                        act.wait_ge(s_o[1], u - 1)
                    act.copy(tu[b][:, :, 0:SUB + CT], ta[:, bass.ds(u, 1), :, :].rearrange("p a c j -> p (a c) j")).then_inc(s_ta, 1)

                def step(u, b, first, last):
                    for f in range(2):
                        act.wait_ge(s_u[f], u + 1)
                        if not (isinstance(u, int) and u == 0):
                            act.wait_ge(s_o[f], u)
                        act.copy(U[f][:, :, :].rearrange("p c v -> p (c v)"), b_u[f]).then_inc(s_U[f], 1)
                    for f in range(2):
                        act.wait_ge(s_o[f], u + 1)
                        act.copy(o[:, bass.ds(u, 1), HC * f:HC * f + HC, :].rearrange("p a c v -> p (a c v)"), b_o[f]).then_inc(s_O[f], 1)
                    if not last:
                        stage(u + 2, b, False)
                act.wait_ge(s_pad, 4)
                for b in range(2):
                    stage(b, b, True)
                for b in range(2):
                    step(b, b, True, False)
                with act.Fori(1, UN // 2 - 1) as j:
                    for b in range(2):
                        step(2 * j + b, b, False, False)
                for b in range(2):
                    step(UN - 2 + b, b, False, True)

            @block.vector
            def _(dve):
                def turn(u, b):
                    dve.wait_ge(s_kd, u + 1)
                    dve.transpose(kr[b][:, :, :].rearrange("p c d -> p (c d)"), kd[b][:, :, :, :].rearrange("p c t r -> p (c t r)")).then_inc(s_kr, 1)

                def step(u, b, last):
                    for f in range(2):
                        ch = slice(HC * f, HC * f + HC)
                        dve.wait_ge(s_r[f], u + 1)
                        dve.tensor_tensor(R[f][:, :, :], v[:, bass.ds(u, 1), ch, :].rearrange("p a c v -> p (a c) v"),
                                          b_r[f].rearrange("p (c v) -> p c v", c=HC), ALU.add).then_inc(s_R[f], 1)
                        if not (isinstance(u, int) and u == 0):
                            dve.wait_ge(s_S[f], u)
                        dve.tensor_tensor(D[f][:, :, :], S[:, ch, :], eg[:, ch, bass.ds(u * GS + CT, 1)].to_broadcast([P, HC, HD]), ALU.mult).then_inc(s_D[f], 1)
                    if not last:
                        turn(u + 1, 1 - b)
                    for f in range(2):
                        ch = slice(HC * f, HC * f + HC)
                        dve.wait_ge(s_D[f], u + 1)
                        dve.wait_ge(s_d[f], u + 1)
                        dve.tensor_tensor(S[:, ch, :], D[f][:, :, :], b_d[f].rearrange("p (c v) -> p c v", c=HC), ALU.add).then_inc(s_S[f], 1)
                dve.memset(v[:, :, :, :], 0.0).then_inc(s_vz, 1)
                turn(0, 0)
                for half in range(2):
                    dve.wait_ge(s_v[half], 16 * CHAINS * HQ)
                    if half == 0:
                        with dve.Fori(0, UN // 4) as j:
                            for b in range(2):
                                step(2 * j + b, b, False)
                    else:
                        with dve.Fori(UN // 4, UN // 2 - 1) as j:
                            for b in range(2):
                                step(2 * j + b, b, False)
                        step(UN - 2, 0, False)
                        step(UN - 1, 1, True)


def epilogue(nc, sb, sem, psum, ident, x_in, x_out, w, g_scr, o_scr):
    with ExitStack() as scope:
        def tb(name, shape):
            return [sb(f"{name}{i}", shape, at=scope) for i in range(2)]

        wo, nw, eps4 = sb("wo", [P, KCH, DIM], at=scope), sb("nw", [P, KCH], at=scope), sb("eps4", [P, 1], at=scope)
        x, g, o, sq, y, yT, res = (tb(n, [P, DIM]) for n in ("ex", "egate", "eo", "esq", "ey", "eyT", "eres"))
        ss, rs = tb("ess", [P, HEADS]), tb("ers", [P, HEADS])
        s_in, s_st = [sem(f"ein{i}", True) for i in range(2)], [sem(f"est{i}", True) for i in range(2)]
        s_eps, s_w, s_wo, s_y, s_sq, s_ss, s_sd, s_rs, s_yn, s_tr, s_yT, s_mm, s_out = (
            sem("e" + n, True) for n in ("eps", "w", "wo", "y", "sq", "ss", "sd", "rs", "yn", "tr", "yT", "mm", "out"))
        p_t, p_o = [psum[0], psum[1]], [psum[2], psum[3]]
        N2 = TILES // 2
        with nc.Block() as block:

            @block.sync
            def _(sp):
                sp.dma_start(wo[:, :, :], w["wo"]).then_inc(s_w, 16)
                sp.dma_start(nw[:, :], w["nw"]).then_inc(s_w, 16)

                def load(i, b, first):
                    if not first:
                        sp.wait_ge(s_out, i - 1)
                    for dst, src in ((x, x_in), (g, g_scr)):
                        sp.dma_start(dst[b][:, :], src[bass.ds(i * P, P), :]).then_inc(s_in[b], 16)
                    for half in range(2):
                        sp.dma_start(o[b][:, half * P:(half + 1) * P], o_scr[bass.ds(half * TOKENS + i * P, P), :]).then_inc(s_in[b], 16)
                for b in range(2):
                    load(b, b, True)
                def store(i, b):
                    sp.wait_ge(s_out, i + 1)
                    sp.dma_start(x_out[bass.ds(i * P, P), :], res[b][:, :]).then_inc(s_st[b], 16)
                with sp.Fori(1, N2) as j:
                    for b in range(2):
                        load(2 * j + b, b, False)
                        store(2 * j + b - 2, b)
                for b in range(2):
                    store(TILES - 2 + b, b)
                for b in range(2):
                    sp.wait_ge(s_st[b], 16 * N2)

            @block.scalar
            def _(act):
                def step(i, j, b, first):
                    act.wait_ge(s_ss, i + 1)
                    act.activation(rs[b][:, :], ss[b][:, :], ACT.Sqrt, bias=eps4[:, 0:1], scale=1.0 / HD).then_inc(s_sd, 1)
                    act.wait_ge(s_tr, i + 1)
                    act.copy(yT[b][:, :], p_t[b][:, 0:DIM]).then_inc(s_yT, 1)
                act.wait_ge(s_eps, 1)
                with act.Fori(0, N2) as j:
                    for b in range(2):
                        step(2 * j + b, j, b, None)

            @block.tensor
            def _(pe):
                def step(i, b):
                    pe.wait_ge(s_yn, i + 1)
                    for c in range(KCH):
                        t = pe.transpose(p_t[b][:, c * P:(c + 1) * P], y[b][:, c * P:(c + 1) * P], ident[:, :])
                    t.then_inc(s_tr, 1)
                    pe.wait_ge(s_yT, i + 1)
                    for c in range(KCH):
                        t = pe.matmul(p_o[b][:, 0:DIM], yT[b][:, c * P:(c + 1) * P], wo[:, c, :], start=(c == 0), stop=(c == KCH - 1))
                    t.then_inc(s_mm, 1)
                pe.wait_ge(s_wo, KCH)
                with pe.Fori(0, N2) as j:
                    for b in range(2):
                        step(2 * j + b, b)

            @block.vector
            def _(dve):
                dve.memset(eps4[:, :], 4 * EPS).then_inc(s_eps, 1)
                dve.wait_ge(s_w, 32)
                for c in range(KCH):
                    dve.tensor_scalar(wo[:, c, :], wo[:, c, :], nw[:, c:c + 1], None, ALU.mult).then_inc(s_wo, 1)

                def before(i, j, b):
                    dve.wait_ge(s_in[b], 64 * j + 64)
                    dve.scalar_tensor_tensor(out=y[b][:, :], in0=g[b][:, :], scalar=1.0, in1=o[b][:, :], op0=ALU.add, op1=ALU.mult).then_inc(s_y, 1)
                    dve.wait_ge(s_y, i + 1)
                    dve.tensor_tensor(sq[b][:, :], y[b][:, :], y[b][:, :], ALU.mult).then_inc(s_sq, 1)
                    dve.wait_ge(s_sq, i + 1)
                    dve.tensor_reduce(ss[b][:, :], sq[b][:, :].rearrange("p (h d) -> p h d", h=HEADS), AX.X, ALU.add).then_inc(s_ss, 1)
                    dve.wait_ge(s_sd, i + 1)
                    dve.reciprocal(rs[b][:, :], rs[b][:, :]).then_inc(s_rs, 1)
                    dve.wait_ge(s_rs, i + 1)
                    yh = y[b][:, :].rearrange("p (h d) -> p h d", h=HEADS)
                    dve.tensor_tensor(yh, yh, rs[b][:, :].unsqueeze(2).to_broadcast([P, HEADS, HD]), ALU.mult).then_inc(s_yn, 1)

                def after(i, stored, b):
                    dve.wait_ge(s_mm, i + 1)
                    if stored is not None:
                        dve.wait_ge(s_st[b], 16 * stored)
                    dve.tensor_tensor(res[b][:, :], x[b][:, :], p_o[b][:, 0:DIM], ALU.add).then_inc(s_out, 1)
                before(0, 0, 0)
                before(1, 0, 1)
                after(0, None, 0)
                before(2, 1, 0)
                after(1, None, 1)
                before(3, 1, 1)
                after(2, 1, 0)
                with dve.Fori(2, N2) as j:
                    before(2 * j, j, 0)
                    after(2 * j - 1, j - 1, 1)
                    before(2 * j + 1, j, 1)
                    after(2 * j, j, 0)
                after(TILES - 1, N2 - 1, 1)


def macaron(nc, a, x, out):
    def scratch(name, shape):
        return nc.dram_tensor(name, shape, F32, kind="Internal").ap()

    ctx = ExitStack()
    pool_sems = [pool_dma_semaphores(nc, ctx, tag) for tag in ("ffn1", "ffn2")]
    x1, x2 = scratch("x1", [TOKENS, DIM]), scratch("x2", [TOKENS, DIM])
    xs, ys = scratch("xs", [XS_ROWS, DIM]), scratch("ys", [ROWS, DIM])
    ffn(nc, "ffn1", x, x1, a["w1t"], a["w2t"], a["rwt"], a, xs, ys, pool_sems[0])
    attn(nc, x1, x2, a, a, scratch("v", [CHAINS * SEQ, P]), scratch("gate", [TOKENS, DIM]),
         scratch("o", [CHAINS * SEQ, P]), scratch("t", [CHAINS, 3 * HQ, SEQ]))
    ffn(nc, "ffn2", x2, out, a["w1t"], a["w2t"], a["rwt"], a, xs, ys, pool_sems[1])
    ctx.close()


def layouts(i):
    def chunks(w):
        return w.reshape(KCH, P, -1).transpose(1, 0, 2)

    w = {n: i["L0_attn_" + n] for n in "Wq Wk Wv Wf1 Wf2 Wbeta Wog1 Wog2 norm_w Wo".split()}
    return {
        "x": i["L0_attn_x"].reshape(TOKENS, DIM),
        "wq": chunks(w["Wq"]), "wk": chunks(w["Wk"]), "wv": chunks(w["Wv"]), "wo": chunks(w["Wo"]),
        "wcat": chunks(np.concatenate([w["Wf1"], w["Wog1"], w["Wbeta"]], 1)),
        "wf2": w["Wf2"], "wog2": w["Wog2"], "nw": w["norm_w"].reshape(KCH, P).T,
        "w1t": i["L0_ffn_w1"].transpose(0, 2, 1).reshape(EXPERTS, KCH, P, 2 * INNER).transpose(0, 2, 1, 3),
        "w2t": i["L0_ffn_w2"].transpose(0, 2, 1).reshape(EXPERTS, ICH, P, DIM).transpose(0, 2, 1, 3),
        "rwt": i["L0_ffn_router_w"].T.reshape(KCH, P, EXPERTS).transpose(1, 0, 2),
        **ffn_constants(), **attn_constants(),
    }


def kernel(**inputs):
    import concourse.bacc as _bacc
    from concourse.bass_utils import run_bass_kernel_spmd as _run

    nc = _bacc.Bacc("TRN2", target_bir_lowering=False, num_devices=1)
    arrays, aps = {}, {}
    for name, a in layouts({k: np.asarray(v) for k, v in inputs.items()}).items():
        a = np.ascontiguousarray(a)
        arrays[f"in_{name}_dram"] = a
        aps[name] = nc.dram_tensor(f"in_{name}_dram", a.shape, mybir.dt.from_np(a.dtype), kind="ExternalInput").ap()
    out = nc.dram_tensor("out_0_dram", (TOKENS, DIM), F32, kind="ExternalOutput").ap()
    macaron(nc, aps, aps["x"], out)
    r = _run(nc, [arrays], core_ids=[0])
    return r.results[0]["out_0_dram"].reshape(BATCH, SEQ, DIM)
```

```python
import numpy as np
from contextlib import ExitStack
import concourse.bass as bass
from concourse import mybir

F32 = mybir.dt.float32
I32 = mybir.dt.int32
U32 = mybir.dt.uint32
ALU = mybir.AluOpType
ACT = mybir.ActivationFunctionType
AX = mybir.AxisListType
P = 128

BATCH, SEQ, DIM = 4, 1024, 256
TOKENS = BATCH * SEQ
KCH = DIM // P
EXPERTS, INNER, TOPK = 8, 512, 2
TILES = TOKENS // P
ICH = INNER // P
LN_EPS = 1e-5
SLOTS = TOKENS * TOPK // P + EXPERTS
SPARE_TILES = EXPERTS
XS_SPARE = EXPERTS * TOKENS
XS_ROWS = XS_SPARE + (SPARE_TILES + EXPERTS) * P
XW = DIM + 4
YS_ROWS = TOPK * TOKENS + (EXPERTS + SPARE_TILES) * P
GROUPS = 4
GT = TOKENS // P // GROUPS

HEADS, HD = 8, 32
HQ = P // HD
CHAINS = (HEADS // HQ) * BATCH
RANK = 32
EPS = 1e-6
CT = 16
SUB = 2 * CT
UN = 16
PT = CT * UN
PASSES = SEQ // PT
GS = CT + 1
LEVELS = (8, 4, 2, 1)
LW, RW = 16, 24
E_OFF = [0]
for _T in LEVELS:
    E_OFF.append(E_OFF[-1] + UN * (8 // _T) * 2 * (_T + 1))
HS = 33 * SUB
FG = 2 * RANK + HEADS


def clear(nc, sems):
    with nc.Block() as block:

        @block.sync
        def _(sp):
            nums = sorted(s.num for s in sems)
            first = 0
            for i in range(1, len(nums) + 1):
                if i == len(nums) or nums[i] != nums[i - 1] + 1:
                    sp.sem_clear(range(nums[first], nums[i - 1] + 1))
                    first = i


def ffn_constants():
    c = {}
    c["ident"] = np.eye(P, dtype=np.float32)
    c["lower"] = np.triu(np.ones((P, P), np.float32), 1)
    c["ones"] = np.ones((P, P), np.float32)
    e = np.arange(EXPERTS)
    row = np.concatenate([
        (e[None, :] < e[:, None]).ravel(),
        e, e * TOKENS,
        XS_SPARE + (SPARE_TILES + e) * P,
        np.arange(TOKENS // P) * P, np.arange(SLOTS),
    ]).astype(np.float32)
    c["row"] = np.repeat(row[None, :], P, 0)
    p = np.arange(P, dtype=np.float32)[:, None]
    i = np.arange(GT, dtype=np.float32)[None, :]
    c["part"] = np.concatenate([p, TOKENS + p + SEQ * (i // (GT // BATCH)) + P * (i % (GT // BATCH))], 1).astype(np.float32)
    return c


class Routing:

    def __init__(self, sb, sem, banks, cst, rw, ident, buffers, scattered):
        self.cst, self.rw, self.ident, self.scattered = cst, rw, ident, scattered
        self.lower, self.ones = sb("lower", [P, P]), sb("ones", [P, P])
        self.row, self.part = sb("row", [P, cst["row"].shape[1]]), sb("part", [P, 1 + GT])
        self.rows = [sb(f"rows{i}", [P, GT, XW]) for i in range(buffers)]
        self.slot_u = [sb(f"slot_u{i}", [P, TOPK, GT], U32) for i in range(buffers)]
        self.stats, self.xt = sb("stats", [P, GT, 6]), [sb(f"xt{i}", [P, KCH, P]) for i in range(2)]
        self.mean, self.var, self.rstd, self.dm = (sb(n, [P, GT]) for n in ("mean", "var", "rstd", "dm"))
        self.prob, self.rank, self.both, self.slot, self.pick = (
            sb(n, [P, GT, EXPERTS]) for n in ("prob", "rank", "both", "slot", "pick"))
        self.tmax, self.tsum = sb("tmax", [P, GT]), sb("tsum", [P, GT])
        self.beats, self.ties = sb("beats", [P, GT * 64]), sb("ties", [P, GT * 64])
        self.sel, self.upto = sb("sel", [P, TOPK, GT, EXPERTS]), sb("upto", [P, EXPERTS, GT])
        self.slot_f, self.wtop = sb("slot_f", [P, TOPK, GT]), sb("wtop", [P, TOPK, GT])
        self.next = sb("next", [P, EXPERTS])
        self.p_t, self.p_g, self.p_c = banks[0:2], banks[2:4], banks[4:6]
        (self.s_stat, self.s_var, self.s_std, self.s_xn, self.s_tr, self.s_xt, self.s_gate, self.s_sub, self.s_exp,
         self.s_both, self.s_cnt, self.s_rows, self.s_own) = (
            sem("r_" + n) for n in "stat var std xn tr xt gate sub exp both cnt rows own".split())
        k = 64
        self.LT = self.row[:, 0:k]
        self.EXPERT, self.FIRST, self.DUMP = (self.row[:, k + EXPERTS * i:k + EXPERTS * (i + 1)] for i in range(3))
        k += 3 * EXPERTS
        self.STEPS, self.COUNT = self.row[:, k:k + TOKENS // P], self.row[:, k + TOKENS // P:]
        self.token = self.part[:, 1:1 + GT]
        self.links = 0

    def load(self, sp, s_cst):
        for dst, src in ((self.lower, "lower"), (self.ones, "ones"), (self.row, "row"), (self.part, "part")):
            sp.dma_start(dst[:, :], self.cst[src]).then_inc(s_cst, 16)

    def link(self, dve, ins):
        self.links += 1
        ins.then_inc(self.s_own, 1)
        dve.wait_ge(self.s_own, self.links)

    def start(self, dve):
        self.link(dve, dve.tensor_copy(self.next[:, :], self.FIRST))

    def norm_vector(self, dve, g, x):
        r, b = self, g % len(self.rows)

        def link(ins):
            r.link(dve, ins)

        for i in range(GT):
            dve.bn_stats(r.stats[:, i, :], x[:, i, :]).then_inc(r.s_stat, 1)
        dve.wait_ge(r.s_stat, GT * (g + 1))
        dve.tensor_tensor(r.mean[:, :], r.stats[:, :, 1], r.stats[:, :, 4], ALU.add)
        dve.tensor_tensor(r.dm[:, :], r.stats[:, :, 1], r.stats[:, :, 4], ALU.subtract)
        link(dve.tensor_tensor(r.var[:, :], r.stats[:, :, 2], r.stats[:, :, 5], ALU.add))
        dve.tensor_tensor(r.dm[:, :], r.dm[:, :], r.dm[:, :], ALU.mult)
        dve.tensor_scalar(r.mean[:, :], r.mean[:, :], 0.5, None, ALU.mult)
        link(dve.tensor_scalar(r.var[:, :], r.var[:, :], 1.0 / DIM, LN_EPS, ALU.mult, ALU.add))
        dve.scalar_tensor_tensor(out=r.var[:, :], in0=r.dm[:, :], scalar=0.25, in1=r.var[:, :],
                                 op0=ALU.mult, op1=ALU.add).then_inc(r.s_var, 1)
        dve.wait_ge(r.s_std, g + 1)
        link(dve.reciprocal(r.rstd[:, :], r.rstd[:, :]))
        r.scattered(dve, g)
        for i in range(GT):
            dve.tensor_scalar(r.rows[b][:, i, 0:DIM], x[:, i, :], r.mean[:, i:i + 1], r.rstd[:, i:i + 1],
                              ALU.subtract, ALU.mult).then_inc(r.s_xn, 1)

    def choose_vector(self, dve, g):
        r, b = self, g % len(self.rows)
        cube3, big = [P, GT, EXPERTS], [P, GT, EXPERTS, EXPERTS]

        def link(ins):
            r.link(dve, ins)

        logits = r.p_g[g % 2][:, 0:GT * EXPERTS].rearrange("p (i e) -> p i e", e=EXPERTS)
        dve.wait_ge(r.s_gate, GT * (g + 1))
        link(dve.tensor_reduce(r.tmax[:, :], logits, AX.X, ALU.max))
        dve.tensor_tensor(r.prob[:, :, :], logits, r.tmax[:, :].unsqueeze(2).to_broadcast(cube3), ALU.subtract).then_inc(r.s_sub, 1)
        dve.wait_ge(r.s_exp, g + 1)
        link(dve.tensor_reduce(r.tsum[:, :], r.prob[:, :, :], AX.X, ALU.add))
        link(dve.reciprocal(r.tsum[:, :], r.tsum[:, :]))
        link(dve.tensor_tensor(r.prob[:, :, :], r.prob[:, :, :], r.tsum[:, :].unsqueeze(2).to_broadcast(cube3), ALU.mult))
        def cube(t):
            return t[:, :].rearrange("p (i e f) -> p i e f", e=EXPERTS, f=EXPERTS)
        other, mine = r.prob[:, :, :].unsqueeze(2).to_broadcast(big), r.prob[:, :, :].unsqueeze(3).to_broadcast(big)
        dve.tensor_tensor(cube(r.beats), other, mine, ALU.is_gt)
        link(dve.tensor_tensor(cube(r.ties), other, mine, ALU.is_equal))
        ties = r.ties[:, :].rearrange("p (i f) -> p i f", f=64)
        link(dve.tensor_tensor(ties, ties, r.LT.unsqueeze(1).to_broadcast([P, GT, 64]), ALU.mult))
        link(dve.tensor_tensor(r.beats[:, :], r.beats[:, :], r.ties[:, :], ALU.add))
        link(dve.tensor_reduce(r.rank[:, :, :], cube(r.beats), AX.X, ALU.add))
        dve.tensor_scalar(r.both[:, :, :], r.rank[:, :, :], float(TOPK), None, ALU.is_lt).then_inc(r.s_both, 1)
        for c in range(TOPK):
            i = dve.tensor_scalar(r.sel[:, c, :, :], r.rank[:, :, :], float(c), None, ALU.is_equal)
        link(i)
        for c in range(TOPK):
            link(dve.tensor_tensor(r.pick[:, :, :], r.sel[:, c, :, :], r.prob[:, :, :], ALU.mult))
            link(dve.tensor_reduce(r.wtop[:, c, :], r.pick[:, :, :], AX.X, ALU.add))
        link(dve.tensor_scalar(r.wtop[:, :, :], r.wtop[:, :, :], 0.5, None, ALU.mult))
        meta = [r.rows[b][:, :, DIM + i] for i in range(4)]
        dve.tensor_copy(meta[0], r.token)
        dve.tensor_tensor(meta[1], r.wtop[:, 0, :], r.wtop[:, 1, :], ALU.subtract)
        dve.tensor_copy(meta[2], r.wtop[:, 1, :])
        link(dve.tensor_tensor(r.pick[:, :, :], r.sel[:, 0, :, :], r.EXPERT.unsqueeze(1).to_broadcast(cube3), ALU.mult))
        link(dve.tensor_reduce(meta[3], r.pick[:, :, :], AX.X, ALU.add))
        link(dve.tensor_scalar(r.token, r.token, float(SEQ // GROUPS), None, ALU.add))
        dve.wait_ge(r.s_cnt, 2 * (g + 1))
        before = r.p_c[0][:, 0:GT * EXPERTS].rearrange("p (i e) -> p i e", e=EXPERTS)
        totals = r.p_c[1][:, 0:GT * EXPERTS].rearrange("p (i e) -> p e i", e=EXPERTS)
        for e in range(EXPERTS):
            i = dve.tensor_tensor_scan(r.upto[:, e, :], r.ones[:, 0:GT], totals[:, e, :], 0.0, ALU.mult, ALU.add)
        link(i)
        link(dve.tensor_tensor(r.slot[:, :, :], r.upto[:, :, :].rearrange("p e i -> p i e"), totals.rearrange("p e i -> p i e"), ALU.subtract))
        link(dve.tensor_tensor(r.slot[:, :, :], r.slot[:, :, :], before, ALU.add))
        link(dve.tensor_tensor(r.slot[:, :, :], r.slot[:, :, :], r.next[:, :].unsqueeze(1).to_broadcast(cube3), ALU.add))
        link(dve.tensor_tensor(r.next[:, :], r.next[:, :], r.upto[:, :, GT - 1], ALU.add))
        for c in range(TOPK):
            link(dve.tensor_tensor(r.pick[:, :, :], r.sel[:, c, :, :], r.slot[:, :, :], ALU.mult))
            link(dve.tensor_reduce(r.slot_f[:, c, :], r.pick[:, :, :], AX.X, ALU.add))
        dve.tensor_copy(r.slot_u[b][:, :, :], r.slot_f[:, :, :]).then_inc(r.s_rows, 1)

    def norm_scalar(self, act, g):
        r = self
        act.wait_ge(r.s_var, g + 1)
        act.activation(r.rstd[:, :], r.var[:, :], ACT.Sqrt).then_inc(r.s_std, 1)
        for i in range(GT):
            n = GT * g + i
            act.wait_ge(r.s_tr, n + 1)
            if n >= 2:
                act.wait_ge(r.s_gate, n - 1)
            act.copy(r.xt[n % 2][:, :, :].rearrange("p k t -> p (k t)"), r.p_t[n % 2][:, 0:DIM]).then_inc(r.s_xt, 1)

    def choose_scalar(self, act, g):
        r = self
        act.wait_ge(r.s_sub, g + 1)
        act.activation(r.prob[:, :, :], r.prob[:, :, :], ACT.Exp).then_inc(r.s_exp, 1)

    def gate_tensor(self, pe, g):
        r, b = self, g % len(self.rows)

        def gate(i):
            n = GT * g + i
            pe.wait_ge(r.s_xt, n + 1)
            if i == 0 and g > 1:
                pe.wait_ge(r.s_sub, g - 1)
            for k in range(KCH):
                t = pe.matmul(r.p_g[g % 2][:, i * EXPERTS:(i + 1) * EXPERTS], r.xt[n % 2][:, k, :], r.rw[:, k, :], start=(k == 0), stop=(k == KCH - 1))
            t.then_inc(r.s_gate, 1)

        for i in range(GT):
            n = GT * g + i
            pe.wait_ge(r.s_xn, n + 1)
            if n >= 2:
                pe.wait_ge(r.s_xt, n - 1)
            for k in range(KCH):
                t = pe.transpose(r.p_t[n % 2][:, k * P:(k + 1) * P], r.rows[b][:, i, k * P:(k + 1) * P], r.ident[:, :])
            t.then_inc(r.s_tr, 1)
            if i > 0:
                gate(i - 1)
        gate(GT - 1)

    def count_tensor(self, pe, g):
        r = self
        pe.wait_ge(r.s_both, g + 1)
        if g > 0:
            pe.wait_ge(r.s_rows, g)
        flat = r.both[:, :, :].rearrange("p i e -> p (i e)")
        pe.matmul(r.p_c[0][:, 0:GT * EXPERTS], r.lower[:, :], flat, start=True, stop=True).then_inc(r.s_cnt, 1)
        pe.matmul(r.p_c[1][:, 0:GT * EXPERTS], r.ones[:, :], flat, start=True, stop=True).then_inc(r.s_cnt, 1)

    def scatter(self, pool, b, i, c, xs, s_scat):
        pool.indirect_dma_start(xs, bass.IndirectOffsetOnAxis(ap=self.slot_u[b][:, c, i:i + 1], axis=0),
                                self.rows[b][:, i, :], None).then_inc(s_scat, 16)


class Table:

    def __init__(self, sb, sem):
        self.tab_f = sb("tab_f", [P, SLOTS])
        self.expert, self.tile = sb("tab_e", [1, SLOTS], I32), sb("tab_t", [1, SLOTS], I32)
        self.tail_u = sb("tail_u", [P, EXPERTS], U32)
        self.s_tab, self.s_tail, self.s_zero = sem("t_tab"), sem("t_tail"), sem("t_zero")

    def empty(self, dve, rows, part):
        dve.memset(rows[:, :, :], 0.0).then_inc(self.s_zero, 1)
        dve.wait_ge(self.s_zero, 1)
        for i in range(EXPERTS + SPARE_TILES):
            dve.tensor_scalar(rows[:, i, DIM:DIM + 1], part, float(TOPK * TOKENS + i * P), None, ALU.add)
        dve.memset(rows[:, :, XW - 1:XW], -1.0).then_inc(self.s_zero, 1)

    def vector(self, dve, r, tb):
        t = self
        need = tb("need", [P, EXPERTS, TOKENS // P])
        cnt, ntile, tend, room = (tb(n, [P, EXPERTS]) for n in ("cnt", "ntile", "tend", "room"))
        tail, tail_ok, tail_d = (tb(n, [P, EXPERTS]) for n in ("tail", "tail_ok", "tail_d"))
        done, tile_f = tb("done", [P, SLOTS, EXPERTS]), tb("tile_f", [P, SLOTS])

        def link(ins):
            r.link(dve, ins)

        big, part = [P, EXPERTS, TOKENS // P], r.part[:, 0:1]
        link(dve.tensor_tensor(cnt[:, :], r.next[:, :], r.FIRST, ALU.subtract))
        link(dve.tensor_tensor(need[:, :, :], cnt[:, :].unsqueeze(2).to_broadcast(big), r.STEPS.unsqueeze(1).to_broadcast(big), ALU.is_gt))
        link(dve.tensor_reduce(ntile[:, :], need[:, :, :], AX.X, ALU.add))
        link(dve.tensor_scalar(tail[:, :], cnt[:, :], part, None, ALU.add))
        dve.tensor_scalar(tail_d[:, :], r.DUMP, part, None, ALU.add)
        link(dve.scalar_tensor_tensor(out=tail_ok[:, :], in0=ntile[:, :], scalar=float(P), in1=tail[:, :], op0=ALU.mult, op1=ALU.is_gt))
        link(dve.tensor_tensor(tail[:, :], tail[:, :], r.FIRST, ALU.add))
        link(dve.tensor_tensor(tail[:, :], tail[:, :], tail_d[:, :], ALU.subtract))
        link(dve.tensor_tensor(tail[:, :], tail[:, :], tail_ok[:, :], ALU.mult))
        link(dve.tensor_tensor(tail[:, :], tail[:, :], tail_d[:, :], ALU.add))
        dve.tensor_copy(t.tail_u[:, :], tail[:, :]).then_inc(t.s_tail, 1)
        link(dve.tensor_tensor_scan(tend[:, :], r.ones[:, 0:EXPERTS], ntile[:, :], 0.0, ALU.mult, ALU.add))
        dve.tensor_scalar(room[:, :], ntile[:, :], -1.0, float(TOKENS // P), ALU.mult, ALU.add)
        big = [P, SLOTS, EXPERTS]
        link(dve.tensor_tensor(done[:, :, :], r.COUNT.unsqueeze(2).to_broadcast(big), tend[:, :].unsqueeze(1).to_broadcast(big), ALU.is_ge))
        link(dve.tensor_reduce(t.tab_f[:, :], done[:, :, :], AX.X, ALU.add))
        dve.tensor_scalar(t.tab_f[:, :], t.tab_f[:, :], float(EXPERTS - 1), None, ALU.min)
        link(dve.tensor_tensor(done[:, :, :], done[:, :, :], room[:, :].unsqueeze(1).to_broadcast(big), ALU.mult))
        link(dve.tensor_reduce(tile_f[:, :], done[:, :, :], AX.X, ALU.add))
        link(dve.tensor_tensor(tile_f[:, :], tile_f[:, :], r.COUNT, ALU.add))
        dve.tensor_copy(t.expert[:, :], t.tab_f[0:1, :]).then_inc(t.s_tab, 1)
        dve.tensor_copy(t.tile[:, :], tile_f[0:1, :]).then_inc(t.s_tab, 1)


def spare_rows(eng, empty, xs, s):
    for m in range(SPARE_TILES):
        eng.dma_start(xs[XS_SPARE + m * P:XS_SPARE + (m + 1) * P, :], empty[:, EXPERTS + m, :]).then_inc(s, 16)


def ffn_first(nc, tag, x_in, a, xs, ys, pool_sems):
    with ExitStack() as ctx:
        sems = []

        def sb(name, shape, dt=F32, at=ctx):
            return at.enter_context(nc.sbuf_tensor(f"{tag}_{name}", shape, dt))

        def sem(name):
            sems.append(ctx.enter_context(nc.semaphore(f"{tag}_{name}")))
            return sems[-1]

        psum = [ctx.enter_context(nc.psum_tensor(f"{tag}_bank{i}", [P, 512], F32)) for i in range(8)]
        ident, rw = sb("ident", [P, P]), sb("rw", [P, KCH, EXPERTS])
        wts = Weights(sb, sem)
        table = Table(sb, sem)
        with ExitStack() as rctx:
            def rb(name, shape, dt=F32):
                return sb(name, shape, dt, rctx)

            s_cst, s_init = sem("cst"), sem("init")
            s_x = [sem(f"x{g}") for g in range(GROUPS)]
            def scattered(dve, g):
                pass

            x = [rb(f"x{i}", [P, GT, DIM]) for i in range(GROUPS)]
            empty = rb("empty", [P, EXPERTS + SPARE_TILES, XW])
            r = Routing(rb, sem, psum, a, rw, ident, GROUPS, scattered)
            with nc.Block() as block:

                @block.sync
                def _(sp):
                    for g in range(GROUPS):
                        for b in range(BATCH):
                            sp.dma_start(x[g][:, 2 * b:2 * b + 2, :], x_in[b * SEQ + g * PT:b * SEQ + (g + 1) * PT, :].rearrange("(i p) d -> p i d", p=P)).then_inc(s_x[g], 16)
                        if g == 0:
                            sp.dma_start(ident[:, :], a["ident"]).then_inc(s_cst, 16)
                            sp.dma_start(rw[:, :, :], a["rwt"]).then_inc(s_cst, 16)
                            r.load(sp, s_cst)
                    sp.wait_ge(table.s_zero, 2)
                    spare_rows(sp, empty, xs, s_init)
                    wts.load(sp, a, range(EXPERTS))
                    sp.wait_ge(s_init, 16 * SPARE_TILES)

                @block.vector
                def _(dve):
                    dve.wait_ge(s_cst, 16 * 6)
                    r.start(dve)
                    for g in range(GROUPS + 1):
                        if g < GROUPS:
                            dve.wait_ge(s_x[g], 16 * BATCH)
                            r.norm_vector(dve, g, x[g])
                        if g == 1:
                            table.empty(dve, empty, r.part[:, 0:1])
                        if g > 0:
                            r.choose_vector(dve, g - 1)
                    table.vector(dve, r, rb)

                @block.scalar
                def _(act):
                    for g in range(GROUPS + 1):
                        if g < GROUPS:
                            r.norm_scalar(act, g)
                        if g > 0:
                            r.choose_scalar(act, g - 1)

                @block.tensor
                def _(pe):
                    pe.wait_ge(s_cst, 16 * 6)
                    for g in range(GROUPS + 1):
                        if g < GROUPS:
                            r.gate_tensor(pe, g)
                        if g > 0:
                            r.count_tensor(pe, g - 1)

                @block.gpsimd
                def _(pool):
                    for g in range(GROUPS):
                        pool.wait_ge(r.s_rows, g + 1)
                        for i in range(GT):
                            for c in range(TOPK):
                                r.scatter(pool, g, i, c, xs, pool_sems["scat"])
                    pool.wait_ge(table.s_tail, 1)
                    for e in range(EXPERTS):
                        pool.indirect_dma_start(xs, bass.IndirectOffsetOnAxis(ap=table.tail_u[:, e:e + 1], axis=0), empty[:, e, :], None).then_inc(pool_sems["tail"], 16)
                    pool.wait_ge(pool_sems["scat"], 16 * TOPK * GT * GROUPS)
                    pool.wait_ge(pool_sems["tail"], 16 * EXPERTS)

        experts(nc, ctx, sb, sem, psum, a, ident, table, wts, EXPERTS, xs, ys, pool_sems)
        clear(nc, sems)


class Weights:

    def __init__(self, sb, sem):
        self.w1, self.w2 = sb("w1", [P, EXPERTS * KCH * 2 * INNER]), sb("w2", [P, EXPERTS * ICH * DIM])
        self.s = sem("w")

    def load(self, sp, a, which):
        for e in which:
            if e > 0:
                sp.wait_ge(self.s, 32 * e)
            sp.dma_start(self.w1[:, e * 2048:(e + 1) * 2048].rearrange("p (k f) -> p k f", k=KCH), a["w1t"][e]).then_inc(self.s, 16)
            sp.dma_start(self.w2[:, e * 1024:(e + 1) * 1024].rearrange("p (k f) -> p k f", k=ICH), a["w2t"][e]).then_inc(self.s, 16)


def experts(nc, ctx, sb, sem, psum, a, ident, table, wts, loaded, xs, ys, pool_sems):
    rows = [sb(f"tile{i}", [P, XW]) for i in range(2)]
    rowsT = [sb(f"tileT{i}", [P, KCH * P]) for i in range(2)]
    gate = [sb(f"gate{i}", [P, INNER]) for i in range(2)]
    actT = [sb(f"actT{i}", [P, ICH * P]) for i in range(2)]
    yout = [sb(f"yout{i}", [P, DIM]) for i in range(2)]
    place = [sb(f"place{i}", [P, 1], U32) for i in range(2)]
    first, weight, place_f = ([sb(f"{n}{i}", [P, 1]) for i in range(2)] for n in ("first", "weight", "place_f"))
    s_out = [pool_sems["out0"], pool_sems["out1"]]
    w1, w2 = wts.w1, wts.w2
    p_x = [psum[0][:, 0:DIM], psum[1][:, 0:DIM]]
    p_g, p_u = [psum[2], psum[3]], [psum[4], psum[5]]
    p_t = p_g
    p_y = [psum[6][:, 0:DIM], psum[7][:, 0:DIM]]
    s_in = [sem(f"in{i}") for i in range(2)]
    s_xT, s_xTs, s_first, s_place, s_wt = sem("xT"), sem("xTs"), sem("first"), sem("place"), sem("wt")
    s_g, s_u, s_silu, s_act = sem("g"), sem("u"), sem("silu"), sem("act")
    s_aT, s_aTs, s_y, s_ys, s_go = sem("aT"), sem("aTs"), sem("y"), sem("ys"), sem("go")

    def early(m):
        return isinstance(m, int) and m < 2

    with nc.Block() as block:

        @block.sync
        def _(sp):
            def load(m, b):
                if not early(m):
                    sp.wait_ge(s_xT, m - 1)
                    sp.wait_ge(s_wt, m - 1)
                t = sp.value_load(table.tile[0:1, bass.ds(m, 1)], min_val=0, max_val=XS_SPARE // P + SPARE_TILES - 1)
                sp.dma_start(rows[b][:, :], xs[bass.ds(t * P, P), :]).then_inc(s_in[b], 16)
            for b in range(2):
                load(b, b)
            wts.load(sp, a, range(loaded, EXPERTS))
            with sp.Fori(1, SLOTS // 2) as j:
                for b in range(2):
                    load(2 * j + b, b)

        @block.tensor
        def _(pe):
            def turn_rows(m, j, b):
                pe.wait_ge(s_in[b], 16 * j + 16)
                if not early(m):
                    pe.wait_ge(s_xTs, m - 1)
                for k in range(KCH):
                    t = pe.transpose(p_x[b][:, k * P:(k + 1) * P], rows[b][:, k * P:(k + 1) * P], ident[:, :])
                t.then_inc(s_xT, 1)

            def up(m, b, e, half):
                if half == 0:
                    pe.wait_ge(wts.s, e * 32 + 32)
                    pe.wait_ge(s_xTs, m + 1)
                    if not early(m):
                        pe.wait_ge(s_aTs, m - 1)
                bank = (p_g if half == 0 else p_u)[b]
                for k in range(KCH):
                    t = pe.matmul(bank[:, :], rowsT[b][:, k * P:(k + 1) * P],
                                  w1[:, bass.ds(e * 2048 + (k * 1024 + half * INNER), INNER)],
                                  start=(k == 0), stop=(k == KCH - 1))
                t.then_inc(s_g if half == 0 else s_u, 1)

            def turn_act(m, b):
                pe.wait_ge(s_act, m + 1)
                for k in range(ICH):
                    t = pe.transpose(p_t[b][:, k * P:(k + 1) * P], gate[b][:, k * P:(k + 1) * P], ident[:, :])
                t.then_inc(s_aT, 1)

            def down(m, b, e):
                pe.wait_ge(s_aTs, m + 1)
                if not early(m):
                    pe.wait_ge(s_ys, m - 1)
                for k in range(ICH):
                    t = pe.matmul(p_y[b], actT[b][:, k * P:(k + 1) * P],
                                  w2[:, bass.ds(e * 1024 + k * DIM, DIM)],
                                  start=(k == 0), stop=(k == ICH - 1))
                t.then_inc(s_y, 1)

            def expert(m):
                return pe.value_load(table.expert[0:1, bass.ds(m, 1)], min_val=0, max_val=EXPERTS - 1)

            def step(j, b, last=False):
                m = 2 * j + b
                lead = isinstance(m, int) and m == 0
                if not last:
                    turn_rows(m + 1, j + (b == 1), 1 - b)
                e = expert(m)
                up(m, b, e, 0)
                if not lead:
                    turn_act(m - 1, 1 - b)
                up(m, b, e, 1)
                if not lead:
                    down(m - 1, 1 - b, expert(m - 1))

            turn_rows(0, 0, 0)
            step(0, 0)
            step(0, 1)
            with pe.Fori(1, SLOTS // 2 - 1) as j:
                step(j, 0)
                step(j, 1)
            step(SLOTS // 2 - 1, 0)
            step(SLOTS // 2 - 1, 1, last=True)
            turn_act(SLOTS - 1, 1)
            down(SLOTS - 1, 1, expert(SLOTS - 1))

        @block.scalar
        def _(act):
            def step(m, b):
                act.wait_ge(s_xT, m + 1)
                if not early(m):
                    act.wait_ge(s_u, m - 1)
                act.copy(rowsT[b][:, :], p_x[b]).then_inc(s_xTs, 1)
                act.wait_ge(s_g, m + 1)
                if not early(m):
                    act.wait_ge(s_aT, m - 1)
                act.activation(gate[b][:, :], p_g[b][:, :], ACT.Silu).then_inc(s_silu, 1)
            for b in range(2):
                step(b, b)
            with act.Fori(1, SLOTS // 2) as j:
                for b in range(2):
                    step(2 * j + b, b)

        @block.vector
        def _(dve):
            def meta(m, j, b):
                dve.wait_ge(s_in[b], 16 * j + 16)
                if not early(m):
                    dve.wait_ge(s_ys, m - 1)
                dve.tensor_tensor(first[b][:, :], rows[b][:, DIM + 3:DIM + 4], table.tab_f[:, bass.ds(m, 1)], ALU.is_equal).then_inc(s_first, 1)
                dve.wait_ge(s_first, m + 1)
                dve.scalar_tensor_tensor(out=place_f[b][:, :], in0=first[b][:, :], scalar=float(-TOKENS), in1=rows[b][:, DIM:DIM + 1],
                                         op0=ALU.mult, op1=ALU.add).then_inc(s_place, 1)
                dve.scalar_tensor_tensor(out=weight[b][:, :], in0=first[b][:, :], scalar=rows[b][:, DIM + 1:DIM + 2], in1=rows[b][:, DIM + 2:DIM + 3],
                                         op0=ALU.mult, op1=ALU.add).then_inc(s_wt, 1)

            def step(m, j, b, last=False):
                if not last:
                    meta(m + 1, j + (b == 1), 1 - b)
                dve.wait_ge(s_silu, m + 1)
                dve.wait_ge(s_u, m + 1)
                dve.tensor_tensor(gate[b][:, :], gate[b][:, :], p_u[b][:, :], ALU.mult).then_inc(s_act, 1)
                dve.wait_ge(s_aT, m + 1)
                if not early(m):
                    dve.wait_ge(s_y, m - 1)
                dve.tensor_copy(actT[b][:, :], p_t[b][:, :]).then_inc(s_aTs, 1)
                dve.wait_ge(s_y, m + 1)
                if not early(m):
                    dve.wait_ge(s_out[b], 16 * j)
                dve.wait_ge(s_place, m + 1)
                dve.tensor_copy(place[b][:, :], place_f[b][:, :])
                dve.wait_ge(s_wt, m + 1)
                dve.tensor_scalar(yout[b][:, :], p_y[b], weight[b][:, 0:1], None, ALU.mult).then_inc(s_ys, 1)
            meta(0, 0, 0)
            for b in range(2):
                step(b, 0, b)
            with dve.Fori(1, SLOTS // 2 - 1) as j:
                for b in range(2):
                    step(2 * j + b, j, b)
            step(SLOTS - 2, SLOTS // 2 - 1, 0)
            step(SLOTS - 1, SLOTS // 2 - 1, 1, last=True)

        @block.gpsimd
        def _(pool):
            def step(m, b):
                pool.wait_ge(s_ys, m + 1)
                pool.sem_inc(s_go, 1)
                pool.indirect_dma_start(ys, bass.IndirectOffsetOnAxis(ap=place[b][:, 0:1], axis=0), yout[b][:, :], None).then_inc(s_out[b], 16)
            for b in range(2):
                step(b, b)
            with pool.Fori(1, SLOTS // 2) as j:
                for b in range(2):
                    step(2 * j + b, b)
            for b in range(2):
                pool.wait_ge(s_out[b], 16 * (SLOTS // 2))


def combine(nc, tag, x_in, x_out, ys):
    with ExitStack() as ctx:
        sems = []

        def sem(name):
            sems.append(ctx.enter_context(nc.semaphore(f"{tag}_{name}")))
            return sems[-1]

        def rows(t, g, first=0):
            n = TOKENS // GROUPS
            return t[first + g * n:first + (g + 1) * n, :].rearrange("(i p) d -> p i d", p=P)

        x, y0, y1 = ([ctx.enter_context(nc.sbuf_tensor(f"{tag}_{n}{g}", [P, GT, DIM], F32)) for g in range(GROUPS)] for n in ("x", "y0", "y1"))
        s_in, s_half, s_sum, s_st = [sem(f"in{g}") for g in range(GROUPS)], sem("half"), sem("sum"), sem("st")
        with nc.Block() as block:

            @block.sync
            def _(sp):
                for g in range(GROUPS):
                    for dst, src in ((x, rows(x_in, g)), (y0, rows(ys, g)), (y1, rows(ys, g, TOKENS))):
                        sp.dma_start(dst[g][:, :, :], src).then_inc(s_in[g], 16)
                for g in range(GROUPS):
                    sp.wait_ge(s_sum, g + 1)
                    sp.dma_start(rows(x_out, g), x[g][:, :, :]).then_inc(s_st, 16)
                sp.wait_ge(s_st, 16 * GROUPS)

            @block.vector
            def _(dve):
                for g in range(GROUPS):
                    dve.wait_ge(s_in[g], 48)
                    dve.tensor_tensor(x[g][:, :, :], x[g][:, :, :], y0[g][:, :, :], ALU.add).then_inc(s_half, 1)
                    dve.wait_ge(s_half, g + 1)
                    dve.tensor_tensor(x[g][:, :, :], x[g][:, :, :], y1[g][:, :, :], ALU.add).then_inc(s_sum, 1)

        clear(nc, sems)


def attn_constants():
    c = {}
    p = np.arange(P)
    c["headsum"] = (p[:, None] // HD == p[None, :] // HD).astype(np.float32)
    hc = np.zeros((P, HD), np.float32)
    hc[p, p // HD] = 1.0
    c["headcol"] = hc
    sel = np.zeros((HEADS, 2, P), np.float32)
    for g in range(2):
        sel[g * HQ + p // HD, g, p] = -1.0
    c["negsel"] = sel.reshape(HEADS, 2 * P)
    return c


def attn(nc, x_in, x_out, w, cst, t_scr):
    with ExitStack() as ctx:
        def sb(name, shape, dt=F32, at=ctx):
            return at.enter_context(nc.sbuf_tensor(f"at_{name}", shape, dt))

        sems, kept = [], []

        def sem(name, keep=False):
            s = ctx.enter_context(nc.semaphore(f"at_{name}"))
            (kept if keep else sems).append(s)
            return s

        psum = [ctx.enter_context(nc.psum_tensor(f"at_bank{i}", [P, 512], F32)) for i in range(8)]

        wq, wk, wv, wo = (sb(n, [P, KCH, DIM]) for n in ("wq", "wk", "wv", "wo"))
        nw = sb("nw", [P, KCH])
        wcat = sb("wcat", [P, KCH, FG])
        wrank = sb("wrank", [P, DIM])
        ident, headsum, headcol = sb("ident", [P, P]), sb("headsum", [P, P]), sb("headcol", [P, HD])
        epsk, eps4 = sb("epsk", [P, 1]), sb("eps4", [P, 1])
        mask = sb("mask", [P, UN * GS])
        k, q, kb, v, gt = (sb(n, [P, CHAINS, PT]) for n in ("k", "q", "kb", "v", "gt"))
        eg, ek = sb("eg", [P, CHAINS, UN * GS]), sb("ek", [P, CHAINS, UN * GS])
        lf = ek
        S = sb("S", [P, CHAINS, HD])
        ta = sb("ta", [P, UN, CHAINS, SUB + CT])

        s_w, s_init = sem("w", True), sem("init", True)
        with nc.Block() as block:

            @block.sync
            def _(sp):
                for dst, src in ((wq, "wq"), (wk, "wk"), (wv, "wv"), (wo, "wo"), (wcat, "wcat")):
                    sp.dma_start(dst[:, :, :], w[src]).then_inc(s_w, 16)
                sp.dma_start(wrank[0:RANK, :], w["wf2"]).then_inc(s_w, 16)
                sp.dma_start(wrank[RANK:2 * RANK, :], w["wog2"]).then_inc(s_w, 16)
                sp.dma_start(wrank[2 * RANK:FG, :], cst["negsel"]).then_inc(s_w, 16)
                sp.dma_start(nw[:, :], w["nw"]).then_inc(s_w, 16)
                for dst, src in ((ident, "ident"), (headsum, "headsum"), (headcol, "headcol")):
                    sp.dma_start(dst[:, :], cst[src]).then_inc(s_w, 16)

            @block.vector
            def _(dve):
                dve.memset(epsk[:, :], EPS)
                dve.memset(eps4[:, :], 4 * EPS)
                dve.memset(mask[:, :], 1.0).then_inc(s_init, 1)
                dve.wait_ge(s_init, 1)
                dve.memset(mask[:, :].rearrange("p (u s) -> p u s", s=GS)[:, :, 0:1], 0.0)
                dve.memset(S[:, :, :], 0.0)
                dve.wait_ge(s_w, 192)
                for t in (wq, wk, wv):
                    dve.tensor_scalar(t[:, :, :], t[:, :, :], 0.5, None, ALU.mult)
                for c in range(KCH):
                    dve.tensor_scalar(wo[:, c, :], wo[:, c, :], nw[:, c:c + 1], None, ALU.mult)

        loop = ctx.enter_context(ExitStack())
        s = loop.enter_context(nc.Fori(0, PASSES))
        project(nc, ctx, sb, sem, psum, s, locals())
        decays_and_triangles(nc, ctx, sb, sem, psum, s, locals())
        scan(nc, ctx, sb, sem, psum, s, locals())
        clear(nc, sems)
        loop.close()
        clear(nc, kept)


def project(nc, ctx, sb, sem, psum, s, env):
    (x_in, wq, wk, wv, wcat, wrank, ident, headsum, epsk, k, q, kb, v, gt, lf) = (
        env[n] for n in "x_in wq wk wv wcat wrank ident headsum epsk k q kb v gt lf".split())
    NT = BATCH * PT // P
    with ExitStack() as scope:
        def tb(name, shape):
            return sb(name, shape, at=scope)

        x = tb("x", [P, NT, DIM])
        stats = tb("stats", [P, NT, 6])
        mean, var, rstd, dm = (tb(n, [P, NT]) for n in ("mean", "var", "rstd", "dm"))
        xT = tb("xT", [P, KCH, BATCH * PT])
        fg = tb("fg", [FG, BATCH * PT])
        th = [tb(f"th{i}", [P, 512]) for i in range(2)]
        sq = [tb(f"sq{i}", [P, 512]) for i in range(2)]
        lg = [tb(f"lg{i}", [P, 512]) for i in range(2)]
        rn = [tb(f"rn{i}", [P, 512]) for i in range(2)]

        s_x = [sem(f"x{b}") for b in range(BATCH)]
        s_stat, s_var, s_std, s_xn = sem("stat"), sem("var"), sem("std"), sem("xn")
        s_dve, s_tr, s_xt = sem("dve"), sem("tr"), sem("xt")
        s_fg, s_fgc, s_bt, s_beta = sem("fg"), sem("fgc"), sem("bt"), sem("beta")
        s_mm, s_th, s_ev, s_gt = sem("mm"), sem("th"), sem("ev"), sem("gt")

        JOBS = [(wh, g, c) for wh in range(4) for g in range(2) for c in range(2)]
        NKQV = 12

        def both(t, g, c):
            return t[:, g * BATCH + 2 * c:g * BATCH + 2 * c + 2, :].rearrange("p c t -> p (c t)")

        with nc.Block() as block:

            @block.sync
            def _(sp):
                for b in range(BATCH):
                    sp.dma_start(x[:, 2 * b:2 * b + 2, :], x_in[bass.ds(b * SEQ + s * PT, PT), :].rearrange("(i p) d -> p i d", p=P)).then_inc(s_x[b], 16)

            @block.vector
            def _(dve):
                n = [0]

                def link(ins):
                    n[0] += 1
                    ins.then_inc(s_dve, 1)
                    dve.wait_ge(s_dve, n[0])

                for i in range(NT):
                    if i % 2 == 0:
                        dve.wait_ge(s_x[i // 2], 16)
                    dve.bn_stats(stats[:, i, :], x[:, i, :]).then_inc(s_stat, 1)
                dve.wait_ge(s_stat, NT)
                link(dve.tensor_tensor(mean[:, :], stats[:, :, 1], stats[:, :, 4], ALU.add))
                link(dve.tensor_tensor(dm[:, :], stats[:, :, 1], stats[:, :, 4], ALU.subtract))
                link(dve.tensor_tensor(var[:, :], stats[:, :, 2], stats[:, :, 5], ALU.add))
                link(dve.tensor_tensor(dm[:, :], dm[:, :], dm[:, :], ALU.mult))
                link(dve.tensor_scalar(mean[:, :], mean[:, :], 0.5, None, ALU.mult))
                link(dve.tensor_scalar(var[:, :], var[:, :], 1.0 / DIM, LN_EPS, ALU.mult, ALU.add))
                dve.scalar_tensor_tensor(out=var[:, :], in0=dm[:, :], scalar=0.25, in1=var[:, :],
                                         op0=ALU.mult, op1=ALU.add).then_inc(s_var, 1)
                dve.wait_ge(s_std, 1)
                link(dve.reciprocal(rstd[:, :], rstd[:, :]))
                for i in range(NT):
                    dve.tensor_scalar(x[:, i, :], x[:, i, :], mean[:, i:i + 1], rstd[:, i:i + 1],
                                      ALU.subtract, ALU.mult).then_inc(s_xn, 1)
                for c in range(2):
                    dve.wait_ge(s_fg, c + 1)
                    dve.tensor_copy(fg[0:2 * RANK, c * 512:(c + 1) * 512], psum[2 + c][0:2 * RANK, :]).then_inc(s_fgc, 1)
                dve.wait_ge(s_bt, 2)
                dve.tensor_scalar(fg[2 * RANK:FG, :], fg[2 * RANK:FG, :], 1.0, None, ALU.add).then_inc(s_beta, 1)
                for j, (wh, g, c) in enumerate(JOBS[:NKQV]):
                    dve.wait_ge(s_th, j + 1)
                    dve.scalar_tensor_tensor(out=both((k, q, v)[wh], g, c), in0=th[j % 2][:, :], scalar=1.0, in1=psum[4 + j % 4][:, :],
                                             op0=ALU.add, op1=ALU.mult).then_inc(s_ev, 1)

            @block.scalar
            def _(act):
                act.wait_ge(s_var, 1)
                act.activation(rstd[:, :], var[:, :], ACT.Sqrt).then_inc(s_std, 1)
                for i in range(NT):
                    act.wait_ge(s_tr, i + 1)
                    act.copy(xT[:, :, i * P:(i + 1) * P], psum[i % 2][:, 0:DIM].rearrange("p (k t) -> p k t", k=KCH)).then_inc(s_xt, 1)
                for c in range(2):
                    act.wait_ge(s_fg, c + 1)
                    act.activation(fg[2 * RANK:FG, c * 512:(c + 1) * 512], psum[2 + c][2 * RANK:FG, :], ACT.Tanh, scale=0.5).then_inc(s_bt, 1)
                for j, (wh, g, c) in enumerate(JOBS):
                    act.wait_ge(s_mm, j + 1)
                    if j >= NKQV:
                        act.activation(both(gt, g, c), psum[4 + j % 4][:, :], ACT.Tanh, scale=0.5).then_inc(s_gt, 1)
                        continue
                    if j >= 2:
                        act.wait_ge(s_ev, j - 1)
                    act.activation(th[j % 2][:, :], psum[4 + j % 4][:, :], ACT.Tanh).then_inc(s_th, 1)

            @block.tensor
            def _(pe):
                for i in range(NT):
                    pe.wait_ge(s_xn, i + 1)
                    if i >= 2:
                        pe.wait_ge(s_xt, i - 1)
                    for c in range(KCH):
                        t = pe.transpose(psum[i % 2][:, c * P:(c + 1) * P], x[:, i, c * P:(c + 1) * P], ident[:, :])
                    t.then_inc(s_tr, 1)
                pe.wait_ge(s_xt, NT)
                for c in range(2):
                    for kc in range(KCH):
                        t = pe.matmul(psum[2 + c][0:FG, :], wcat[:, kc, :], xT[:, kc, c * 512:(c + 1) * 512],
                                      start=(kc == 0), stop=(kc == KCH - 1))
                    t.then_inc(s_fg, 1)
                for j, (wh, g, c) in enumerate(JOBS):
                    bank = psum[4 + j % 4]
                    if j >= 4:
                        pe.wait_ge(s_ev, j - 3)
                    if j < NKQV:
                        for kc in range(KCH):
                            t = pe.matmul(bank[:, :], (wk, wq, wv)[wh][:, kc, g * P:(g + 1) * P], xT[:, kc, c * 512:(c + 1) * 512],
                                          start=(kc == 0), stop=(kc == KCH - 1))
                    else:
                        if j == NKQV:
                            pe.wait_ge(s_fgc, 2)
                        t = pe.matmul(bank[:, :], wrank[RANK:2 * RANK, g * P:(g + 1) * P], fg[RANK:2 * RANK, c * 512:(c + 1) * 512], start=True, stop=True)
                    t.then_inc(s_mm, 1)

        s_f, s_a, s_e, s_l, s_lf = sem("f"), sem("a"), sem("e"), sem("l"), sem("lf")
        s_sq, s_ss, s_n1, s_n2, s_kn, s_bb, s_kb = (sem(n) for n in ("sq", "ss", "n1", "n2", "kn", "bb", "kb"))
        JB = [(g, c) for g in range(2) for c in range(2)]

        def pair(t, j):
            g, c = JB[j]
            return t[:, g * BATCH + 2 * c:g * BATCH + 2 * c + 2, :]

        with nc.Block() as block:

            @block.gpsimd
            def _(pool):
                for j in range(4):
                    if j >= 2:
                        pool.wait_ge(s_ss, j - 1)
                    kk = pair(k, j).rearrange("p c t -> p (c t)")
                    pool.tensor_tensor(sq[j % 2][:, :], kk, kk, ALU.mult).then_inc(s_sq, 1)

            @block.tensor
            def _(pe):
                for j, (g, c) in enumerate(JB):
                    pe.matmul(psum[j][:, :], wrank[0:RANK, g * P:(g + 1) * P], fg[0:RANK, c * 512:(c + 1) * 512],
                              start=True, stop=True).then_inc(s_f, 1)
                for j in range(4):
                    pe.wait_ge(s_sq, j + 1)
                    pe.matmul(psum[4 + j][:, :], headsum[:, :], sq[j % 2][:, :], start=True, stop=True).then_inc(s_ss, 1)
                for j, (g, c) in enumerate(JB):
                    pe.wait_ge(s_lf, j + 1)
                    pe.matmul(psum[j][:, :], wrank[2 * RANK:FG, g * P:(g + 1) * P], fg[2 * RANK:FG, c * 512:(c + 1) * 512],
                              start=True, stop=True).then_inc(s_bb, 1)

            @block.scalar
            def _(act):
                act.preload_act_table_set("natural_log_exp_and_others")
                for j in range(4):
                    act.wait_ge(s_f, j + 1)
                    if j >= 2:
                        act.wait_ge(s_lf, j - 1)
                    act.activation(lg[j % 2][:, :], psum[j][:, :], ACT.Abs).then_inc(s_a, 1)
                    act.wait_ge(s_a, j + 1)
                    act.activation(lg[j % 2][:, :], lg[j % 2][:, :], ACT.Exp, scale=-1.0).then_inc(s_e, 1)
                    act.wait_ge(s_e, j + 1)
                    act.activation(lg[j % 2][:, :], lg[j % 2][:, :], ACT.Ln, bias=1.0).then_inc(s_l, 1)
                for j in range(4):
                    act.wait_ge(s_ss, j + 1)
                    if j >= 2:
                        act.wait_ge(s_kn, j - 1)
                    act.activation(rn[j % 2][:, :], psum[4 + j][:, :], ACT.Ln, bias=epsk[:, 0:1]).then_inc(s_n1, 1)
                    act.wait_ge(s_n1, j + 1)
                    act.activation(rn[j % 2][:, :], rn[j % 2][:, :], ACT.Exp, scale=-0.5).then_inc(s_n2, 1)

            @block.vector
            def _(dve):
                dve.memset(lf[:, :, :].rearrange("p c (u s) -> p (c u) s", s=GS)[:, :, 0:1], 0.0)
                for j in range(4):
                    dve.wait_ge(s_l, j + 1)
                    dve.scalar_tensor_tensor(
                        out=pair(lf, j).rearrange("p c (u s) -> p (c u) s", s=GS)[:, :, 1:GS],
                        in0=psum[j][:, :].rearrange("p (u t) -> p u t", t=CT), scalar=0.0,
                        in1=lg[j % 2][:, :].rearrange("p (u t) -> p u t", t=CT), op0=ALU.min, op1=ALU.subtract).then_inc(s_lf, 1)
                for j in range(4):
                    kk = pair(k, j).rearrange("p c t -> p (c t)")
                    dve.wait_ge(s_n2, j + 1)
                    dve.tensor_tensor(kk, kk, rn[j % 2][:, :], ALU.mult).then_inc(s_kn, 1)
                    dve.wait_ge(s_kn, j + 1)
                    dve.wait_ge(s_bb, j + 1)
                    dve.tensor_tensor(pair(kb, j).rearrange("p c t -> p (c t)"), kk, psum[j][:, :], ALU.mult).then_inc(s_kb, 1)


def decays_and_triangles(nc, ctx, sb, sem, psum, s, env):
    (k, q, kb, lf, eg, ek, ta, mask, ident, headcol, t_scr) = (
        env[n] for n in "k q kb lf eg ek ta mask ident headcol t_scr".split())
    NG = CHAINS * UN
    with ExitStack() as outer:
        a_sb = sb("a_sb", [P, NG, 4 * RW], at=outer)
        with ExitStack() as scope:
            def tb(name, shape):
                return sb(name, shape, at=scope)

            E = [tb(f"E{i}", [P, E_OFF[-1]]) for i in range(2)]
            gx = [tb(f"gx{i}", [P, UN * GS]) for i in range(2)]
            fd = [tb(f"fd{i}", [P, PT]) for i in range(2)]
            left = [tb(f"left{i}", [P, UN, 4, LW]) for i in range(2)]
            right = [tb(f"right{i}", [P, UN, 4, RW]) for i in range(2)]
            prod = [tb(f"prod{i}", [P, 3, PT]) for i in range(2)]
            tsum = [tb(f"tsum{i}", [3 * HD, PT]) for i in range(2)]

            s_gx, s_sub, s_exp, s_f = sem("gx"), sem("sub"), sem("exp"), sem("fd")
            s_lr, s_qr, s_kf, s_pr = sem("lr"), sem("qr"), sem("kf"), sem("pr")
            s_A, s_ts, s_tse, s_go = sem("A"), sem("ts"), sem("tse"), sem("ago")
            s_Ae = [sem(f"Ae{i}") for i in range(4)]
            s_tst = [sem(f"tst{i}") for i in range(2)]

            def one(t, c):
                return t[:, bass.ds(c, 1), :]

            def gview(b, lo, T, first, last):
                v = gx[b][:, :].rearrange("p (u s) -> p u s", s=GS)[:, :, lo:lo + CT]
                return v.rearrange("p u (m x) -> p u m x", x=2 * T)[:, :, :, first:last]

            def e_out(b, l, side):
                T = LEVELS[l]
                v = E[b][:, E_OFF[l]:E_OFF[l + 1]].rearrange("p (u m z e) -> p u m z e", m=8 // T, z=2, e=T + 1)
                return v[:, :, :, side, :]

            def e_keys(b, l, side):
                T = LEVELS[l]
                nb = 8 // T
                row = 2 * (T + 1)
                return bass.AP(tensor=E[b], offset=E_OFF[l] + side * (T + 1),
                               ap=[[E_OFF[-1], P], [nb * row, UN], [row, nb], [1, T], [1, 2]])

            def tok(t, c, T, half):
                return one(t, c).rearrange("p a (u m x) -> p (a u) m x", u=UN, x=2 * T)[:, :, :, half * T:half * T + T]

            with nc.Block() as block:

                @block.vector
                def _(dve):
                    def decay(c, b, first):
                        if not first:
                            dve.wait_ge(s_exp, c - 1)
                        dve.tensor_tensor_scan(gx[b][:, :], mask[:, :], one(lf, c).rearrange("p a t -> p (a t)"),
                                               0.0, ALU.mult, ALU.add).then_inc(s_gx, 1)
                        dve.wait_ge(s_gx, c + 1)
                        if not first:
                            dve.wait_ge(s_qr, c - 1)
                        for l, T in enumerate(LEVELS):
                            nb = 8 // T
                            mid = gview(b, 0, T, T, T + 1).to_broadcast([P, UN, nb, T + 1])
                            dve.tensor_tensor(e_out(b, l, 0), mid, gview(b, 0, T, 0, T + 1), ALU.subtract)
                            dve.tensor_tensor(e_out(b, l, 1), gview(b, 1, T, T - 1, 2 * T), mid, ALU.subtract)
                        dve.wait_ge(s_f, c + 1)
                        g17 = gx[b][:, :].rearrange("p (u s) -> p u s", s=GS)
                        dve.tensor_tensor(one(ek, c).rearrange("p a (u s) -> p (a u) s", s=GS),
                                          g17[:, :, CT:GS].to_broadcast([P, UN, GS]), g17, ALU.subtract).then_inc(s_sub, 1)

                    def keys(c, b, first):
                        dve.wait_ge(s_exp, c + 1)
                        if not first:
                            dve.wait_ge(s_A, 4 * c - 4)
                        for l, T in enumerate(LEVELS):
                            nb = 8 // T
                            for dst, t, half in ((left[b][:, :, l, :], k, 0), (right[b][:, :, l, 0:LW], kb, 1)):
                                i = dve.tensor_tensor(dst.rearrange("p u (m t r) -> p u m t r", m=nb, r=2),
                                                      tok(t, c, T, half).unsqueeze(4).to_broadcast([P, UN, nb, T, 2]),
                                                      e_keys(b, l, half), ALU.mult)
                        i.then_inc(s_lr, 1)

                    for b in range(2):
                        decay(b, b, True)
                    for b in range(2):
                        keys(b, b, True)
                    with dve.Fori(1, CHAINS // 2) as j:
                        for b in range(2):
                            decay(2 * j + b, b, False)
                        for b in range(2):
                            keys(2 * j + b, b, False)

                @block.gpsimd
                def _(pool):
                    def step(c, b, first):
                        pool.wait_ge(s_f, c + 1)
                        if not first:
                            pool.wait_ge(s_ts, c - 1)
                        kf, kt, qt = fd[b][:, :], one(k, c).rearrange("p a t -> p (a t)"), one(q, c).rearrange("p a t -> p (a t)")
                        pool.tensor_tensor(kf, kf, kt, ALU.mult).then_inc(s_kf, 1)
                        pool.tensor_tensor(prod[b][:, 2, :], kt, qt, ALU.mult)
                        pool.wait_ge(s_kf, c + 1)
                        pool.tensor_tensor(prod[b][:, 0, :], kf, one(kb, c).rearrange("p a t -> p (a t)"), ALU.mult)
                        pool.tensor_tensor(prod[b][:, 1, :], kf, qt, ALU.mult).then_inc(s_pr, 1)
                        pool.wait_ge(s_exp, c + 1)
                        if not first:
                            pool.wait_ge(s_A, 4 * c - 4)
                        for l, T in enumerate(LEVELS):
                            nb = 8 // T
                            i = pool.tensor_tensor(right[b][:, :, l, LW:RW].rearrange("p u (m t) -> p u m t", m=nb),
                                                   tok(q, c, T, 1), e_out(b, l, 1)[:, :, :, 1:T + 1], ALU.mult)
                        i.then_inc(s_qr, 1)
                    for b in range(2):
                        step(b, b, True)
                    with pool.Fori(1, CHAINS // 2) as j:
                        for b in range(2):
                            step(2 * j + b, b, False)

                @block.scalar
                def _(act):
                    def exps(c, b, first):
                        if not first:
                            act.wait_ge(s_pr, c - 1)
                        act.activation(fd[b][:, :].rearrange("p (u t) -> p u t", t=CT),
                                       one(lf, c).rearrange("p a (u s) -> p (a u) s", s=GS)[:, :, 1:GS], ACT.Exp).then_inc(s_f, 1)
                        act.wait_ge(s_sub, c + 1)
                        act.activation(one(eg, c).rearrange("p a t -> p (a t)"), gx[b][:, :], ACT.Exp)
                        act.activation(one(ek, c), one(ek, c), ACT.Exp)
                        act.activation(E[b][:, :], E[b][:, :], ACT.Exp).then_inc(s_exp, 1)

                    def evac(c, b, stored):
                        for u4 in range(4):
                            act.wait_ge(s_A, 4 * c + u4 + 1)
                            act.copy(a_sb[:, bass.ds(c * UN + 4 * u4, 4), :].rearrange("p u c -> p (u c)"), psum[u4][:, 0:16 * RW]).then_inc(s_Ae[u4], 1)
                        act.wait_ge(s_ts, c + 1)
                        if stored is not None:
                            act.wait_ge(s_tst[b], 48 * stored)
                        act.copy(tsum[b][:, :], psum[4 + b][0:3 * HD, 0:PT]).then_inc(s_tse, 1)
                    for b in range(2):
                        exps(b, b, True)
                    for b in range(2):
                        exps(2 + b, b, False)
                        evac(b, b, None)
                    with act.Fori(1, CHAINS // 2 - 1) as j:
                        for b in range(2):
                            exps(2 * j + 2 + b, b, False)
                            evac(2 * j + b, b, j)
                    for b in range(2):
                        evac(CHAINS - 2 + b, b, CHAINS // 2 - 1)

                @block.tensor
                def _(pe):
                    def step(c, b, first):
                        pe.wait_ge(s_pr, c + 1)
                        if not first:
                            pe.wait_ge(s_tse, c - 1)
                        pe.wait_ge(s_lr, c + 1)
                        pe.wait_ge(s_qr, c + 1)
                        if not (isinstance(c, int) and c == 0):
                            pe.wait_ge(s_Ae[0], c)
                        for kind in range(3):
                            t = pe.matmul(psum[4 + b][kind * HD:kind * HD + HD, 0:PT], headcol[:, :], prod[b][:, kind, :], start=True, stop=True)
                        t.then_inc(s_ts, 1)
                        for u4 in range(4):
                            if u4 > 0 and not (isinstance(c, int) and c == 0):
                                pe.wait_ge(s_Ae[u4], c)
                                pe.sem_inc(s_go, 1)
                            for uu in range(4):
                                u = 4 * u4 + uu
                                for pk in range(2):
                                    for h in range(HQ):
                                        r = slice(HD * h, HD * h + HD)
                                        o = uu * 4 * RW + pk * 2 * RW
                                        t = pe.matmul(psum[u4][r, o:o + 2 * RW],
                                                      left[b][r, u, 2 * pk:2 * pk + 2, :].rearrange("p l c -> p (l c)"),
                                                      right[b][r, u, 2 * pk:2 * pk + 2, :].rearrange("p l c -> p (l c)"), start=True, stop=True)
                            t.then_inc(s_A, 1)
                    for b in range(2):
                        step(b, b, True)
                    with pe.Fori(1, CHAINS // 2) as j:
                        for b in range(2):
                            step(2 * j + b, b, False)

                @block.sync
                def _(sp):
                    def step(c, b):
                        sp.wait_ge(s_tse, c + 1)
                        for kind in range(3):
                            sp.dma_start(t_scr[bass.ds(c, 1), HQ * kind:HQ * kind + HQ, bass.ds(s * PT, PT)].rearrange("a h t -> (a h) t"),
                                         tsum[b][kind * HD:kind * HD + HQ, :]).then_inc(s_tst[b], 16)
                    with sp.Fori(0, CHAINS // 2) as j:
                        for b in range(2):
                            step(2 * j + b, b)
                    for b in range(2):
                        sp.wait_ge(s_tst[b], 48 * (CHAINS // 2))

        invert(nc, outer, sb, sem, psum, s, env, a_sb)


def invert(nc, scope, sb, sem, psum, s, env, a_sb):
    ident, ta, t_scr = (env[n] for n in ("ident", "ta", "t_scr"))

    def tb(name, shape):
        return sb(name, shape, at=scope)

    ng, tm = tb("ng", [P, HQ * HS]), tb("tm", [P, HQ * HS])
    aq = tb("aq", [P, CT, HQ, SUB])
    zz, pr = tb("zz", [P, HQ * CT * CT]), tb("pr", [P, 3, HQ * CT * CT])
    tk = tb("tk", [P, 3 * HQ, CT])

    s_tk, s_zero, s_one, s_tp, s_ev = sem("tk"), sem("zero"), sem("one"), sem("tp"), sem("gev")
    s_diag, s_aq, s_tc, s_bk, s_bke = sem("diag"), sem("aq"), sem("tc"), sem("bk"), sem("bke")
    s_inv = {"vector": sem("invV"), "pool": sem("invP")}
    SHARE = {"vector": (0, 3), "pool": (3, 4)}
    GROUPS = 24
    SIZES = (2, 4, 8, 16)
    LAST = 2 * (2 * CT - 1)
    STEPS = sum(2 * (2 * m - 1) for m in SIZES)

    def square(t):
        return t[:, :].rearrange("p (h x) -> p h x", h=HQ)[:, :, 0:SUB * SUB].rearrange("p h (j i) -> p h j i", i=SUB)

    ngv, tmv = square(ng), square(tm)
    tc = a_sb[:, :, :].rearrange("p g c -> p (g c)")[:, 0:SUB * HQ * SUB].rearrange("p (j h i) -> p j h i", j=SUB, h=HQ)

    def level(n):
        return len(LEVELS) - 1 - n // 6

    def runs(n):
        gq, T = n % 6, LEVELS[level(n)]
        out = []
        per = 2 * T if gq < 4 else T
        base = 4 * (gq if gq < 4 else gq - 4)
        cc = 0
        while cc < 4:
            m, xx = (base + cc) // per, (base + cc) % per
            cnt = min(4 - cc, per - xx)
            row0 = 4 * T * m + 2 * T + xx if gq < 4 else 2 * T * m + T + xx
            out.append((cc, cnt, gq >= 4, row0, 4 * T * m, 2 * T * m, 2 * T))
            cc += cnt
        return out

    def inverse(eng, name):
        h0, h1 = SHARE[name]
        done = s_inv[name]
        n = [0]

        def step(ins):
            n[0] += 1
            ins.then_inc(done, 1)
            if n[0] > 1:
                eng.wait_ge(done, n[0] - 1)

        for size, m in enumerate(SIZES):
            eng.wait_ge(s_ev, 6 * (size + 1))
            blocks = (h1 - h0) * SUB // (2 * m)

            def blk(t, j0, nj, i0, ni, dj=SUB, di=1):
                return bass.AP(tensor=t, offset=h0 * HS + j0 * SUB + i0,
                               ap=[[HQ * HS, P], [2 * m * (SUB + 1), blocks], [dj, nj], [di, ni]])

            def temp(t):
                return t[:, h0 * CT * CT:h0 * CT * CT + blocks * m * m].rearrange("p (b j i) -> p b j i", b=blocks, j=m)

            z, pv = temp(zz), [temp(pr[:, i, :]) for i in range(3)]

            def product(mult, add):
                step(mult(0))
                for x in range(1, m):
                    step(mult(x))
                    if x > 1:
                        step(add(x - 1))
                step_wait()
                step(add(m - 1))
                step_wait()

            def step_wait():
                eng.wait_ge(done, n[0])

            def zmult(x):
                kk = m - 1 - x
                dst = z if x == 0 else pv[x % 3]
                return eng.tensor_tensor(dst[:, :, :, 0:kk + 1], blk(ng, m, m, kk, kk + 1, di=0), blk(tm, kk, m, 0, kk + 1, dj=0), ALU.mult)

            def zadd(x):
                kk = m - 1 - x
                return eng.tensor_tensor(z[:, :, :, 0:kk + 1], z[:, :, :, 0:kk + 1], pv[x % 3][:, :, :, 0:kk + 1], ALU.add)

            def xmult(kk):
                rows = m - kk
                out = blk(tm, m, m, 0, m) if kk == 0 else pv[kk % 3][:, :, 0:rows, :]
                return eng.tensor_tensor(out, blk(tm, m + kk, rows, m + kk, m, di=0), z[:, :, kk:kk + 1, :].to_broadcast([P, blocks, rows, m]), ALU.mult)

            def xadd(kk):
                rows = m - kk
                out = blk(tm, m + kk, rows, 0, m)
                return eng.tensor_tensor(out, out, pv[kk % 3][:, :, 0:rows, :], ALU.add)

            product(zmult, zadd)
            product(xmult, xadd)
        assert n[0] == STEPS

    with nc.Block() as block:

        @block.sync
        def _(sp):
            for c in range(CHAINS):
                sp.dma_start(tk[c * UN:(c + 1) * UN, :, :],
                             t_scr[c, :, bass.ds(s * PT, PT)].rearrange("k (u t) -> u k t", t=CT)).then_inc(s_tk, 16)

        @block.tensor
        def _(pe):
            for n in range(GROUPS):
                if n >= 8:
                    pe.wait_ge(s_ev, n - 7)
                for cc in range(4):
                    col = level(n) * RW + 4 * (n % 6) + cc
                    t = pe.transpose(psum[n % 8][:, cc * P:(cc + 1) * P], a_sb[:, :, col], ident[:, :])
                t.then_inc(s_tp, 1)
            for n in range(12):
                if n == 0:
                    pe.wait_ge(s_ev, GROUPS)
                    pe.wait_ge(s_aq, 2)
                if n == 4:
                    pe.wait_ge(s_tc, 2)
                if n == 8:
                    pe.wait_ge(s_tc, 3)
                if n >= 8:
                    pe.wait_ge(s_bke, n - 7)
                for cc in range(4):
                    src = aq[:, 4 * n + cc, :, :] if n < 4 else tc[:, 4 * (n - 4) + cc, :, :]
                    t = pe.transpose(psum[n % 8][:, cc * P:(cc + 1) * P], src.rearrange("p h i -> p (h i)"), ident[:, :])
                t.then_inc(s_bk, 1)

        @block.scalar
        def _(act):
            act.wait_ge(s_zero, 1)
            for n in range(GROUPS):
                act.wait_ge(s_tp, n + 1)
                bank = psum[n % 8][:, :].rearrange("p (c h l i) -> p h c l i", c=4, h=HQ, l=2)
                for cc, cnt, isq, row0, i0, l0, width in runs(n):
                    src = bank[:, :, cc:cc + cnt, level(n) % 2, l0:l0 + width]
                    dst = (aq[:, :, :, :].rearrange("p t h i -> p h t i") if isq else ngv)[:, :, row0:row0 + cnt, i0:i0 + width]
                    i = act.copy(dst, src)
                i.then_inc(s_ev, 1)

            def compact(rows, cols):
                act.copy(tc[:, rows, :, cols], tmv[:, :, rows, cols].rearrange("p h j i -> p j h i")).then_inc(s_tc, 1)

            for n in range(12):
                if n == 4:
                    for e in s_inv.values():
                        act.wait_ge(e, STEPS - LAST)
                    compact(slice(0, CT), slice(0, SUB))
                    compact(slice(CT, SUB), slice(CT, SUB))
                if n == 8:
                    for e in s_inv.values():
                        act.wait_ge(e, STEPS)
                    compact(slice(CT, SUB), slice(0, CT))
                act.wait_ge(s_bk, n + 1)
                col = SUB + 4 * n if n < 4 else 4 * (n - 4)
                act.copy(ta[:, :, :, col:col + 4].rearrange("p u c j -> p c u j"),
                         psum[n % 8][:, :].rearrange("p (j c u) -> p c u j", j=4, c=CHAINS)).then_inc(s_bke, 1)

        @block.gpsimd
        def _(pool):
            pool.memset(aq[:, :, :, :], 0.0).then_inc(s_zero, 1)
            pool.wait_ge(s_zero, 1)
            pool.wait_ge(s_tk, 16 * CHAINS)
            for x in range(2):
                dst = bass.AP(tensor=aq, offset=x, ap=[[HQ * CT * SUB, P], [SUB, HQ], [HQ * SUB + 2, CT]])
                pool.tensor_copy(dst, tk[:, (1 + x) * HQ:(2 + x) * HQ, :]).then_inc(s_aq, 1)
            pool.wait_ge(s_one, 2)
            pool.wait_ge(s_diag, 1)
            inverse(pool, "pool")

        @block.vector
        def _(dve):
            dve.memset(tm[:, :], 0.0).then_inc(s_one, 1)
            dve.wait_ge(s_one, 1)
            dve.memset(tm[:, :].rearrange("p (h j s) -> p h j s", h=HQ, s=SUB + 1)[:, :, :, 0:1], 1.0).then_inc(s_one, 1)
            dve.wait_ge(s_tk, 16 * CHAINS)
            dst = bass.AP(tensor=tm, offset=SUB, ap=[[HQ * HS, P], [HS, HQ], [2 * (SUB + 1), CT]])
            dve.tensor_copy(dst, tk[:, 0:HQ, :]).then_inc(s_diag, 1)
            dve.wait_ge(s_one, 2)
            dve.wait_ge(s_diag, 1)
            inverse(dve, "vector")


def scan(nc, ctx, sb, sem, psum, s, env):
    k, q, kb, v, gt, eg, ek, ta, S, x_in, x_out, wo, headsum, eps4 = (
        env[n] for n in "k q kb v gt eg ek ta S x_in x_out wo headsum eps4".split())
    HC = CHAINS // 2
    KQ = SUB + CT
    RO = KQ + SUB
    with ExitStack() as scope:
        def tb(name, shape):
            return sb(name, shape, at=scope)

        o = tb("o", [P, CHAINS, PT])
        kq = [tb(f"kq{i}", [P, CHAINS, KQ]) for i in range(2)]
        kd = [tb(f"kd{i}", [P, CHAINS, SUB]) for i in range(2)]
        tu = [tb(f"tu{i}", [P, CHAINS, SUB]) for i in range(2)]
        ar = [tb(f"ar{i}", [P, CHAINS, KQ]) for i in range(2)]
        vi = [tb(f"vi{i}", [P, CHAINS, CT, 2]) for i in range(2)]
        Rt = [tb(f"Rt{i}", [P, HC, SUB]) for i in range(2)]
        R, U, D, dS = ([tb(f"{n}{i}", [P, HC, HD]) for i in range(2)] for n in ("R", "U", "D", "dS"))
        b_p = [psum[f][:, 0:HC * RO].rearrange("p (c x) -> p c x", c=HC) for f in range(2)]
        b_u = [psum[2 + f][:, 0:HC * HD] for f in range(2)]

        s_pad, s_go = sem("pad"), sem("go")
        s_kq, s_kd, s_kr, s_ta, s_vi = sem("kq"), sem("kd"), sem("kr"), sem("ta"), sem("vi")
        s_r, s_u, s_d, s_Rt, s_R, s_dec, s_dS, s_S, s_U, s_O = ([sem(f"{n}{f}") for f in range(2)] for n in
            ("r", "u", "d", "Rts", "Rs", "dec", "dSs", "Ss", "Us", "Os"))

        with nc.Block() as block:

            @block.gpsimd
            def _(pool):
                for i in range(2):
                    pool.memset(vi[i][:, :, :, 0:1], 0.0).then_inc(s_pad, 1)

                def stage(u, b, first):
                    def t(x, at=0, step=CT):
                        return x[:, :, bass.ds(u * step + at, CT)]
                    if not first:
                        pool.wait_ge(s_r[1], u - 1)
                        pool.wait_ge(s_kr, u - 1)
                        pool.wait_ge(s_Rt[1], u - 1)
                    keys = kq[b][:, :, 0:SUB].rearrange("p c (t r) -> p c t r", r=2)
                    ends = kd[b][:, :, :].rearrange("p c (t r) -> p c t r", r=2)
                    for r in range(2):
                        pool.tensor_tensor(keys[:, :, :, r], t(kb), t(eg, r, GS), ALU.mult)
                    pool.tensor_tensor(kq[b][:, :, SUB:KQ], t(q), t(eg, 1, GS), ALU.mult).then_inc(s_kq, 1)
                    pool.tensor_copy(vi[b][:, :, :, 1], t(v)).then_inc(s_vi, 1)
                    for r in range(2):
                        i = pool.tensor_tensor(ends[:, :, :, r], t(k), t(ek, r, GS), ALU.mult)
                    i.then_inc(s_kd, 1)
                for b in range(2):
                    stage(b, b, True)
                with pool.Fori(1, UN // 2) as j:
                    for b in range(2):
                        stage(2 * j + b, b, False)

            @block.tensor
            def _(pe):
                def step(u, b, first):
                    def tiles(product):
                        for c in range(HC):
                            for h in range(HQ):
                                i = product(c, slice(HD * h, HD * h + HD))
                        return i
                    for f in range(2):
                        ch = HC * f
                        if f == 0:
                            pe.wait_ge(s_kq, u + 1)
                        if not (isinstance(u, int) and u == 0):
                            pe.wait_ge(s_S[f], u)
                            pe.wait_ge(s_O[f], u)
                        pe.sem_inc(s_go, 1)
                        tiles(lambda c, r: pe.matmul(b_p[f][r, c, 0:KQ], S[r, ch + c, :], kq[b][r, ch + c, :],
                                                     start=(c == 0), stop=False, skip_group_check=True)).then_inc(s_r[f], 1)
                    for f in range(2):
                        ch = HC * f
                        if f == 0:
                            pe.wait_ge(s_ta, u + 1)
                        pe.wait_ge(s_R[f], u + 1)
                        pe.sem_inc(s_go, 1)
                        tiles(lambda c, r: pe.matmul(b_u[f][r, c * HD:(c + 1) * HD], tu[b][r, ch + c, :], R[f][r, c, :],
                                                     start=True, stop=True)).then_inc(s_u[f], 1)
                    for f in range(2):
                        ch = HC * f
                        if f == 0:
                            pe.wait_ge(s_kr, u + 1)
                        pe.wait_ge(s_U[f], u + 1)
                        pe.sem_inc(s_go, 1)
                        tiles(lambda c, r: pe.matmul(b_p[f][r, c, SUB:RO], U[f][r, c, :], ar[b][r, ch + c, :],
                                                     start=False, stop=(c == HC - 1), skip_group_check=True)).then_inc(s_d[f], 1)
                for b in range(2):
                    step(b, b, True)
                with pe.Fori(1, UN // 2) as j:
                    for b in range(2):
                        step(2 * j + b, b, False)

            @block.scalar
            def _(act):
                def stage(u, b, first):
                    if not first:
                        act.wait_ge(s_d[1], u - 1)
                    row = ta[:, bass.ds(u, 1), :, :].rearrange("p a c j -> p (a c) j")
                    act.copy(tu[b][:, :, :], row[:, :, 0:SUB])
                    act.copy(ar[b][:, :, 0:CT], row[:, :, SUB:KQ]).then_inc(s_ta, 1)

                def step(u, b, first, last):
                    for f in range(2):
                        act.wait_ge(s_u[f], u + 1)
                        if not (isinstance(u, int) and u == 0):
                            act.wait_ge(s_d[f], u)
                        act.copy(U[f][:, :, :].rearrange("p c v -> p (c v)"), b_u[f]).then_inc(s_U[f], 1)
                    for f in range(2):
                        act.wait_ge(s_dS[f], u + 1)
                        act.copy(o[:, HC * f:HC * f + HC, bass.ds(u * CT, CT)], b_p[f][:, :, SUB:KQ]).then_inc(s_O[f], 1)
                    if not last:
                        stage(u + 2, b, False)
                for b in range(2):
                    stage(b, b, True)
                for b in range(2):
                    step(b, b, True, False)
                with act.Fori(1, UN // 2 - 1) as j:
                    for b in range(2):
                        step(2 * j + b, b, False, False)
                for b in range(2):
                    step(UN - 2 + b, b, False, True)

            @block.vector
            def _(dve):
                def turn(u, b):
                    dve.wait_ge(s_kd, u + 1)
                    dve.transpose(ar[b][:, :, CT:KQ], kd[b][:, :, :]).then_inc(s_kr, 1)

                def step(u, b, last):
                    for f in range(2):
                        ch = slice(HC * f, HC * f + HC)
                        if f == 0:
                            dve.wait_ge(s_vi, u + 1)
                        dve.wait_ge(s_r[f], u + 1)
                        dve.tensor_tensor(Rt[f][:, :, :], vi[b][:, ch, :, :].rearrange("p c t r -> p c (t r)"),
                                          b_p[f][:, :, 0:SUB], ALU.add).then_inc(s_Rt[f], 1)
                        dve.wait_ge(s_Rt[f], u + 1)
                        dve.transpose(R[f][:, :, :], Rt[f][:, :, :]).then_inc(s_R[f], 1)
                        if not (isinstance(u, int) and u == 0):
                            dve.wait_ge(s_S[f], u)
                        dve.tensor_tensor(D[f][:, :, :], S[:, ch, :], eg[:, ch, bass.ds(u * GS + CT, 1)].to_broadcast([P, HC, HD]), ALU.mult).then_inc(s_dec[f], 1)
                    if not last:
                        turn(u + 1, 1 - b)
                    for f in range(2):
                        ch = slice(HC * f, HC * f + HC)
                        dve.wait_ge(s_d[f], u + 1)
                        dve.transpose(dS[f][:, :, :], b_p[f][:, :, KQ:RO]).then_inc(s_dS[f], 1)
                        dve.wait_ge(s_dec[f], u + 1)
                        dve.wait_ge(s_dS[f], u + 1)
                        dve.tensor_tensor(S[:, ch, :], D[f][:, :, :], dS[f][:, :, :], ALU.add).then_inc(s_S[f], 1)
                dve.wait_ge(s_pad, 2)
                turn(0, 0)
                step(0, 0, False)
                step(1, 1, False)
                with dve.Fori(1, UN // 2 - 1) as j:
                    for b in range(2):
                        step(2 * j + b, b, False)
                step(UN - 2, 0, False)
                step(UN - 1, 1, True)

        NT = BATCH * PT // P
        x, y = tb("res", [P, NT, DIM]), tb("y", [P, NT, DIM])
        sq = [tb(f"ysq{i}", [P, 512]) for i in range(2)]
        rn = [tb(f"yrn{i}", [P, 512]) for i in range(2)]
        s_x, s_y, s_sq, s_ss, s_l, s_rn, s_yn, s_mm, s_out, s_st = (
            sem("e" + n) for n in ("x", "y", "sq", "ss", "l", "rn", "yn", "mm", "out", "st"))

        def rows(t, b):
            return t[bass.ds(b * SEQ + s * PT, PT), :].rearrange("(i p) d -> p i d", p=P)

        JOBS = [(g, c) for c in range(2) for g in range(2)]

        def both(t, j):
            g, c = JOBS[j]
            return t[:, g * BATCH + 2 * c:g * BATCH + 2 * c + 2, :].rearrange("p c t -> p (c t)")

        with nc.Block() as block:

            @block.sync
            def _(sp):
                for b in range(BATCH):
                    sp.dma_start(x[:, 2 * b:2 * b + 2, :], rows(x_in, b)).then_inc(s_x, 16)
                for b in range(BATCH):
                    sp.wait_ge(s_out, 2 * b + 2)
                    sp.dma_start(rows(x_out, b), y[:, 2 * b:2 * b + 2, :]).then_inc(s_st, 16)
                sp.wait_ge(s_st, 16 * BATCH)

            @block.gpsimd
            def _(pool):
                for j in range(4):
                    pool.wait_ge(s_y, j + 1)
                    if j >= 2:
                        pool.wait_ge(s_ss, j - 1)
                    pool.tensor_tensor(sq[j % 2][:, :], both(o, j), both(o, j), ALU.mult).then_inc(s_sq, 1)

            @block.tensor
            def _(pe):
                for j in range(4):
                    pe.wait_ge(s_sq, j + 1)
                    pe.matmul(psum[j][:, :], headsum[:, :], sq[j % 2][:, :], start=True, stop=True).then_inc(s_ss, 1)
                for i in range(NT):
                    b, half = i // 2, i % 2
                    pe.wait_ge(s_yn, 2 * (b // 2) + 2)
                    if i >= 4:
                        pe.wait_ge(s_out, i - 3)
                    for g in range(2):
                        t = pe.matmul(psum[4 + i % 4][:, 0:DIM], o[:, g * BATCH + b, half * P:(half + 1) * P], wo[:, g, :], start=(g == 0), stop=(g == 1))
                    t.then_inc(s_mm, 1)

            @block.scalar
            def _(act):
                for j in range(4):
                    act.wait_ge(s_ss, j + 1)
                    if j >= 2:
                        act.wait_ge(s_yn, j - 1)
                    act.activation(rn[j % 2][:, :], psum[j][:, :], ACT.Ln, bias=eps4[:, 0:1], scale=1.0 / HD).then_inc(s_l, 1)
                    act.wait_ge(s_l, j + 1)
                    act.activation(rn[j % 2][:, :], rn[j % 2][:, :], ACT.Exp, scale=-0.5).then_inc(s_rn, 1)

            @block.vector
            def _(dve):
                for j in range(4):
                    dve.scalar_tensor_tensor(out=both(o, j), in0=both(gt, j), scalar=1.0, in1=both(o, j), op0=ALU.add, op1=ALU.mult).then_inc(s_y, 1)
                for j in range(4):
                    dve.wait_ge(s_rn, j + 1)
                    dve.tensor_tensor(both(o, j), both(o, j), rn[j % 2][:, :], ALU.mult).then_inc(s_yn, 1)
                dve.wait_ge(s_x, 16 * BATCH)
                for i in range(NT):
                    dve.wait_ge(s_mm, i + 1)
                    dve.tensor_tensor(y[:, i, :], x[:, i, :], psum[4 + i % 4][:, 0:DIM], ALU.add).then_inc(s_out, 1)


def pool_dma_semaphores(nc, ctx, tag):
    return {n: ctx.enter_context(nc.semaphore(f"{tag}_{n}")) for n in ("scat", "tail", "out0", "out1")}


def macaron(nc, a, x, out):
    def scratch(name, shape):
        return nc.dram_tensor(name, shape, F32, kind="Internal").ap()

    with ExitStack() as ctx:
        pool_sems = [pool_dma_semaphores(nc, ctx, tag) for tag in ("pool1", "pool2")]
        x1, x2 = scratch("x1", [TOKENS, DIM]), scratch("x2", [TOKENS, DIM])
        xs, ys = scratch("xs", [XS_ROWS, XW]), scratch("ys", [YS_ROWS, DIM])
        ffn_first(nc, "ffn1", x, a, xs, ys, pool_sems[0])
        combine(nc, "sum1", x, x1, ys)
        attn(nc, x1, x2, a, a, scratch("t", [CHAINS, 3 * HQ, SEQ]))
        ffn_first(nc, "ffn2", x2, a, xs, ys, pool_sems[1])
        combine(nc, "sum2", x2, out, ys)


def layouts(i):
    def chunks(w):
        return w.reshape(KCH, P, -1).transpose(1, 0, 2)

    w = {n: i["L0_attn_" + n] for n in "Wq Wk Wv Wf1 Wf2 Wbeta Wog1 Wog2 norm_w Wo".split()}
    return {
        "x": i["L0_attn_x"].reshape(TOKENS, DIM),
        "wq": chunks(w["Wq"]), "wk": chunks(w["Wk"]), "wv": chunks(w["Wv"]), "wo": chunks(w["Wo"]),
        "wcat": chunks(np.concatenate([w["Wf1"], w["Wog1"], w["Wbeta"]], 1)),
        "wf2": w["Wf2"], "wog2": w["Wog2"], "nw": w["norm_w"].reshape(KCH, P).T,
        "w1t": i["L0_ffn_w1"].transpose(0, 2, 1).reshape(EXPERTS, KCH, P, 2 * INNER).transpose(0, 2, 1, 3),
        "w2t": i["L0_ffn_w2"].transpose(0, 2, 1).reshape(EXPERTS, ICH, P, DIM).transpose(0, 2, 1, 3),
        "rwt": i["L0_ffn_router_w"].T.reshape(KCH, P, EXPERTS).transpose(1, 0, 2),
        **ffn_constants(), **attn_constants(),
    }


def kernel(**inputs):
    import concourse.bacc as _bacc
    from concourse.bass_utils import run_bass_kernel_spmd as _run

    nc = _bacc.Bacc("TRN2", target_bir_lowering=False, num_devices=1)
    arrays, aps = {}, {}
    for name, a in layouts({k: np.asarray(v) for k, v in inputs.items()}).items():
        a = np.ascontiguousarray(a)
        arrays[f"in_{name}_dram"] = a
        aps[name] = nc.dram_tensor(f"in_{name}_dram", a.shape, mybir.dt.from_np(a.dtype), kind="ExternalInput").ap()
    out = nc.dram_tensor("out_0_dram", (TOKENS, DIM), F32, kind="ExternalOutput").ap()
    macaron(nc, aps, aps["x"], out)
    r = _run(nc, [arrays], core_ids=[0])
    return r.results[0]["out_0_dram"].reshape(BATCH, SEQ, DIM)
```

```python
import numpy as np
from contextlib import ExitStack
import concourse.bass as bass
from concourse import mybir

F32 = mybir.dt.float32
I32 = mybir.dt.int32
U32 = mybir.dt.uint32
ALU = mybir.AluOpType
ACT = mybir.ActivationFunctionType
AX = mybir.AxisListType
P = 128

BATCH, SEQ, DIM = 4, 1024, 256
TOKENS = BATCH * SEQ
KCH = DIM // P
EXPERTS, INNER, TOPK = 8, 512, 2
TILES = TOKENS // P
ICH = INNER // P
LN_EPS = 1e-5
SLOTS = TOKENS * TOPK // P + EXPERTS - 1
PAIRS = SLOTS // 2
assert SLOTS == 2 * PAIRS + 1
SPARE_TILES = EXPERTS - 1
ROOM = TOKENS + P
XS_SPARE = EXPERTS * ROOM
XS_ROWS = XS_SPARE + SPARE_TILES * P
XW = DIM + 4
YS_ROWS = TOPK * TOKENS + (EXPERTS + SPARE_TILES) * P
GROUPS = 4
GT = TOKENS // P // GROUPS

HEADS, HD = 8, 32
HQ = P // HD
CHAINS = (HEADS // HQ) * BATCH
RANK = 32
EPS = 1e-6
CT = 16
SUB = 2 * CT
UN = 16
PT = CT * UN
PASSES = SEQ // PT
GS = CT + 1
LEVELS = (8, 4, 2, 1)
LW, RW = 16, 24
COARSE = 2
FINE = []
for _l in range(COARSE, len(LEVELS)):
    for _q in range(2):
        FINE.append((_l, _q, sum(f[3] * f[4] * f[5] for f in FINE), 8 // LEVELS[_l], 2 * LEVELS[_l], (2 - _q) * LEVELS[_l]))
FE = sum(f[3] * f[4] * f[5] for f in FINE)
PIECE = UN * FE // 8
E_OFF = [0]
for _T in LEVELS:
    E_OFF.append(E_OFF[-1] + UN * (8 // _T) * 2 * (_T + 1))
HS = 33 * SUB
FG = 2 * RANK + HEADS


def clear(nc, sems):
    nums = sorted(s.num for s in sems)
    starts = [n for i, n in enumerate(nums) if i == 0 or nums[i - 1] != n - 1]
    ends = [n for i, n in enumerate(nums) if i == len(nums) - 1 or nums[i + 1] != n + 1]
    runs = [range(a, b + 1) for a, b in zip(starts, ends)]
    with nc.Block() as block:

        @block.sync
        def _(sp):
            for x in runs[0::3]:
                sp.sem_clear(x)

        @block.scalar
        def _(act):
            for x in runs[1::3]:
                act.sem_clear(x)

        @block.vector
        def _(dve):
            for x in runs[2::3]:
                dve.sem_clear(x)


def ffn_constants():
    c = {}
    c["ident"] = np.eye(P, dtype=np.float32)
    c["lower"] = np.triu(np.ones((P, P), np.float32), 1)
    c["ones"] = np.ones((P, P), np.float32)
    e = np.arange(EXPERTS)
    row = np.concatenate([
        (e[None, :] < e[:, None]).ravel(),
        e, e * ROOM,
        np.arange(TOKENS // P) * P, np.arange(SLOTS),
    ]).astype(np.float32)
    c["row"] = np.repeat(row[None, :], P, 0)
    p = np.arange(P, dtype=np.float32)[:, None]
    i = np.arange(GT, dtype=np.float32)[None, :]
    c["part"] = np.concatenate([p, TOKENS + p + SEQ * (i // (GT // BATCH)) + P * (i % (GT // BATCH))], 1).astype(np.float32)
    return c


class Routing:

    def __init__(self, lasting, sb, sem, banks, rw, ident, buffers):
        self.rw, self.ident = rw, ident
        self.lower, self.ones, self.row, self.part, self.next = (lasting[n] for n in ("lower", "ones", "row", "part", "next"))
        self.rows = [sb(f"rows{i}", [P, GT, XW]) for i in range(buffers)]
        self.slot_u = [sb(f"slot_u{i}", [P, TOPK, GT], U32) for i in range(buffers)]
        self.stats, self.xt = sb("stats", [P, GT, 6]), [sb(f"xt{i}", [P, KCH, P]) for i in range(2)]
        self.mean, self.var, self.rstd, self.dm = (sb(n, [P, GT]) for n in ("mean", "var", "rstd", "dm"))
        self.prob, self.rank, self.both, self.slot, self.pick = (
            sb(n, [P, GT, EXPERTS]) for n in ("prob", "rank", "both", "slot", "pick"))
        self.tmax, self.tsum = sb("tmax", [P, GT]), sb("tsum", [P, GT])
        self.beats, self.ties = sb("beats", [P, GT * 64]), sb("ties", [P, GT * 64])
        self.sel, self.upto = sb("sel", [P, TOPK, GT, EXPERTS]), sb("upto", [P, EXPERTS, GT])
        self.slot_f, self.wtop = sb("slot_f", [P, TOPK, GT]), sb("wtop", [P, TOPK, GT])
        self.p_t, self.p_g, self.p_c = banks[0:2], banks[2:4], banks[4:6]
        (self.s_stat, self.s_var, self.s_std, self.s_xn, self.s_tr, self.s_xt, self.s_gate, self.s_sub, self.s_exp,
         self.s_both, self.s_cnt, self.s_rows, self.s_own) = (
            sem("r_" + n) for n in "stat var std xn tr xt gate sub exp both cnt rows own".split())
        k = 64
        self.LT = self.row[:, 0:k]
        self.EXPERT, self.FIRST = (self.row[:, k + EXPERTS * i:k + EXPERTS * (i + 1)] for i in range(2))
        k += 2 * EXPERTS
        self.STEPS, self.COUNT = self.row[:, k:k + TOKENS // P], self.row[:, k + TOKENS // P:]
        self.token = self.part[:, 1:1 + GT]
        self.links = 0

    @staticmethod
    def lasting(sb, cst):
        return {"lower": sb("lower", [P, P]), "ones": sb("ones", [P, P]), "row": sb("row", [P, cst["row"].shape[1]]),
                "part": sb("part", [P, 1 + GT]), "next": sb("next", [P, EXPERTS])}

    @staticmethod
    def load(sp, lasting, cst, s_cst):
        for n in ("lower", "ones", "row", "part"):
            sp.dma_start(lasting[n][:, :], cst[n]).then_inc(s_cst, 16)

    @staticmethod
    def start(dve, lasting):
        return dve.tensor_copy(lasting["next"][:, :], lasting["row"][:, 64 + EXPERTS:64 + 2 * EXPERTS])

    def link(self, dve, ins):
        self.links += 1
        ins.then_inc(self.s_own, 1)
        dve.wait_ge(self.s_own, self.links)

    def stats_vector(self, dve, x, i):
        dve.bn_stats(self.stats[:, i, :], x[:, i, :]).then_inc(self.s_stat, 1)

    def moments_vector(self, dve, g):
        r = self

        def link(ins):
            r.link(dve, ins)

        dve.wait_ge(r.s_stat, GT * (g + 1))
        dve.tensor_tensor(r.mean[:, :], r.stats[:, :, 1], r.stats[:, :, 4], ALU.add)
        dve.tensor_tensor(r.dm[:, :], r.stats[:, :, 1], r.stats[:, :, 4], ALU.subtract)
        link(dve.tensor_tensor(r.var[:, :], r.stats[:, :, 2], r.stats[:, :, 5], ALU.add))
        dve.tensor_tensor(r.dm[:, :], r.dm[:, :], r.dm[:, :], ALU.mult)
        dve.tensor_scalar(r.mean[:, :], r.mean[:, :], 0.5, None, ALU.mult)
        link(dve.tensor_scalar(r.var[:, :], r.var[:, :], 1.0 / DIM, LN_EPS, ALU.mult, ALU.add))
        dve.scalar_tensor_tensor(out=r.var[:, :], in0=r.dm[:, :], scalar=0.25, in1=r.var[:, :],
                                 op0=ALU.mult, op1=ALU.add).then_inc(r.s_var, 1)

    def norm_vector(self, dve, g, x):
        r, b = self, g % len(self.rows)
        dve.wait_ge(r.s_std, g + 1)
        r.link(dve, dve.reciprocal(r.rstd[:, :], r.rstd[:, :]))
        for i in range(GT):
            dve.tensor_scalar(r.rows[b][:, i, 0:DIM], x[:, i, :], r.mean[:, i:i + 1], r.rstd[:, i:i + 1],
                              ALU.subtract, ALU.mult).then_inc(r.s_xn, 1)

    def logits_vector(self, dve, g):
        r = self
        logits = r.p_g[g % 2][:, 0:GT * EXPERTS].rearrange("p (i e) -> p i e", e=EXPERTS)
        dve.wait_ge(r.s_gate, GT * (g + 1))
        r.link(dve, dve.tensor_reduce(r.tmax[:, :], logits, AX.X, ALU.max))
        dve.tensor_tensor(r.prob[:, :, :], logits, r.tmax[:, :].unsqueeze(2).to_broadcast([P, GT, EXPERTS]), ALU.subtract).then_inc(r.s_sub, 1)

    def choose_vector(self, dve, g, meanwhile=None):
        r, b = self, g % len(self.rows)
        cube3, big = [P, GT, EXPERTS], [P, GT, EXPERTS, EXPERTS]

        def link(ins):
            r.link(dve, ins)

        dve.wait_ge(r.s_exp, g + 1)
        link(dve.tensor_reduce(r.tsum[:, :], r.prob[:, :, :], AX.X, ALU.add))
        link(dve.reciprocal(r.tsum[:, :], r.tsum[:, :]))
        link(dve.tensor_tensor(r.prob[:, :, :], r.prob[:, :, :], r.tsum[:, :].unsqueeze(2).to_broadcast(cube3), ALU.mult))
        def cube(t):
            return t[:, :].rearrange("p (i e f) -> p i e f", e=EXPERTS, f=EXPERTS)
        other, mine = r.prob[:, :, :].unsqueeze(2).to_broadcast(big), r.prob[:, :, :].unsqueeze(3).to_broadcast(big)
        dve.tensor_tensor(cube(r.beats), other, mine, ALU.is_gt)
        link(dve.tensor_tensor(cube(r.ties), other, mine, ALU.is_equal))
        ties = r.ties[:, :].rearrange("p (i f) -> p i f", f=64)
        link(dve.tensor_tensor(ties, ties, r.LT.unsqueeze(1).to_broadcast([P, GT, 64]), ALU.mult))
        link(dve.tensor_tensor(r.beats[:, :], r.beats[:, :], r.ties[:, :], ALU.add))
        link(dve.tensor_reduce(r.rank[:, :, :], cube(r.beats), AX.X, ALU.add))
        dve.tensor_scalar(r.both[:, :, :], r.rank[:, :, :], float(TOPK), None, ALU.is_lt).then_inc(r.s_both, 1)
        for c in range(TOPK):
            i = dve.tensor_scalar(r.sel[:, c, :, :], r.rank[:, :, :], float(c), None, ALU.is_equal)
        link(i)
        for c in range(TOPK):
            link(dve.tensor_tensor(r.pick[:, :, :], r.sel[:, c, :, :], r.prob[:, :, :], ALU.mult))
            link(dve.tensor_reduce(r.wtop[:, c, :], r.pick[:, :, :], AX.X, ALU.add))
        link(dve.tensor_scalar(r.wtop[:, :, :], r.wtop[:, :, :], 0.5, None, ALU.mult))
        meta = [r.rows[b][:, :, DIM + i] for i in range(4)]
        dve.tensor_copy(meta[0], r.token)
        dve.tensor_tensor(meta[1], r.wtop[:, 0, :], r.wtop[:, 1, :], ALU.subtract)
        dve.tensor_copy(meta[2], r.wtop[:, 1, :])
        link(dve.tensor_tensor(r.pick[:, :, :], r.sel[:, 0, :, :], r.EXPERT.unsqueeze(1).to_broadcast(cube3), ALU.mult))
        link(dve.tensor_reduce(meta[3], r.pick[:, :, :], AX.X, ALU.add))
        link(dve.tensor_scalar(r.token, r.token, float(SEQ // GROUPS), None, ALU.add))
        if meanwhile is not None:
            meanwhile()
        dve.wait_ge(r.s_cnt, 2 * (g + 1))
        before = r.p_c[0][:, 0:GT * EXPERTS].rearrange("p (i e) -> p i e", e=EXPERTS)
        totals = r.p_c[1][:, 0:GT * EXPERTS].rearrange("p (i e) -> p e i", e=EXPERTS)
        for e in range(EXPERTS):
            i = dve.tensor_tensor_scan(r.upto[:, e, :], r.ones[:, 0:GT], totals[:, e, :], 0.0, ALU.mult, ALU.add)
        link(i)
        link(dve.tensor_tensor(r.slot[:, :, :], r.upto[:, :, :].rearrange("p e i -> p i e"), totals.rearrange("p e i -> p i e"), ALU.subtract))
        link(dve.tensor_tensor(r.slot[:, :, :], r.slot[:, :, :], before, ALU.add))
        link(dve.tensor_tensor(r.slot[:, :, :], r.slot[:, :, :], r.next[:, :].unsqueeze(1).to_broadcast(cube3), ALU.add))
        link(dve.tensor_tensor(r.next[:, :], r.next[:, :], r.upto[:, :, GT - 1], ALU.add))
        for c in range(TOPK):
            link(dve.tensor_tensor(r.pick[:, :, :], r.sel[:, c, :, :], r.slot[:, :, :], ALU.mult))
            link(dve.tensor_reduce(r.slot_f[:, c, :], r.pick[:, :, :], AX.X, ALU.add))
        dve.tensor_copy(r.slot_u[b][:, :, :], r.slot_f[:, :, :]).then_inc(r.s_rows, 1)

    def std_scalar(self, act, g):
        act.wait_ge(self.s_var, g + 1)
        act.activation(self.rstd[:, :], self.var[:, :], ACT.Sqrt).then_inc(self.s_std, 1)

    def turn_scalar(self, act, g):
        r = self
        for i in range(GT):
            n = GT * g + i
            act.wait_ge(r.s_tr, n + 1)
            if n >= 2:
                act.wait_ge(r.s_gate, n - 1)
            act.copy(r.xt[n % 2][:, :, :].rearrange("p k t -> p (k t)"), r.p_t[n % 2][:, 0:DIM]).then_inc(r.s_xt, 1)

    def choose_scalar(self, act, g):
        r = self
        act.wait_ge(r.s_sub, g + 1)
        act.activation(r.prob[:, :, :], r.prob[:, :, :], ACT.Exp).then_inc(r.s_exp, 1)

    def gate_tensor(self, pe, g):
        r, b = self, g % len(self.rows)

        def gate(i):
            n = GT * g + i
            pe.wait_ge(r.s_xt, n + 1)
            if i == 0 and g > 1:
                pe.wait_ge(r.s_sub, g - 1)
            for k in range(KCH):
                t = pe.matmul(r.p_g[g % 2][:, i * EXPERTS:(i + 1) * EXPERTS], r.xt[n % 2][:, k, :], r.rw[:, k, :], start=(k == 0), stop=(k == KCH - 1))
            t.then_inc(r.s_gate, 1)

        for i in range(GT):
            n = GT * g + i
            pe.wait_ge(r.s_xn, n + 1)
            if n >= 2:
                pe.wait_ge(r.s_xt, n - 1)
            for k in range(KCH):
                t = pe.transpose(r.p_t[n % 2][:, k * P:(k + 1) * P], r.rows[b][:, i, k * P:(k + 1) * P], r.ident[:, :])
            t.then_inc(r.s_tr, 1)
            if i > 0:
                gate(i - 1)
        gate(GT - 1)

    def count_tensor(self, pe, g):
        r = self
        pe.wait_ge(r.s_both, g + 1)
        if g > 0:
            pe.wait_ge(r.s_rows, g)
        flat = r.both[:, :, :].rearrange("p i e -> p (i e)")
        pe.matmul(r.p_c[0][:, 0:GT * EXPERTS], r.lower[:, :], flat, start=True, stop=True).then_inc(r.s_cnt, 1)
        pe.matmul(r.p_c[1][:, 0:GT * EXPERTS], r.ones[:, :], flat, start=True, stop=True).then_inc(r.s_cnt, 1)

    def scatter(self, pool, b, i, c, xs, s_scat):
        pool.indirect_dma_start(xs, bass.IndirectOffsetOnAxis(ap=self.slot_u[b][:, c, i:i + 1], axis=0),
                                self.rows[b][:, i, :], None).then_inc(s_scat, 16)


class Table:

    def __init__(self, sb, sem):
        self.tab_f = sb("tab_f", [P, SLOTS])
        self.expert, self.tile = sb("tab_e", [1, SLOTS], I32), sb("tab_t", [1, SLOTS], I32)
        self.tail = sb("tail", [1, EXPERTS], I32)
        self.s_tab, self.s_tail, self.s_zero = sem("t_tab"), sem("t_tail"), sem("t_zero")

    def empty(self, pool, rows, part):
        pool.memset(rows[:, :, :], 0.0).then_inc(self.s_zero, 1)
        pool.wait_ge(self.s_zero, 1)
        for i in range(EXPERTS + SPARE_TILES):
            pool.tensor_scalar(rows[:, i, DIM:DIM + 1], part, float(TOPK * TOKENS + i * P), None, ALU.add)
        pool.memset(rows[:, :, XW - 1:XW], -1.0).then_inc(self.s_zero, 1)

    def vector(self, dve, r, tb):
        t = self
        need = tb("need", [P, EXPERTS, TOKENS // P])
        cnt, ntile, tend, room = (tb(n, [P, EXPERTS]) for n in ("cnt", "ntile", "tend", "room"))
        done, tile_f = tb("done", [P, SLOTS, EXPERTS]), tb("tile_f", [P, SLOTS])

        def link(ins):
            r.link(dve, ins)

        dve.tensor_copy(t.tail[:, :], r.next[0:1, :]).then_inc(t.s_tail, 1)
        big = [P, EXPERTS, TOKENS // P]
        link(dve.tensor_tensor(cnt[:, :], r.next[:, :], r.FIRST, ALU.subtract))
        link(dve.tensor_tensor(need[:, :, :], cnt[:, :].unsqueeze(2).to_broadcast(big), r.STEPS.unsqueeze(1).to_broadcast(big), ALU.is_gt))
        link(dve.tensor_reduce(ntile[:, :], need[:, :, :], AX.X, ALU.add))
        link(dve.tensor_tensor_scan(tend[:, :], r.ones[:, 0:EXPERTS], ntile[:, :], 0.0, ALU.mult, ALU.add))
        dve.tensor_scalar(room[:, :], ntile[:, :], -1.0, float(ROOM // P), ALU.mult, ALU.add)
        big = [P, SLOTS, EXPERTS]
        link(dve.tensor_tensor(done[:, :, :], r.COUNT.unsqueeze(2).to_broadcast(big), tend[:, :].unsqueeze(1).to_broadcast(big), ALU.is_ge))
        link(dve.tensor_reduce(t.tab_f[:, :], done[:, :, :], AX.X, ALU.add))
        dve.tensor_scalar(t.tab_f[:, :], t.tab_f[:, :], float(EXPERTS - 1), None, ALU.min)
        link(dve.tensor_tensor(done[:, :, :], done[:, :, :], room[:, :].unsqueeze(1).to_broadcast(big), ALU.mult))
        link(dve.tensor_reduce(tile_f[:, :], done[:, :, :], AX.X, ALU.add))
        link(dve.tensor_tensor(tile_f[:, :], tile_f[:, :], r.COUNT, ALU.add))
        dve.tensor_copy(t.expert[:, :], t.tab_f[0:1, :]).then_inc(t.s_tab, 1)
        dve.tensor_copy(t.tile[:, :], tile_f[0:1, :]).then_inc(t.s_tab, 1)


    def tails(self, sp, empty, xs, s):
        sp.wait_ge(self.s_zero, 2)
        sp.wait_ge(self.s_tail, 1)
        for e in range(EXPERTS):
            row = sp.value_load(self.tail[0:1, e:e + 1], min_val=0, max_val=XS_SPARE - P)
            sp.dma_start(xs[bass.ds(row, P), :], empty[:, e, :]).then_inc(s, 16)


def spare_rows(eng, empty, xs, s):
    for m in range(SPARE_TILES):
        eng.dma_start(xs[XS_SPARE + m * P:XS_SPARE + (m + 1) * P, :], empty[:, EXPERTS + m, :]).then_inc(s, 16)


def ffn_first(nc, tag, x_in, a, xs, ys, pool_sems):
    with ExitStack() as ctx:
        sems = []

        def sb(name, shape, dt=F32, at=ctx):
            return at.enter_context(nc.sbuf_tensor(f"{tag}_{name}", shape, dt))

        def sem(name):
            sems.append(ctx.enter_context(nc.semaphore(f"{tag}_{name}")))
            return sems[-1]

        psum = [ctx.enter_context(nc.psum_tensor(f"{tag}_bank{i}", [P, 512], F32)) for i in range(8)]
        ident, rw = sb("ident", [P, P]), sb("rw", [P, KCH, EXPERTS])
        wts = Weights(sb, sem)
        table = Table(sb, sem)
        with ExitStack() as rctx:
            def rb(name, shape, dt=F32):
                return sb(name, shape, dt, rctx)

            s_cst, s_init = sem("cst"), sem("init")
            s_x = [sem(f"x{g}") for g in range(GROUPS)]
            x = [rb(f"x{i}", [P, GT, DIM]) for i in range(GROUPS)]
            empty = rb("empty", [P, EXPERTS + SPARE_TILES, XW])
            lasting = Routing.lasting(rb, a)
            r = Routing(lasting, rb, sem, psum, rw, ident, GROUPS)
            with nc.Block() as block:

                @block.sync
                def _(sp):
                    for g in range(GROUPS):
                        for b in range(BATCH):
                            sp.dma_start(x[g][:, 2 * b:2 * b + 2, :], x_in[b * SEQ + g * PT:b * SEQ + (g + 1) * PT, :].rearrange("(i p) d -> p i d", p=P)).then_inc(s_x[g], 16)
                        if g == 0:
                            sp.dma_start(ident[:, :], a["ident"]).then_inc(s_cst, 16)
                            sp.dma_start(rw[:, :, :], a["rwt"]).then_inc(s_cst, 16)
                            Routing.load(sp, lasting, a, s_cst)
                    sp.wait_ge(table.s_zero, 2)
                    spare_rows(sp, empty, xs, s_init)
                    wts.load(sp, a, range(EXPERTS))
                    table.tails(sp, empty, xs, s_init)
                    sp.wait_ge(s_init, 16 * (SPARE_TILES + EXPERTS))

                @block.vector
                def _(dve):
                    dve.wait_ge(s_cst, 16 * 6)
                    r.link(dve, Routing.start(dve, lasting))
                    for g in range(GROUPS + 1):
                        if g < GROUPS:
                            dve.wait_ge(s_x[g], 16 * BATCH)
                            for i in range(GT):
                                r.stats_vector(dve, x[g], i)
                            r.moments_vector(dve, g)
                        if g > 0:
                            r.logits_vector(dve, g - 1)
                        if g < GROUPS:
                            r.norm_vector(dve, g, x[g])
                        if g > 0:
                            r.choose_vector(dve, g - 1)
                    table.vector(dve, r, rb)

                @block.scalar
                def _(act):
                    for g in range(GROUPS + 1):
                        if g < GROUPS:
                            r.std_scalar(act, g)
                        if g > 0:
                            r.choose_scalar(act, g - 1)
                        if g < GROUPS:
                            r.turn_scalar(act, g)

                @block.tensor
                def _(pe):
                    pe.wait_ge(s_cst, 16 * 6)
                    for g in range(GROUPS + 1):
                        if g > 0:
                            r.count_tensor(pe, g - 1)
                        if g < GROUPS:
                            r.gate_tensor(pe, g)

                @block.gpsimd
                def _(pool):
                    pool.wait_ge(s_cst, 16 * 6)
                    table.empty(pool, empty, r.part[:, 0:1])
                    for g in range(GROUPS):
                        pool.wait_ge(r.s_rows, g + 1)
                        for i in range(GT):
                            for c in range(TOPK):
                                r.scatter(pool, g, i, c, xs, pool_sems["scat"])
                    pool.wait_ge(pool_sems["scat"], 16 * TOPK * GT * GROUPS)

        experts(nc, ctx, sb, sem, psum, a, ident, table, wts, EXPERTS, xs, ys, pool_sems)
        clear(nc, sems)


def ffn_second(nc, tag, a, table, x_in, x_out, xs, ys, pool_sems):
    with ExitStack() as ctx:
        sems = []

        def sb(name, shape, dt=F32, at=ctx):
            return at.enter_context(nc.sbuf_tensor(f"{tag}_{name}", shape, dt))

        def sem(name):
            sems.append(ctx.enter_context(nc.semaphore(f"{tag}_{name}")))
            return sems[-1]

        psum = [ctx.enter_context(nc.psum_tensor(f"{tag}_bank{i}", [P, 512], F32)) for i in range(8)]
        ident, x, s_x = sb("ident", [P, P]), sb("x", [P, TILES, DIM]), sem("x")
        experts(nc, ctx, sb, sem, psum, a, ident, table, Weights(sb, sem), 0, xs, ys, pool_sems, (x_in, x, s_x))
        combine(nc, sb, sem, x, s_x, x_out, ys)
        clear(nc, sems)


class Weights:

    def __init__(self, sb, sem):
        self.w1, self.w2 = sb("w1", [P, EXPERTS * KCH * 2 * INNER]), sb("w2", [P, EXPERTS * ICH * DIM])
        self.s = sem("w")

    def load(self, sp, a, which):
        for e in which:
            if e > 0:
                sp.wait_ge(self.s, 32 * e)
            sp.dma_start(self.w1[:, e * 2048:(e + 1) * 2048].rearrange("p (k f) -> p k f", k=KCH), a["w1t"][e]).then_inc(self.s, 16)
            sp.dma_start(self.w2[:, e * 1024:(e + 1) * 1024].rearrange("p (k f) -> p k f", k=ICH), a["w2t"][e]).then_inc(self.s, 16)


def token_rows(t, first, count):
    return t[first:first + count * P, :].rearrange("(i p) d -> p i d", p=P)


def experts(nc, ctx, sb, sem, psum, a, ident, table, wts, loaded, xs, ys, pool_sems, residual=None):
    rows = [sb(f"tile{i}", [P, XW]) for i in range(2)]
    rowsT = [sb(f"tileT{i}", [P, KCH * P]) for i in range(2)]
    gate = [sb(f"gate{i}", [P, INNER]) for i in range(2)]
    actT = [sb(f"actT{i}", [P, ICH * P]) for i in range(2)]
    yout = [sb(f"yout{i}", [P, DIM]) for i in range(2)]
    place = [sb(f"place{i}", [P, 1], U32) for i in range(2)]
    first, weight, place_f = ([sb(f"{n}{i}", [P, 1]) for i in range(2)] for n in ("first", "weight", "place_f"))
    s_out = [pool_sems["out0"], pool_sems["out1"]]
    w1, w2 = wts.w1, wts.w2
    p_x = [psum[0][:, 0:DIM], psum[1][:, 0:DIM]]
    p_g, p_u = [psum[2], psum[3]], [psum[4], psum[5]]
    p_t = p_g
    p_y = [psum[6][:, 0:DIM], psum[7][:, 0:DIM]]
    s_in = [sem(f"in{i}") for i in range(2)]
    s_xT, s_xTs, s_first, s_place, s_wt = sem("xT"), sem("xTs"), sem("first"), sem("place"), sem("wt")
    s_g, s_u, s_silu, s_act = sem("g"), sem("u"), sem("silu"), sem("act")
    s_aT, s_aTs, s_y, s_ys, s_go, s_id = sem("aT"), sem("aTs"), sem("y"), sem("ys"), sem("go"), sem("id")

    def early(m):
        return isinstance(m, int) and m < 2

    with nc.Block() as block:

        @block.sync
        def _(sp):
            def load(m, b):
                if not early(m):
                    sp.wait_ge(s_xT, m - 1)
                    sp.wait_ge(s_wt, m - 1)
                t = sp.value_load(table.tile[0:1, bass.ds(m, 1)], min_val=0, max_val=XS_SPARE // P + SPARE_TILES - 1)
                sp.dma_start(rows[b][:, :], xs[bass.ds(t * P, P), :]).then_inc(s_in[b], 16)
            sp.dma_start(ident[:, :], a["ident"]).then_inc(s_id, 16)
            for b in range(2):
                load(b, b)
            if loaded == 0:
                wts.load(sp, a, range(1))
            rest = list(range(max(loaded, 1), EXPERTS))
            ahead = 2 * ((len(rest) + 1) // 2)
            for m in range(2, 2 + ahead):
                load(m, m % 2)
                wts.load(sp, a, rest[m - 2:m - 1])
            if residual is not None:
                src, dst, s_dst = residual
                for g in range(GROUPS):
                    sp.dma_start(dst[:, g * GT:(g + 1) * GT, :], token_rows(src, g * GT * P, GT)).then_inc(s_dst, 16)
            with sp.Fori(1 + ahead // 2, PAIRS) as j:
                for b in range(2):
                    load(2 * j + b, b)
            load(SLOTS - 1, 0)

        @block.tensor
        def _(pe):
            def turn_rows(m, j, b):
                pe.wait_ge(s_in[b], 16 * j + 16)
                if not early(m):
                    pe.wait_ge(s_xTs, m - 1)
                for k in range(KCH):
                    t = pe.transpose(p_x[b][:, k * P:(k + 1) * P], rows[b][:, k * P:(k + 1) * P], ident[:, :])
                t.then_inc(s_xT, 1)

            def up(m, b, e, half):
                if half == 0:
                    pe.wait_ge(wts.s, e * 32 + 32)
                    pe.wait_ge(s_xTs, m + 1)
                    if not early(m):
                        pe.wait_ge(s_aTs, m - 1)
                bank = (p_g if half == 0 else p_u)[b]
                for k in range(KCH):
                    t = pe.matmul(bank[:, :], rowsT[b][:, k * P:(k + 1) * P],
                                  w1[:, bass.ds(e * 2048 + (k * 1024 + half * INNER), INNER)],
                                  start=(k == 0), stop=(k == KCH - 1))
                t.then_inc(s_g if half == 0 else s_u, 1)

            def turn_act(m, b):
                pe.wait_ge(s_act, m + 1)
                for k in range(ICH):
                    t = pe.transpose(p_t[b][:, k * P:(k + 1) * P], gate[b][:, k * P:(k + 1) * P], ident[:, :])
                t.then_inc(s_aT, 1)

            def down(m, b, e):
                pe.wait_ge(s_aTs, m + 1)
                if not early(m):
                    pe.wait_ge(s_ys, m - 1)
                for k in range(ICH):
                    t = pe.matmul(p_y[b], actT[b][:, k * P:(k + 1) * P],
                                  w2[:, bass.ds(e * 1024 + k * DIM, DIM)],
                                  start=(k == 0), stop=(k == ICH - 1))
                t.then_inc(s_y, 1)

            def expert(m):
                return pe.value_load(table.expert[0:1, bass.ds(m, 1)], min_val=0, max_val=EXPERTS - 1)

            def step(j, b, last=False):
                m = 2 * j + b
                lead = isinstance(m, int) and m == 0
                if not last:
                    turn_rows(m + 1, j + (b == 1), 1 - b)
                e = expert(m)
                up(m, b, e, 0)
                if not lead:
                    turn_act(m - 1, 1 - b)
                up(m, b, e, 1)
                if not lead:
                    down(m - 1, 1 - b, expert(m - 1))

            pe.wait_ge(s_id, 16)
            turn_rows(0, 0, 0)
            step(0, 0)
            step(0, 1)
            with pe.Fori(1, PAIRS) as j:
                step(j, 0)
                step(j, 1)
            step(PAIRS, 0, last=True)
            turn_act(SLOTS - 1, 0)
            down(SLOTS - 1, 0, expert(SLOTS - 1))

        @block.scalar
        def _(act):
            def step(m, b):
                act.wait_ge(s_xT, m + 1)
                if not early(m):
                    act.wait_ge(s_u, m - 1)
                act.copy(rowsT[b][:, :], p_x[b]).then_inc(s_xTs, 1)
                act.wait_ge(s_g, m + 1)
                if not early(m):
                    act.wait_ge(s_aT, m - 1)
                act.activation(gate[b][:, :], p_g[b][:, :], ACT.Silu).then_inc(s_silu, 1)
            for b in range(2):
                step(b, b)
            with act.Fori(1, PAIRS) as j:
                for b in range(2):
                    step(2 * j + b, b)
            step(SLOTS - 1, 0)

        @block.vector
        def _(dve):
            def meta(m, j, b):
                dve.wait_ge(s_in[b], 16 * j + 16)
                if not early(m):
                    dve.wait_ge(s_ys, m - 1)
                dve.tensor_tensor(first[b][:, :], rows[b][:, DIM + 3:DIM + 4], table.tab_f[:, bass.ds(m, 1)], ALU.is_equal).then_inc(s_first, 1)
                dve.wait_ge(s_first, m + 1)
                dve.scalar_tensor_tensor(out=place_f[b][:, :], in0=first[b][:, :], scalar=float(-TOKENS), in1=rows[b][:, DIM:DIM + 1],
                                         op0=ALU.mult, op1=ALU.add).then_inc(s_place, 1)
                dve.scalar_tensor_tensor(out=weight[b][:, :], in0=first[b][:, :], scalar=rows[b][:, DIM + 1:DIM + 2], in1=rows[b][:, DIM + 2:DIM + 3],
                                         op0=ALU.mult, op1=ALU.add).then_inc(s_wt, 1)

            def weigh(m, j, b):
                dve.wait_ge(s_y, m + 1)
                if not early(m):
                    dve.wait_ge(s_out[b], 16 * j)
                dve.wait_ge(s_place, m + 1)
                dve.tensor_copy(place[b][:, :], place_f[b][:, :])
                dve.wait_ge(s_wt, m + 1)
                dve.tensor_scalar(yout[b][:, :], p_y[b], weight[b][:, 0:1], None, ALU.mult).then_inc(s_ys, 1)

            def step(m, j, b, last=False):
                dve.wait_ge(s_silu, m + 1)
                dve.wait_ge(s_u, m + 1)
                dve.tensor_tensor(gate[b][:, :], gate[b][:, :], p_u[b][:, :], ALU.mult).then_inc(s_act, 1)
                if not (isinstance(m, int) and m == 0):
                    weigh(m - 1, j if b == 1 else j - 1, 1 - b)
                if not last:
                    meta(m + 1, j + (b == 1), 1 - b)
                dve.wait_ge(s_aT, m + 1)
                if not early(m):
                    dve.wait_ge(s_y, m - 1)
                dve.tensor_copy(actT[b][:, :], p_t[b][:, :]).then_inc(s_aTs, 1)
            meta(0, 0, 0)
            for b in range(2):
                step(b, 0, b)
            for b in range(2):
                step(2 + b, 1, b)
            with dve.Fori(2, PAIRS) as j:
                for b in range(2):
                    step(2 * j + b, j, b)
            step(SLOTS - 1, PAIRS, 0, last=True)
            weigh(SLOTS - 1, PAIRS, 0)

        @block.gpsimd
        def _(pool):
            def step(m, b):
                pool.wait_ge(s_ys, m + 1)
                pool.sem_inc(s_go, 1)
                pool.indirect_dma_start(ys, bass.IndirectOffsetOnAxis(ap=place[b][:, 0:1], axis=0), yout[b][:, :], None).then_inc(s_out[b], 16)
            for b in range(2):
                step(b, b)
            with pool.Fori(1, PAIRS) as j:
                for b in range(2):
                    step(2 * j + b, b)
            step(SLOTS - 1, 0)
            for b in range(2):
                pool.wait_ge(s_out[b], 16 * (PAIRS + 1 - b))


def combine(nc, sb, sem, x, s_x, x_out, ys):
    y0, y1 = ([sb(f"{n}{g}", [P, GT, DIM]) for g in range(GROUPS)] for n in ("y0", "y1"))
    s_y, s_half, s_sum, s_st = [sem(f"ys{g}") for g in range(GROUPS)], sem("half"), sem("sum"), sem("st")
    with nc.Block() as block:

        @block.sync
        def _(sp):
            for g in range(GROUPS):
                for dst, first in ((y0, 0), (y1, TOKENS)):
                    sp.dma_start(dst[g][:, :, :], token_rows(ys, first + g * GT * P, GT)).then_inc(s_y[g], 16)
            for g in range(GROUPS):
                sp.wait_ge(s_sum, g + 1)
                sp.dma_start(token_rows(x_out, g * GT * P, GT), x[:, g * GT:(g + 1) * GT, :]).then_inc(s_st, 16)
            sp.wait_ge(s_st, 16 * GROUPS)

        @block.vector
        def _(dve):
            dve.wait_ge(s_x, 16 * GROUPS)
            for g in range(GROUPS):
                mine = x[:, g * GT:(g + 1) * GT, :]
                dve.wait_ge(s_y[g], 32)
                dve.tensor_tensor(mine, mine, y0[g][:, :, :], ALU.add).then_inc(s_half, 1)
                dve.wait_ge(s_half, g + 1)
                dve.tensor_tensor(mine, mine, y1[g][:, :, :], ALU.add).then_inc(s_sum, 1)


def attn_constants():
    c = {}
    p = np.arange(P)
    c["headsum"] = (p[:, None] // HD == p[None, :] // HD).astype(np.float32)
    hc = np.zeros((P, HD), np.float32)
    hc[p, p // HD] = 1.0
    c["headcol"] = hc
    sel = np.zeros((HEADS, 2, P), np.float32)
    for g in range(2):
        sel[g * HQ + p // HD, g, p] = -1.0
    c["negsel"] = sel.reshape(HEADS, 2 * P)
    return c


def attn(nc, x_in, x1, x2, xs, ys, w, t_scr, f_scr, table, pool_sems):
    cst = w
    with ExitStack() as ctx:
        def last(name, shape, dt=F32):
            return ctx.enter_context(nc.sbuf_tensor(f"at_{name}", shape, dt))

        kept = []

        psum = [ctx.enter_context(nc.psum_tensor(f"at_bank{i}", [P, 512], F32)) for i in range(8)]

        wq, wk, wv, wo = (last(n, [P, KCH, DIM]) for n in ("wq", "wk", "wv", "wo"))
        nw, rw = last("nw", [P, KCH]), last("rw", [P, KCH, EXPERTS])
        wcat = last("wcat", [P, KCH, FG])
        wrank = last("wrank", [P, DIM])
        ident, headsum, headcol = last("ident", [P, P]), last("headsum", [P, P]), last("headcol", [P, HD])
        epsk, eps4 = last("epsk", [P, 1]), last("eps4", [P, 1])
        mask = last("mask", [P, UN * GS])
        lasting = Routing.lasting(last, cst)
        k, q, kb, v, gt = (last(n, [P, CHAINS, PT]) for n in ("k", "q", "kb", "v", "gt"))
        eg, ek = last("eg", [P, CHAINS, UN * GS]), last("ek", [P, CHAINS, UN * GS])
        lf = ek
        S = last("S", [P, CHAINS, HD])
        ta = last("ta", [P, UN, CHAINS, SUB + CT])

        for n in ("w", "init", "half", "x1", "stat", "st", "in0", "in1"):
            kept.append(ctx.enter_context(nc.semaphore(f"at_{n}")))
        s_w, s_init, s_half, s_x1, s_stat, s_st, *s_x = kept
        begin = ctx.enter_context(ExitStack())
        first_rows = {n: begin.enter_context(nc.sbuf_tensor(f"begin_{n}", [P, BATCH * PT // P, DIM], F32)) for n in ("xa", "ya", "yb")}
        first_rows["stats"] = begin.enter_context(nc.sbuf_tensor("begin_stats", [P, BATCH * PT // P, 6], F32))
        with nc.Block() as block:

            @block.sync
            def _(sp):
                for b in range(BATCH):
                    for n, src, row in (("xa", x_in, 0), ("ya", ys, 0), ("yb", ys, TOKENS)):
                        sp.dma_start(first_rows[n][:, 2 * b:2 * b + 2, :], token_rows(src, row + b * SEQ, PT // P)).then_inc(s_x[b // 2], 16)
                for dst, src in ((wq, "wq"), (wk, "wk"), (wv, "wv"), (wo, "wo"), (wcat, "wcat"), (rw, "rwt")):
                    sp.dma_start(dst[:, :, :], w[src]).then_inc(s_w, 16)
                sp.dma_start(wrank[0:RANK, :], w["wf2"]).then_inc(s_w, 16)
                sp.dma_start(wrank[RANK:2 * RANK, :], w["wog2"]).then_inc(s_w, 16)
                sp.dma_start(wrank[2 * RANK:FG, :], cst["negsel"]).then_inc(s_w, 16)
                sp.dma_start(nw[:, :], w["nw"]).then_inc(s_w, 16)
                for dst, src in ((ident, "ident"), (headsum, "headsum"), (headcol, "headcol")):
                    sp.dma_start(dst[:, :], cst[src]).then_inc(s_w, 16)
                Routing.load(sp, lasting, cst, s_w)
                for b in range(BATCH):
                    sp.wait_ge(s_x1, b // 2 + 1)
                    sp.dma_start(token_rows(x1, b * SEQ, PT // P), first_rows["xa"][:, 2 * b:2 * b + 2, :]).then_inc(s_st, 16)
                sp.wait_ge(s_st, 16 * BATCH)

            @block.vector
            def _(dve):
                dve.memset(epsk[:, :], EPS)
                dve.memset(eps4[:, :], 4 * EPS)
                dve.memset(mask[:, :], 1.0).then_inc(s_init, 1)
                dve.wait_ge(s_init, 1)
                dve.memset(mask[:, :].rearrange("p (u s) -> p u s", s=GS)[:, :, 0:1], 0.0)
                dve.memset(S[:, :, :], 0.0)
                xa, ya, yb, stats = (first_rows[n] for n in ("xa", "ya", "yb", "stats"))
                for h in range(2):
                    t = slice(h * BATCH * PT // P // 2, (h + 1) * BATCH * PT // P // 2)
                    dve.wait_ge(s_x[h], 16 * 3 * BATCH // 2)
                    dve.tensor_tensor(xa[:, t, :], xa[:, t, :], ya[:, t, :], ALU.add).then_inc(s_half, 1)
                    dve.wait_ge(s_half, h + 1)
                    dve.tensor_tensor(xa[:, t, :], xa[:, t, :], yb[:, t, :], ALU.add).then_inc(s_x1, 1)
                    dve.wait_ge(s_x1, h + 1)
                    for i in range(t.start, t.stop):
                        dve.bn_stats(stats[:, i, :], xa[:, i, :]).then_inc(s_stat, 1)
                dve.wait_ge(s_w, 16 * 17)
                for t in (wq, wk, wv):
                    dve.tensor_scalar(t[:, :, :], t[:, :, :], 0.5, None, ALU.mult)
                for c in range(KCH):
                    dve.tensor_scalar(wo[:, c, :], wo[:, c, :], nw[:, c:c + 1], None, ALU.mult)
                Routing.start(dve, lasting)

        env = locals()

        def emission(tag):
            scope, sems = ExitStack(), []

            def sb(name, shape, dt=F32, at=scope):
                return at.enter_context(nc.sbuf_tensor(f"{tag}_{name}", shape, dt))

            def sem(name):
                sems.append(scope.enter_context(nc.semaphore(f"{tag}_{name}")))
                return sems[-1]

            return scope, sb, sem, sems

        def routing(sb, sem, banks):
            return Routing(lasting, sb, sem, banks, rw, ident, 1)

        def rows(sb, z, begins):
            b = dict.fromkeys(("o", "xr", "xa", "ya", "yb", "stats"))
            b["o"], b["xr"] = sb("o", [P, CHAINS, PT], at=z), sb("xr", [P, BATCH * PT // P, DIM], at=z)
            if begins:
                b.update({n: sb(n, [P, BATCH * PT // P, DIM], at=z) for n in ("xa", "ya", "yb")})
                b["stats"] = sb("stats", [P, BATCH * PT // P, 6], at=z)
            return b

        def one(tag, s, nxt):
            scope, sb, sem, sems = emission(tag)
            with scope:
                decays_and_triangles(nc, sb, sem, psum, s, env)
                with ExitStack() as z:
                    b = rows(sb, z, nxt is not None)
                    scan(nc, sb, sem, psum, s, env, b, nxt)
                    between(nc, sb, sem, psum, s, nxt, env, b, routing)
                clear(nc, sems)

        scope, sb, sem, sems = emission("begin")
        with scope:
            between(nc, sb, sem, psum, None, 0, env, {"o": None, "xr": None, **first_rows}, routing)
            clear(nc, sems)
        begin.close()
        with nc.Fori(0, PASSES - 1) as s:
            one("pass", s, s + 1)
        one("end", PASSES - 1, None)
        clear(nc, kept)


def between(nc, sb, sem, psum, prev, nxt, env, z, routing):
    (x2, xs, wq, wk, wv, wo, wcat, wrank, ident, headsum, epsk, eps4, k, q, kb, v, gt, lf, table, pool_sems) = (
        env[n] for n in ("x2 xs wq wk wv wo wcat wrank ident headsum epsk eps4 k q kb v gt lf table pool_sems").split())
    o, xr, xa, ya, yb, stats = (z[n] for n in ("o", "xr", "xa", "ya", "yb", "stats"))
    ends, begins = prev is not None, nxt is not None
    NT = BATCH * PT // P
    JOBS = [(wh, g, c) for wh in range(4) for g in range(2) for c in range(2)]
    NKQV = 12
    EARLY = 2
    QUARTERS = [(g, c) for g in range(2) for c in range(2)]

    def both(t, g, c):
        return t[:, g * BATCH + 2 * c:g * BATCH + 2 * c + 2, :].rearrange("p c t -> p (c t)")

    def rows(t, n, b, first=0):
        return t[bass.ds(first + b * SEQ + n * PT, PT), :].rearrange("(i p) d -> p i d", p=P)

    with ExitStack() as scope:
        def tb(name, shape, dt=F32):
            return sb(name, shape, dt, at=scope)

        mean, var, rstd, dm = (tb(n, [P, NT]) for n in ("mean", "var", "rstd", "dm"))
        xT = tb("xT", [P, KCH, BATCH * PT])
        fg = tb("fg", [FG, BATCH * PT])
        th, sqy, ry, rn = ([tb(f"{n}{i}", [P, 512]) for i in range(2)] for n in ("th", "sqy", "ry", "rn"))
        sqk, lg = ([tb(f"{n}{i}", [P, 512]) for i in range(4)] for n in ("sqk", "lg"))
        xn = ya

        s_st = sem("st")
        s_var, s_std, s_xn, s_dve, s_tr, s_xt = (sem(n) for n in ("var", "std", "xn", "dve", "tr", "xt"))
        s_fg, s_fgc, s_bt, s_beta = sem("fg"), sem("fgc"), sem("bt"), sem("beta")
        s_mm, s_th, s_ev, s_gt = sem("mm"), sem("th"), sem("ev"), sem("gt")
        s_y, s_sqy, s_ssy, s_ly, s_ry, s_yn, s_wo, s_out = (sem("y" + n) for n in ("y", "sq", "ss", "l", "r", "n", "wo", "out"))
        s_f, s_a, s_e, s_l, s_lf, s_zero = (sem(n) for n in ("f", "a", "e", "l", "lf", "lz"))
        s_sq, s_ss, s_n1, s_n2, s_kn, s_bb, s_kb = (sem(n) for n in ("sq", "ss", "n1", "n2", "kn", "bb", "kb"))
        r = None
        if ends:
            r = routing(lambda n, sh, dt=F32: sb("r_" + n, sh, dt, at=scope), sem, [psum[i] for i in (0, 1, 2, 2, 3, 0)])
            if not begins:
                empty = tb("empty", [P, EXPERTS + SPARE_TILES, XW])

        with nc.Block() as block:

            @block.sync
            def _(sp):
                stores = 0
                if ends:
                    for b in range(BATCH):
                        sp.wait_ge(s_out, 2 * b + 2)
                        sp.dma_start(rows(x2, prev, b), xr[:, 2 * b:2 * b + 2, :]).then_inc(s_st, 16)
                        stores += 16
                if not begins:
                    table.tails(sp, empty, xs, s_st)
                    stores += 16 * EXPERTS
                if stores:
                    sp.wait_ge(s_st, stores)

            @block.gpsimd
            def _(pool):
                if ends:
                    for j, (g, c) in enumerate(QUARTERS):
                        pool.wait_ge(s_y, j + 1)
                        if j >= 2:
                            pool.wait_ge(s_ssy, j - 1)
                        pool.tensor_tensor(sqy[j % 2][:, :], both(o, g, c), both(o, g, c), ALU.mult).then_inc(s_sqy, 1)
                if begins:
                    for j, (g, c) in enumerate(QUARTERS):
                        pool.wait_ge(s_ev, j + 1)
                        pool.tensor_tensor(sqk[j][:, :], both(k, g, c), both(k, g, c), ALU.mult).then_inc(s_sq, 1)
                if ends:
                    if not begins:
                        table.empty(pool, empty, r.part[:, 0:1])
                    pool.wait_ge(r.s_rows, 1)
                    for i in range(GT):
                        for c in range(TOPK):
                            r.scatter(pool, 0, i, c, xs, pool_sems["scat"])
                    pool.wait_ge(pool_sems["scat"], (prev + 1) * (16 * TOPK * GT))

            @block.tensor
            def _(pe):
                def job(j):
                    wh, g, c = JOBS[j]
                    bank = psum[4 + j % 4]
                    if j >= 4:
                        pe.wait_ge(s_ev, j - 3)
                    else:
                        pe.wait_ge(s_lf, j + 1)
                    if j < NKQV:
                        for kc in range(KCH):
                            t = pe.matmul(bank[:, :], (wk, wq, wv)[wh][:, kc, g * P:(g + 1) * P], xT[:, kc, c * 512:(c + 1) * 512],
                                          start=(kc == 0), stop=(kc == KCH - 1))
                    else:
                        t = pe.matmul(bank[:, :], wrank[RANK:2 * RANK, g * P:(g + 1) * P], fg[RANK:2 * RANK, c * 512:(c + 1) * 512], start=True, stop=True)
                    t.then_inc(s_mm, 1)

                for j in range(4):
                    if ends:
                        pe.wait_ge(s_sqy, j + 1)
                        pe.matmul(psum[4 + j][:, :], headsum[:, :], sqy[j % 2][:, :], start=True, stop=True).then_inc(s_ssy, 1)
                    for i in range(2 * j, 2 * j + 2) if begins else ():
                        pe.wait_ge(s_xn, i + 1)
                        if i >= 2:
                            pe.wait_ge(s_xt, i - 1)
                        for c in range(KCH):
                            t = pe.transpose(psum[i % 2][:, c * P:(c + 1) * P], xn[:, i, c * P:(c + 1) * P], ident[:, :])
                        t.then_inc(s_tr, 1)
                if begins:
                    pe.wait_ge(s_xt, NT)
                    for c in range(2):
                        for kc in range(KCH):
                            t = pe.matmul(psum[2 + c][0:FG, :], wcat[:, kc, :], xT[:, kc, c * 512:(c + 1) * 512],
                                          start=(kc == 0), stop=(kc == KCH - 1))
                        t.then_inc(s_fg, 1)
                    pe.wait_ge(s_fgc, 2)
                    for j, (g, c) in enumerate(QUARTERS):
                        if ends:
                            pe.wait_ge(s_ly, j + 1)
                        pe.matmul(psum[4 + j][:, :], wrank[0:RANK, g * P:(g + 1) * P], fg[0:RANK, c * 512:(c + 1) * 512],
                                  start=True, stop=True).then_inc(s_f, 1)
                if ends:
                    pe.wait_ge(s_yn, 4)
                    for i in range(NT):
                        b, half = i // 2, i % 2
                        if i >= 2:
                            pe.wait_ge(s_out, i - 1)
                        for g in range(2):
                            t = pe.matmul(psum[2 + i % 2][:, 0:DIM], o[:, g * BATCH + b, half * P:(half + 1) * P], wo[:, g, :], start=(g == 0), stop=(g == 1))
                        t.then_inc(s_wo, 1)
                if begins:
                    for j in range(2):
                        job(j)
                if ends:
                    r.gate_tensor(pe, 0)
                if begins:
                    for j in range(2, EARLY + 4):
                        job(j)
                if ends:
                    r.count_tensor(pe, 0)
                if begins:
                    for j in range(EARLY + 4, len(JOBS)):
                        job(j)
                    for j in range(4):
                        pe.wait_ge(s_sq, j + 1)
                        pe.wait_ge(s_gt, j + 1)
                        pe.matmul(psum[4 + j][:, :], headsum[:, :], sqk[j][:, :], start=True, stop=True).then_inc(s_ss, 1)
                    pe.wait_ge(s_beta, 1)
                    for j, (g, c) in enumerate(QUARTERS):
                        pe.wait_ge(s_n1, j + 1)
                        pe.matmul(psum[4 + j][:, :], wrank[2 * RANK:FG, g * P:(g + 1) * P], fg[2 * RANK:FG, c * 512:(c + 1) * 512],
                                  start=True, stop=True).then_inc(s_bb, 1)

            @block.scalar
            def _(act):
                def job(j):
                    wh, g, c = JOBS[j]
                    act.wait_ge(s_mm, j + 1)
                    if j >= NKQV:
                        if j == NKQV and ends:
                            act.wait_ge(s_y, 4)
                        act.activation(both(gt, g, c), psum[4 + j % 4][:, :], ACT.Tanh, scale=0.5).then_inc(s_gt, 1)
                        return
                    if j >= 2:
                        act.wait_ge(s_ev, j - 1)
                    act.activation(th[j % 2][:, :], psum[4 + j % 4][:, :], ACT.Tanh).then_inc(s_th, 1)

                def turn(i):
                    act.wait_ge(s_tr, i + 1)
                    act.copy(xT[:, :, i * P:(i + 1) * P], psum[i % 2][:, 0:DIM].rearrange("p (k t) -> p k t", k=KCH)).then_inc(s_xt, 1)

                if begins:
                    act.wait_ge(s_var, 1)
                    act.activation(rstd[:, :], var[:, :], ACT.Sqrt).then_inc(s_std, 1)
                if ends:
                    act.preload_act_table_set("natural_log_exp_and_others")
                for j in range(4):
                    if ends:
                        act.wait_ge(s_ssy, j + 1)
                        if j >= 2:
                            act.wait_ge(s_yn, j - 1)
                        act.activation(ry[j % 2][:, :], psum[4 + j][:, :], ACT.Ln, bias=eps4[:, 0:1], scale=1.0 / HD).then_inc(s_ly, 1)
                    if begins:
                        turn(2 * j)
                    if ends:
                        act.wait_ge(s_ly, j + 1)
                        act.activation(ry[j % 2][:, :], ry[j % 2][:, :], ACT.Exp, scale=-0.5).then_inc(s_ry, 1)
                    if begins:
                        turn(2 * j + 1)
                if begins:
                    if not ends:
                        act.preload_act_table_set("natural_log_exp_and_others")
                    for j in range(4):
                        act.wait_ge(s_f, j + 1)
                        act.activation(lg[j][:, :], psum[4 + j][:, :], ACT.Abs).then_inc(s_a, 1)
                    for j in range(4):
                        act.wait_ge(s_a, j + 1)
                        act.activation(lg[j][:, :], lg[j][:, :], ACT.Exp, scale=-1.0).then_inc(s_e, 1)
                    for j in range(4):
                        act.wait_ge(s_e, j + 1)
                        act.activation(lg[j][:, :], lg[j][:, :], ACT.Ln, bias=1.0).then_inc(s_l, 1)
                if ends:
                    r.std_scalar(act, 0)
                if begins:
                    act.activation(fg[2 * RANK:FG, :], fg[2 * RANK:FG, :], ACT.Tanh, scale=0.5).then_inc(s_bt, 1)
                    for j in range(2):
                        job(j)
                if ends:
                    r.turn_scalar(act, 0)
                if begins:
                    for j in range(2, EARLY):
                        job(j)
                if ends:
                    r.choose_scalar(act, 0)
                if begins:
                    for j in range(EARLY, len(JOBS)):
                        job(j)
                    act.preload_act_table_set("natural_log_exp_and_others")
                    for first in (0, 2):
                        two = range(first, first + 2)
                        for j in two:
                            act.wait_ge(s_ss, j + 1)
                            if j >= 2:
                                act.wait_ge(s_kn, j - 1)
                            act.activation(rn[j % 2][:, :], psum[4 + j][:, :], ACT.Ln, bias=epsk[:, 0:1]).then_inc(s_n1, 1)
                        for j in two:
                            act.wait_ge(s_n1, j + 1)
                            act.activation(rn[j % 2][:, :], rn[j % 2][:, :], ACT.Exp, scale=-0.5).then_inc(s_n2, 1)

            @block.vector
            def _(dve):
                n = [0]

                def link(ins):
                    n[0] += 1
                    ins.then_inc(s_dve, 1)
                    dve.wait_ge(s_dve, n[0])

                def silu(j):
                    wh, g, c = JOBS[j]
                    dve.wait_ge(s_th, j + 1)
                    dve.scalar_tensor_tensor(out=both((k, q, v)[wh], g, c), in0=th[j % 2][:, :], scalar=1.0, in1=psum[4 + j % 4][:, :],
                                             op0=ALU.add, op1=ALU.mult).then_inc(s_ev, 1)

                def log_f(j):
                    g, c = QUARTERS[j]
                    dve.wait_ge(s_l, j + 1)
                    dve.scalar_tensor_tensor(
                        out=lf[:, g * BATCH + 2 * c:g * BATCH + 2 * c + 2, :].rearrange("p c (u s) -> p (c u) s", s=GS)[:, :, 1:GS],
                        in0=psum[4 + j][:, :].rearrange("p (u t) -> p u t", t=CT), scalar=0.0,
                        in1=lg[j][:, :].rearrange("p (u t) -> p u t", t=CT), op0=ALU.min, op1=ALU.subtract).then_inc(s_lf, 1)

                if begins:
                    dve.memset(lf[:, :, :].rearrange("p c (u s) -> p (c u) s", s=GS)[:, :, 0:1], 0.0)
                    dve.tensor_tensor(mean[:, :], stats[:, :, 1], stats[:, :, 4], ALU.add)
                    dve.tensor_tensor(dm[:, :], stats[:, :, 1], stats[:, :, 4], ALU.subtract)
                    link(dve.tensor_tensor(var[:, :], stats[:, :, 2], stats[:, :, 5], ALU.add))
                    dve.tensor_tensor(dm[:, :], dm[:, :], dm[:, :], ALU.mult)
                    dve.tensor_scalar(mean[:, :], mean[:, :], 0.5, None, ALU.mult)
                    link(dve.tensor_scalar(var[:, :], var[:, :], 1.0 / DIM, LN_EPS, ALU.mult, ALU.add))
                    dve.scalar_tensor_tensor(out=var[:, :], in0=dm[:, :], scalar=0.25, in1=var[:, :],
                                             op0=ALU.mult, op1=ALU.add).then_inc(s_var, 1)
                if ends:
                    for g, c in QUARTERS:
                        dve.scalar_tensor_tensor(out=both(o, g, c), in0=both(gt, g, c), scalar=1.0, in1=both(o, g, c), op0=ALU.add, op1=ALU.mult).then_inc(s_y, 1)
                if begins:
                    dve.wait_ge(s_std, 1)
                    link(dve.reciprocal(rstd[:, :], rstd[:, :]))
                    for i in range(NT):
                        dve.tensor_scalar(xn[:, i, :], xa[:, i, :], mean[:, i:i + 1], rstd[:, i:i + 1],
                                          ALU.subtract, ALU.mult).then_inc(s_xn, 1)
                if ends:
                    for j, (g, c) in enumerate(QUARTERS):
                        dve.wait_ge(s_ry, j + 1)
                        dve.tensor_tensor(both(o, g, c), both(o, g, c), ry[j % 2][:, :], ALU.mult).then_inc(s_yn, 1)
                if begins:
                    for c in range(2):
                        dve.wait_ge(s_fg, c + 1)
                        dve.tensor_copy(fg[:, c * 512:(c + 1) * 512], psum[2 + c][0:FG, :]).then_inc(s_fgc, 1)
                if ends:
                    for i in range(NT + 1):
                        if i < NT:
                            dve.wait_ge(s_wo, i + 1)
                            dve.tensor_tensor(xr[:, i, :], xr[:, i, :], psum[2 + i % 2][:, 0:DIM], ALU.add).then_inc(s_out, 1)
                        if i > 0:
                            dve.wait_ge(s_out, i)
                            r.stats_vector(dve, xr, i - 1)
                        if begins and i > 0 and i % 2 == 0:
                            log_f(i // 2 - 1)
                    r.moments_vector(dve, 0)
                    r.norm_vector(dve, 0, xr)
                else:
                    for j in range(4):
                        log_f(j)
                if begins:
                    for j in range(EARLY):
                        silu(j)
                if ends:
                    r.logits_vector(dve, 0)
                    r.choose_vector(dve, 0, (lambda: [silu(j) for j in range(EARLY, EARLY + 4)]) if begins else None)
                if begins:
                    for j in range(EARLY + 4 if ends else EARLY, NKQV):
                        silu(j)
                    dve.wait_ge(s_bt, 1)
                    dve.tensor_scalar(fg[2 * RANK:FG, :], fg[2 * RANK:FG, :], 1.0, None, ALU.add).then_inc(s_beta, 1)
                    for j, (g, c) in enumerate(QUARTERS):
                        dve.wait_ge(s_n2, j + 1)
                        dve.tensor_tensor(both(k, g, c), both(k, g, c), rn[j % 2][:, :], ALU.mult).then_inc(s_kn, 1)
                        dve.wait_ge(s_kn, j + 1)
                        dve.wait_ge(s_bb, j + 1)
                        dve.tensor_tensor(both(kb, g, c), both(k, g, c), psum[4 + j][:, :], ALU.mult).then_inc(s_kb, 1)
                if ends and not begins:
                    table.vector(dve, r, tb)


def decays_and_triangles(nc, sb, sem, psum, s, env):
    (k, q, kb, lf, eg, ek, ta, mask, ident, headcol, t_scr, f_scr) = (
        env[n] for n in "k q kb lf eg ek ta mask ident headcol t_scr f_scr".split())
    NG = CHAINS * UN
    with ExitStack() as outer:
        a_sb = sb("a_sb", [P, NG, COARSE * RW], at=outer)
        fine = sb("fine", [P, HQ * FE], at=outer)
        s_tk, s_tst = sem("tk"), [sem(f"tst{i}") for i in range(2)]
        tsum = [sb(f"tsum{i}", [3 * HD, PT], at=outer) for i in range(2)]
        fsum = [sb(f"fsum{i}", [P, 2, PIECE], at=outer) for i in range(2)]
        STORES = 3 + HQ
        tk = sb("tk", [P, 3 * HQ, CT], at=outer)

        def regroup(sp, c):
            sp.wait_ge(s_tst[c % 2], 16 * STORES * (c // 2 + 1))
            for _, _, first, nb, nx, ny in FINE:
                size = nb * nx * ny
                sp.dma_start(fine[c * UN:(c + 1) * UN, HQ * first:HQ * (first + size)].rearrange("u (h x) -> u h x", h=HQ),
                             f_scr[c, :, UN * first:UN * (first + size)].rearrange("h (u x) -> u h x", u=UN)).then_inc(s_tk, 16)
            sp.dma_start(tk[c * UN:(c + 1) * UN, :, :], t_scr[c].rearrange("k (u t) -> u k t", t=CT)).then_inc(s_tk, 16)

        with ExitStack() as scope:
            def tb(name, shape):
                return sb(name, shape, at=scope)

            E = [tb(f"E{i}", [P, E_OFF[-1]]) for i in range(2)]
            gx = [tb(f"gx{i}", [P, UN * GS]) for i in range(2)]
            fd = [tb(f"fd{i}", [P, PT]) for i in range(2)]
            left = [tb(f"left{i}", [P, UN, COARSE, LW]) for i in range(2)]
            right = [tb(f"right{i}", [P, UN, COARSE, RW]) for i in range(2)]
            f_left, f_keys = ([tb(f"{n}{i}", [P, len(LEVELS) - COARSE, UN, LW]) for i in range(2)] for n in ("f_left", "f_keys"))
            f_query = [tb(f"f_query{i}", [P, len(LEVELS) - COARSE, UN, RW - LW]) for i in range(2)]
            prod = [tb(f"prod{i}", [P, 3, PT]) for i in range(2)]
            fprod = [tb(f"fprod{i}", [P, UN * FE]) for i in range(2)]

            s_gx, s_sub, s_E, s_exp, s_f = sem("gx"), sem("sub"), sem("E"), sem("exp"), sem("fd")
            s_lr, s_qr, s_kf, s_pr = sem("lr"), sem("qr"), sem("kf"), sem("pr")
            s_A, s_ts, s_tse, s_go = sem("A"), sem("ts"), sem("tse"), sem("ago")
            s_lf, s_fk, s_fq = sem("lff"), sem("fk"), sem("fq")
            s_Ae = [sem(f"Ae{i}") for i in range(4)]

            def one(t, c):
                return t[:, bass.ds(c, 1), :]

            def gview(b, lo, T, first, last):
                v = gx[b][:, :].rearrange("p (u s) -> p u s", s=GS)[:, :, lo:lo + CT]
                return v.rearrange("p u (m x) -> p u m x", x=2 * T)[:, :, :, first:last]

            def e_out(b, l, side):
                T = LEVELS[l]
                v = E[b][:, E_OFF[l]:E_OFF[l + 1]].rearrange("p (u m z e) -> p u m z e", m=8 // T, z=2, e=T + 1)
                return v[:, :, :, side, :]

            def e_keys(b, l, side):
                T = LEVELS[l]
                nb = 8 // T
                row = 2 * (T + 1)
                return bass.AP(tensor=E[b], offset=E_OFF[l] + side * (T + 1),
                               ap=[[E_OFF[-1], P], [nb * row, UN], [row, nb], [1, T], [1, 2]])

            def products(eng, b, of_q):
                for l, q, first, nb, nx, ny in FINE:
                    if q == of_q:
                        n, src = UN * nb, (f_keys, f_query)[q][b]
                        out = bass.AP(tensor=fprod[b], offset=UN * first, ap=[[UN * FE, P], [nx * ny, n], [ny, nx], [1, ny]])
                        x = bass.AP(tensor=f_left[b], offset=(l - COARSE) * n * nx, ap=[[(len(LEVELS) - COARSE) * n * nx, P], [nx, n], [1, nx], [0, ny]])
                        y = bass.AP(tensor=src, offset=(l - COARSE) * n * ny, ap=[[(len(LEVELS) - COARSE) * n * ny, P], [ny, n], [0, nx], [1, ny]])
                        i = eng.tensor_tensor(out, x, y, ALU.mult)
                return i

            def tok(t, c, T, half):
                return one(t, c).rearrange("p a (u m x) -> p (a u) m x", u=UN, x=2 * T)[:, :, :, half * T:half * T + T]

            with nc.Block() as block:

                @block.vector
                def _(dve):
                    def decay(c, b, first):
                        if not first:
                            dve.wait_ge(s_exp, c - 1)
                        dve.tensor_tensor_scan(gx[b][:, :], mask[:, :], one(lf, c).rearrange("p a t -> p (a t)"),
                                               0.0, ALU.mult, ALU.add).then_inc(s_gx, 1)
                        dve.wait_ge(s_gx, c + 1)
                        if not first:
                            dve.wait_ge(s_qr, c - 1)
                        for l, T in enumerate(LEVELS):
                            nb = 8 // T
                            mid = gview(b, 0, T, T, T + 1).to_broadcast([P, UN, nb, T + 1])
                            dve.tensor_tensor(e_out(b, l, 0), mid, gview(b, 0, T, 0, T + 1), ALU.subtract)
                            dve.tensor_tensor(e_out(b, l, 1), gview(b, 1, T, T - 1, 2 * T), mid, ALU.subtract)
                        dve.wait_ge(s_f, c + 1)
                        g17 = gx[b][:, :].rearrange("p (u s) -> p u s", s=GS)
                        dve.tensor_tensor(one(ek, c).rearrange("p a (u s) -> p (a u) s", s=GS),
                                          g17[:, :, CT:GS].to_broadcast([P, UN, GS]), g17, ALU.subtract).then_inc(s_sub, 1)

                    def keys(c, b, first):
                        dve.wait_ge(s_E, c + 1)
                        if not first:
                            dve.wait_ge(s_A, 2 * c - 2)
                            dve.wait_ge(s_fq, c - 1)
                            dve.wait_ge(s_fk, c - 1)
                        for l, T in enumerate(LEVELS):
                            nb = 8 // T
                            to = (left[b][:, :, l, :], right[b][:, :, l, 0:LW]) if l < COARSE else (f_left[b][:, l - COARSE, :, :], f_keys[b][:, l - COARSE, :, :])
                            for dst, t, half in ((to[0], k, 0), (to[1], kb, 1)):
                                i = dve.tensor_tensor(dst.rearrange("p u (m t r) -> p u m t r", m=nb, r=2),
                                                      tok(t, c, T, half).unsqueeze(4).to_broadcast([P, UN, nb, T, 2]),
                                                      e_keys(b, l, half), ALU.mult)
                            if l == COARSE - 1:
                                i.then_inc(s_lr, 1)
                        i.then_inc(s_lf, 1)
                        dve.wait_ge(s_lf, c + 1)
                        if not first:
                            dve.wait_ge(s_ts, c - 1)
                        products(dve, b, 0).then_inc(s_fk, 1)

                    for b in range(2):
                        decay(b, b, True)
                        keys(b, b, True)
                    with dve.Fori(1, CHAINS // 2) as j:
                        for b in range(2):
                            decay(2 * j + b, b, False)
                        for b in range(2):
                            keys(2 * j + b, b, False)

                @block.gpsimd
                def _(pool):
                    def step(c, b, first):
                        pool.wait_ge(s_f, c + 1)
                        if not first:
                            pool.wait_ge(s_ts, c - 1)
                        kf, kt, qt = fd[b][:, :], one(k, c).rearrange("p a t -> p (a t)"), one(q, c).rearrange("p a t -> p (a t)")
                        pool.tensor_tensor(kf, kf, kt, ALU.mult).then_inc(s_kf, 1)
                        pool.tensor_tensor(prod[b][:, 2, :], kt, qt, ALU.mult)
                        pool.wait_ge(s_kf, c + 1)
                        pool.tensor_tensor(prod[b][:, 0, :], kf, one(kb, c).rearrange("p a t -> p (a t)"), ALU.mult)
                        pool.tensor_tensor(prod[b][:, 1, :], kf, qt, ALU.mult).then_inc(s_pr, 1)
                        pool.wait_ge(s_E, c + 1)
                        if not first:
                            pool.wait_ge(s_A, 2 * c - 2)
                            pool.wait_ge(s_fq, c - 1)
                        for l, T in enumerate(LEVELS):
                            nb = 8 // T
                            to = right[b][:, :, l, LW:RW] if l < COARSE else f_query[b][:, l - COARSE, :, :]
                            i = pool.tensor_tensor(to.rearrange("p u (m t) -> p u m t", m=nb),
                                                   tok(q, c, T, 1), e_out(b, l, 1)[:, :, :, 1:T + 1], ALU.mult)
                        i.then_inc(s_qr, 1)
                        pool.wait_ge(s_qr, c + 1)
                        pool.wait_ge(s_lf, c + 1)
                        products(pool, b, 1).then_inc(s_fq, 1)
                    for b in range(2):
                        step(b, b, True)
                    with pool.Fori(1, CHAINS // 2) as j:
                        for b in range(2):
                            step(2 * j + b, b, False)

                @block.scalar
                def _(act):
                    def exps(c, b, first):
                        if not first:
                            act.wait_ge(s_pr, c - 1)
                        act.activation(fd[b][:, :].rearrange("p (u t) -> p u t", t=CT),
                                       one(lf, c).rearrange("p a (u s) -> p (a u) s", s=GS)[:, :, 1:GS], ACT.Exp).then_inc(s_f, 1)
                        act.wait_ge(s_sub, c + 1)
                        act.activation(E[b][:, :], E[b][:, :], ACT.Exp).then_inc(s_E, 1)
                        act.activation(one(eg, c).rearrange("p a t -> p (a t)"), gx[b][:, :], ACT.Exp)
                        act.activation(one(ek, c), one(ek, c), ACT.Exp).then_inc(s_exp, 1)

                    def evac(c, b, stored):
                        for half in range(2):
                            act.wait_ge(s_A, 2 * c + half + 1)
                            act.copy(a_sb[:, bass.ds(c * UN + half * UN // 2, UN // 2), :].rearrange("p u c -> p (u c)"),
                                     psum[2 * b + half][:, 0:UN // 2 * COARSE * RW]).then_inc(s_Ae[2 * b + half], 1)
                        act.wait_ge(s_ts, c + 1)
                        if stored is not None:
                            act.wait_ge(s_tst[b], 16 * STORES * stored)
                        act.copy(tsum[b][:, :], psum[4 + b][0:3 * HD, 0:PT])
                        for e in range(2):
                            i = act.copy(fsum[b][:, e, :], psum[6 + e][:, 0:PIECE])
                        i.then_inc(s_tse, 1)
                    for b in range(2):
                        exps(b, b, True)
                    for b in range(2):
                        exps(2 + b, b, False)
                        evac(b, b, None)
                    with act.Fori(1, CHAINS // 2 - 1) as j:
                        for b in range(2):
                            exps(2 * j + 2 + b, b, False)
                            evac(2 * j + b, b, j)
                    for b in range(2):
                        evac(CHAINS - 2 + b, b, CHAINS // 2 - 1)

                @block.tensor
                def _(pe):
                    def step(j, b, first):
                        c = 2 * j + b
                        pe.wait_ge(s_lr, c + 1)
                        pe.wait_ge(s_qr, c + 1)
                        for half in range(2):
                            if not first:
                                pe.wait_ge(s_Ae[2 * b + half], j)
                            pe.sem_inc(s_go, 1)
                            for uu in range(UN // 2):
                                u = UN // 2 * half + uu
                                for h in range(HQ):
                                    r = slice(HD * h, HD * h + HD)
                                    t = pe.matmul(psum[2 * b + half][r, uu * COARSE * RW:(uu + 1) * COARSE * RW],
                                                  left[b][r, u, :, :].rearrange("p l c -> p (l c)"),
                                                  right[b][r, u, :, :].rearrange("p l c -> p (l c)"), start=True, stop=True)
                            t.then_inc(s_A, 1)
                        pe.wait_ge(s_pr, c + 1)
                        pe.wait_ge(s_fk, c + 1)
                        pe.wait_ge(s_fq, c + 1)
                        if not (isinstance(c, int) and c == 0):
                            pe.wait_ge(s_tse, c)
                        for kind in range(3):
                            pe.matmul(psum[4 + b][kind * HD:kind * HD + HD, 0:PT], headcol[:, :], prod[b][:, kind, :], start=True, stop=True)
                        for n in range(8):
                            quad = slice(n % 4 * HD, n % 4 * HD + HD)
                            t = pe.matmul(psum[6 + n // 4][quad, 0:PIECE], headcol[:, :], fprod[b][:, n * PIECE:(n + 1) * PIECE], start=True, stop=True)
                        t.then_inc(s_ts, 1)
                    for b in range(2):
                        step(0, b, True)
                    with pe.Fori(1, CHAINS // 2) as j:
                        for b in range(2):
                            step(j, b, False)

                @block.sync
                def _(sp):
                    for c in range(CHAINS):
                        if c > 0:
                            regroup(sp, c - 1)
                        sp.wait_ge(s_tse, c + 1)
                        for kind in range(3):
                            sp.dma_start(t_scr[c, HQ * kind:HQ * kind + HQ, :], tsum[c % 2][kind * HD:kind * HD + HQ, :]).then_inc(s_tst[c % 2], 16)
                        for h in range(HQ):
                            src = bass.AP(tensor=fsum[c % 2], offset=h * 2 * PIECE, ap=[[HD * 2 * PIECE, 4], [PIECE, 2], [1, PIECE]])
                            sp.dma_start(f_scr[c, h, :].rearrange("(e q x) -> q e x", e=2, q=4), src).then_inc(s_tst[c % 2], 16)

        invert(nc, outer, sb, sem, psum, env, a_sb, tk, fine, s_tk, regroup)


def invert(nc, scope, sb, sem, psum, env, a_sb, tk, fine, s_tk, regroup):
    ident, ta, mask = (env[n] for n in ("ident", "ta", "mask"))

    def tb(name, shape):
        return sb(name, shape, at=scope)

    ng, tm = tb("ng", [P, HQ * HS]), tb("tm", [P, HQ * HS])
    aq = tb("aq", [P, CT, HQ, SUB])
    zz, pr = tb("zz", [P, HQ * CT * CT]), tb("pr", [P, 3, HQ * CT * CT])

    s_zero, s_one, s_tp, s_ev, s_fine = sem("zero"), sem("one"), sem("tp"), sem("gev"), sem("fine")
    s_diag, s_aq, s_tc, s_bk, s_bke = sem("diag"), sem("aq"), sem("tc"), sem("bk"), sem("bke")
    s_inv = {"vector": sem("invV"), "pool": sem("invP")}
    SHARE = {"vector": (0, 3), "pool": (3, 4)}
    KEYS, GROUPS = 4 * COARSE, 6 * COARSE
    SIZES = (2, 4, 8, 16)
    LAST = 2 * (2 * CT - 1)
    STEPS = sum(2 * (2 * m - 1) for m in SIZES)

    def square(t):
        return t[:, :].rearrange("p (h x) -> p h x", h=HQ)[:, :, 0:SUB * SUB].rearrange("p h (j i) -> p h j i", i=SUB)

    ngv, tmv = square(ng), square(tm)
    tc = a_sb[:, :, :].rearrange("p g c -> p (g c)")[:, 0:SUB * HQ * SUB].rearrange("p (j h i) -> p j h i", j=SUB, h=HQ)

    def place(n):
        return (COARSE - 1 - n // 4, n % 4) if n < KEYS else (COARSE - 1 - (n - KEYS) // 2, 4 + n % 2)

    def runs(n):
        level, gq = place(n)
        T = LEVELS[level]
        out = []
        per = 2 * T if gq < 4 else T
        base = 4 * (gq if gq < 4 else gq - 4)
        cc = 0
        while cc < 4:
            m, xx = (base + cc) // per, (base + cc) % per
            cnt = min(4 - cc, per - xx)
            row0 = 4 * T * m + 2 * T + xx if gq < 4 else 2 * T * m + T + xx
            out.append((cc, cnt, gq >= 4, row0, 4 * T * m, 2 * T * m, 2 * T))
            cc += cnt
        return out

    def entries(f, h, nh):
        _, _, first, nb, nx, ny = f
        return bass.AP(tensor=fine, offset=HQ * first + h * nb * nx * ny, ap=[[HQ * FE, P], [nx * ny, nh * nb], [1, ny], [ny, nx]])

    def inverse(eng, name):
        h0, h1 = SHARE[name]
        done = s_inv[name]
        n = [0]

        def step(ins):
            n[0] += 1
            ins.then_inc(done, 1)
            if n[0] > 1:
                eng.wait_ge(done, n[0] - 1)

        for size, m in enumerate(SIZES):
            if size < len(LEVELS) - COARSE:
                eng.wait_ge(s_fine, size + 1)
            else:
                eng.wait_ge(s_ev, 4 * (size + 1 - len(LEVELS) + COARSE))
            blocks = (h1 - h0) * SUB // (2 * m)

            def blk(t, j0, nj, i0, ni, dj=SUB, di=1):
                return bass.AP(tensor=t, offset=h0 * HS + j0 * SUB + i0,
                               ap=[[HQ * HS, P], [2 * m * (SUB + 1), blocks], [dj, nj], [di, ni]])

            def temp(t):
                return t[:, h0 * CT * CT:h0 * CT * CT + blocks * m * m].rearrange("p (b j i) -> p b j i", b=blocks, j=m)

            z, pv = temp(zz), [temp(pr[:, i, :]) for i in range(3)]

            def product(mult, add):
                step(mult(0))
                for x in range(1, m):
                    step(mult(x))
                    if x > 1:
                        step(add(x - 1))
                step_wait()
                step(add(m - 1))
                step_wait()

            def step_wait():
                eng.wait_ge(done, n[0])

            def zmult(x):
                kk = m - 1 - x
                dst = z if x == 0 else pv[x % 3]
                return eng.tensor_tensor(dst[:, :, :, 0:kk + 1], blk(ng, m, m, kk, kk + 1, di=0), blk(tm, kk, m, 0, kk + 1, dj=0), ALU.mult)

            def zadd(x):
                kk = m - 1 - x
                return eng.tensor_tensor(z[:, :, :, 0:kk + 1], z[:, :, :, 0:kk + 1], pv[x % 3][:, :, :, 0:kk + 1], ALU.add)

            def xmult(kk):
                rows = m - kk
                out = blk(tm, m, m, 0, m) if kk == 0 else pv[kk % 3][:, :, 0:rows, :]
                return eng.tensor_tensor(out, blk(tm, m + kk, rows, m + kk, m, di=0), z[:, :, kk:kk + 1, :].to_broadcast([P, blocks, rows, m]), ALU.mult)

            def xadd(kk):
                rows = m - kk
                out = blk(tm, m + kk, rows, 0, m)
                return eng.tensor_tensor(out, out, pv[kk % 3][:, :, 0:rows, :], ALU.add)

            product(zmult, zadd)
            product(xmult, xadd)
        assert n[0] == STEPS

    with nc.Block() as block:

        @block.sync
        def _(sp):
            regroup(sp, CHAINS - 1)

        @block.tensor
        def _(pe):
            for n in range(GROUPS):
                if n >= 8:
                    pe.wait_ge(s_ev, n - 7)
                for cc in range(4):
                    col = place(n)[0] * RW + 4 * place(n)[1] + cc
                    t = pe.transpose(psum[n % 8][:, cc * P:(cc + 1) * P], a_sb[:, :, col], ident[:, :])
                t.then_inc(s_tp, 1)
            for n in range(12):
                if n == 0:
                    pe.wait_ge(s_ev, GROUPS)
                    pe.wait_ge(s_aq, 2 + HQ * (len(LEVELS) - COARSE))
                if n == 4:
                    pe.wait_ge(s_tc, 2)
                if n == 8:
                    pe.wait_ge(s_tc, 3)
                if n == 10:
                    pe.wait_ge(s_tc, 4)
                if n >= 8:
                    pe.wait_ge(s_bke, n - 7)
                for cc in range(4):
                    src = aq[:, 4 * n + cc, :, :] if n < 4 else tc[:, 4 * (n - 4) + cc, :, :]
                    t = pe.transpose(psum[n % 8][:, cc * P:(cc + 1) * P], src.rearrange("p h i -> p (h i)"), ident[:, :])
                t.then_inc(s_bk, 1)

        @block.scalar
        def _(act):
            def zeros(shape):
                return bass.AP(tensor=mask, offset=0, ap=[[UN * GS, P]] + [[0, n] for n in shape])

            def rest():
                for m in (1,) + SIZES:
                    blocks = HQ * SUB // (2 * m)
                    dst = bass.AP(tensor=tm, offset=m, ap=[[HQ * HS, P], [2 * m * (SUB + 1), blocks], [SUB, m], [1, m]])
                    act.copy(dst, zeros((blocks, m, m))).then_inc(s_zero, 1)
                act.copy(aq[:, :, :, :], zeros((CT, HQ, SUB))).then_inc(s_zero, 1)
                act.wait_ge(s_zero, len(SIZES) + 2)
                act.wait_ge(s_tk, 16 * (1 + len(FINE)) * CHAINS)
                for x in range(2):
                    dst = bass.AP(tensor=aq, offset=x, ap=[[HQ * CT * SUB, P], [SUB, HQ], [HQ * SUB + 2, CT]])
                    act.copy(dst, tk[:, (1 + x) * HQ:(2 + x) * HQ, :]).then_inc(s_aq, 1)
                for f in FINE:
                    T = LEVELS[f[0]]
                    if f[1] == 1:
                        for h in range(HQ):
                            dst = bass.AP(tensor=aq, offset=T * HQ * SUB + h * SUB, ap=[[HQ * CT * SUB, P], [2 * T * HQ * SUB + 4 * T, f[3]], [HQ * SUB, f[5]], [1, f[4]]])
                            act.copy(dst, entries(f, h, 1)).then_inc(s_aq, 1)

            for n in range(GROUPS):
                if n == KEYS:
                    rest()
                act.wait_ge(s_tp, n + 1)
                bank = psum[n % 8][:, :].rearrange("p (c h l i) -> p h c l i", c=4, h=HQ, l=COARSE)
                for cc, cnt, isq, row0, i0, l0, width in runs(n):
                    src = bank[:, :, cc:cc + cnt, place(n)[0], l0:l0 + width]
                    dst = (aq[:, :, :, :].rearrange("p t h i -> p h t i") if isq else ngv)[:, :, row0:row0 + cnt, i0:i0 + width]
                    i = act.copy(dst, src)
                i.then_inc(s_ev, 1)

            def compact(rows, cols):
                act.copy(tc[:, rows, :, cols], tmv[:, :, rows, cols].rearrange("p h j i -> p j h i")).then_inc(s_tc, 1)

            for n in range(12):
                if n == 4:
                    for e in s_inv.values():
                        act.wait_ge(e, STEPS - LAST)
                    compact(slice(0, CT), slice(0, SUB))
                    compact(slice(CT, SUB), slice(CT, SUB))
                if n == 8:
                    for e in s_inv.values():
                        act.wait_ge(e, STEPS - LAST // 2 + CT)
                    compact(slice(CT, CT + CT // 2), slice(0, CT))
                if n == 10:
                    for e in s_inv.values():
                        act.wait_ge(e, STEPS)
                    compact(slice(CT + CT // 2, SUB), slice(0, CT))
                act.wait_ge(s_bk, n + 1)
                col = SUB + 4 * n if n < 4 else 4 * (n - 4)
                act.copy(ta[:, :, :, col:col + 4].rearrange("p u c j -> p c u j"),
                         psum[n % 8][:, :].rearrange("p (j c u) -> p c u j", j=4, c=CHAINS)).then_inc(s_bke, 1)

        @block.gpsimd
        def _(pool):
            pool.wait_ge(s_one, 1)
            pool.wait_ge(s_diag, 1)
            inverse(pool, "pool")

        @block.vector
        def _(dve):
            dve.memset(tm[:, :].rearrange("p (h j s) -> p h j s", h=HQ, s=SUB + 1)[:, :, :, 0:1], 1.0).then_inc(s_one, 1)
            dve.wait_ge(s_tk, 16 * (1 + len(FINE)) * CHAINS)
            dst = bass.AP(tensor=tm, offset=SUB, ap=[[HQ * HS, P], [HS, HQ], [2 * (SUB + 1), CT]])
            dve.tensor_copy(dst, tk[:, 0:HQ, :]).then_inc(s_diag, 1)
            for f in reversed(FINE):
                T = LEVELS[f[0]]
                if f[1] == 0:
                    dst = bass.AP(tensor=ng, offset=2 * T * SUB, ap=[[HQ * HS, P], [4 * T * (SUB + 1), HQ * f[3]], [SUB, f[5]], [1, f[4]]])
                    dve.tensor_copy(dst, entries(f, 0, HQ)).then_inc(s_fine, 1)
            dve.wait_ge(s_one, 1)
            dve.wait_ge(s_diag, 1)
            inverse(dve, "vector")


def scan(nc, sb, sem, psum, s, env, z, nxt):
    k, q, kb, v, eg, ek, ta, S, x_in, x1, ys = (env[n] for n in "k q kb v eg ek ta S x_in x1 ys".split())
    o, xr, xa, ya, yb, stats = (z[n] for n in ("o", "xr", "xa", "ya", "yb", "stats"))
    NT = BATCH * PT // P
    HC = CHAINS // 2
    KQ = SUB + CT
    RO = KQ + SUB
    with ExitStack() as scope:
        def tb(name, shape):
            return sb(name, shape, at=scope)

        kq = [tb(f"kq{i}", [P, CHAINS, KQ]) for i in range(2)]
        kd = [tb(f"kd{i}", [P, CHAINS, SUB]) for i in range(2)]
        tu = [tb(f"tu{i}", [P, CHAINS, SUB]) for i in range(2)]
        ar = [tb(f"ar{i}", [P, CHAINS, KQ]) for i in range(2)]
        vi = [tb(f"vi{i}", [P, CHAINS, CT, 2]) for i in range(2)]
        Rt = [tb(f"Rt{i}", [P, HC, SUB]) for i in range(2)]
        R, U, D, dS = ([tb(f"{n}{i}", [P, HC, HD]) for i in range(2)] for n in ("R", "U", "D", "dS"))
        b_p = [psum[f][:, 0:HC * RO].rearrange("p (c x) -> p c x", c=HC) for f in range(2)]
        b_u = [psum[2 + f][:, 0:HC * HD] for f in range(2)]

        s_pad, s_go = sem("pad"), sem("go")
        s_kq, s_kd, s_kr, s_ta, s_vi = sem("kq"), sem("kd"), sem("kr"), sem("ta"), sem("vi")
        s_r, s_u, s_d, s_Rt, s_R, s_dec, s_dS, s_S, s_U, s_O = ([sem(f"{n}{f}") for f in range(2)] for n in
            ("r", "u", "d", "Rts", "Rs", "dec", "dSs", "Ss", "Us", "Os"))

        s_pre, s_nxt, s_half, s_x1, s_st, s_stat = (sem(n) for n in ("pre", "nxt", "nhalf", "nx1", "nst", "nstat"))

        def rows(t, n, b, first=0):
            return t[bass.ds(first + b * SEQ + n * PT, PT), :].rearrange("(i p) d -> p i d", p=P)

        with nc.Block() as block:

            @block.sync
            def _(sp):
                loads = [(xa, x_in, nxt, 0, s_nxt), (ya, ys, nxt, 0, s_nxt), (yb, ys, nxt, TOKENS, s_nxt)] if nxt is not None else []
                for dst, src, n, first, done in loads + [(xr, x1, s, 0, s_pre)]:
                    for b in range(BATCH):
                        sp.dma_start(dst[:, 2 * b:2 * b + 2, :], rows(src, n, b, first)).then_inc(done, 16)
                if nxt is not None:
                    sp.wait_ge(s_x1, 1)
                    for b in range(BATCH):
                        sp.dma_start(rows(x1, nxt, b), xa[:, 2 * b:2 * b + 2, :]).then_inc(s_st, 16)
                    sp.wait_ge(s_st, 16 * BATCH)
                sp.wait_ge(s_pre, 16 * BATCH)

            @block.gpsimd
            def _(pool):
                for i in range(2):
                    pool.memset(vi[i][:, :, :, 0:1], 0.0).then_inc(s_pad, 1)

                def stage(u, b, first):
                    def t(x, at=0, step=CT):
                        return x[:, :, bass.ds(u * step + at, CT)]
                    if not first:
                        pool.wait_ge(s_r[1], u - 1)
                        pool.wait_ge(s_kr, u - 1)
                        pool.wait_ge(s_Rt[1], u - 1)
                    keys = kq[b][:, :, 0:SUB].rearrange("p c (t r) -> p c t r", r=2)
                    ends = kd[b][:, :, :].rearrange("p c (t r) -> p c t r", r=2)
                    for r in range(2):
                        pool.tensor_tensor(keys[:, :, :, r], t(kb), t(eg, r, GS), ALU.mult)
                    pool.tensor_tensor(kq[b][:, :, SUB:KQ], t(q), t(eg, 1, GS), ALU.mult).then_inc(s_kq, 1)
                    pool.tensor_copy(vi[b][:, :, :, 1], t(v)).then_inc(s_vi, 1)
                    for r in range(2):
                        i = pool.tensor_tensor(ends[:, :, :, r], t(k), t(ek, r, GS), ALU.mult)
                    i.then_inc(s_kd, 1)
                for b in range(2):
                    stage(b, b, True)
                with pool.Fori(1, UN // 4) as j:
                    for b in range(2):
                        stage(2 * j + b, b, False)
                if nxt is not None:
                    pool.wait_ge(s_nxt, 16 * 3 * BATCH)
                    pool.tensor_tensor(xa[:, :, :], xa[:, :, :], ya[:, :, :], ALU.add).then_inc(s_half, 1)
                    pool.wait_ge(s_half, 1)
                    pool.tensor_tensor(xa[:, :, :], xa[:, :, :], yb[:, :, :], ALU.add).then_inc(s_x1, 1)
                with pool.Fori(UN // 4, UN // 2) as j:
                    for b in range(2):
                        stage(2 * j + b, b, False)

            @block.tensor
            def _(pe):
                def step(u, b, first):
                    def tiles(product):
                        for c in range(HC):
                            for h in range(HQ):
                                i = product(c, slice(HD * h, HD * h + HD))
                        return i
                    for f in range(2):
                        ch = HC * f
                        if f == 0:
                            pe.wait_ge(s_kq, u + 1)
                        if not (isinstance(u, int) and u == 0):
                            pe.wait_ge(s_S[f], u)
                            pe.wait_ge(s_O[f], u)
                        pe.sem_inc(s_go, 1)
                        tiles(lambda c, r: pe.matmul(b_p[f][r, c, 0:KQ], S[r, ch + c, :], kq[b][r, ch + c, :],
                                                     start=(c == 0), stop=False, skip_group_check=True)).then_inc(s_r[f], 1)
                    for f in range(2):
                        ch = HC * f
                        if f == 0:
                            pe.wait_ge(s_ta, u + 1)
                        pe.wait_ge(s_R[f], u + 1)
                        pe.sem_inc(s_go, 1)
                        tiles(lambda c, r: pe.matmul(b_u[f][r, c * HD:(c + 1) * HD], tu[b][r, ch + c, :], R[f][r, c, :],
                                                     start=True, stop=True)).then_inc(s_u[f], 1)
                    for f in range(2):
                        ch = HC * f
                        if f == 0:
                            pe.wait_ge(s_kr, u + 1)
                        pe.wait_ge(s_U[f], u + 1)
                        pe.sem_inc(s_go, 1)
                        tiles(lambda c, r: pe.matmul(b_p[f][r, c, SUB:RO], U[f][r, c, :], ar[b][r, ch + c, :],
                                                     start=False, stop=(c == HC - 1), skip_group_check=True)).then_inc(s_d[f], 1)
                for b in range(2):
                    step(b, b, True)
                with pe.Fori(1, UN // 2) as j:
                    for b in range(2):
                        step(2 * j + b, b, False)

            @block.scalar
            def _(act):
                def stage(u, b, first):
                    if not first:
                        act.wait_ge(s_d[1], u - 1)
                    row = ta[:, bass.ds(u, 1), :, :].rearrange("p a c j -> p (a c) j")
                    act.copy(tu[b][:, :, :], row[:, :, 0:SUB])
                    act.copy(ar[b][:, :, 0:CT], row[:, :, SUB:KQ]).then_inc(s_ta, 1)

                def step(u, b, first, last):
                    for f in range(2):
                        act.wait_ge(s_u[f], u + 1)
                        if not (isinstance(u, int) and u == 0):
                            act.wait_ge(s_d[f], u)
                        act.copy(U[f][:, :, :].rearrange("p c v -> p (c v)"), b_u[f]).then_inc(s_U[f], 1)
                    for f in range(2):
                        act.wait_ge(s_dS[f], u + 1)
                        act.copy(o[:, HC * f:HC * f + HC, bass.ds(u * CT, CT)], b_p[f][:, :, SUB:KQ]).then_inc(s_O[f], 1)
                    if not last:
                        stage(u + 2, b, False)
                for b in range(2):
                    stage(b, b, True)
                for b in range(2):
                    step(b, b, True, False)
                with act.Fori(1, UN // 2 - 1) as j:
                    for b in range(2):
                        step(2 * j + b, b, False, False)
                for b in range(2):
                    step(UN - 2 + b, b, False, True)

            @block.vector
            def _(dve):
                def turn(u, b):
                    dve.wait_ge(s_kd, u + 1)
                    dve.transpose(ar[b][:, :, CT:KQ], kd[b][:, :, :]).then_inc(s_kr, 1)

                def step(u, b, last, statistics=()):
                    for f in range(2):
                        ch = slice(HC * f, HC * f + HC)
                        if f == 0:
                            dve.wait_ge(s_vi, u + 1)
                        dve.wait_ge(s_r[f], u + 1)
                        dve.tensor_tensor(Rt[f][:, :, :], vi[b][:, ch, :, :].rearrange("p c t r -> p c (t r)"),
                                          b_p[f][:, :, 0:SUB], ALU.add).then_inc(s_Rt[f], 1)
                        dve.wait_ge(s_Rt[f], u + 1)
                        dve.transpose(R[f][:, :, :], Rt[f][:, :, :]).then_inc(s_R[f], 1)
                        if not (isinstance(u, int) and u == 0):
                            dve.wait_ge(s_S[f], u)
                        dve.tensor_tensor(D[f][:, :, :], S[:, ch, :], eg[:, ch, bass.ds(u * GS + CT, 1)].to_broadcast([P, HC, HD]), ALU.mult).then_inc(s_dec[f], 1)
                    if not last:
                        turn(u + 1, 1 - b)
                    for i in statistics:
                        dve.bn_stats(stats[:, i, :], xa[:, i, :]).then_inc(s_stat, 1)
                    for f in range(2):
                        ch = slice(HC * f, HC * f + HC)
                        dve.wait_ge(s_d[f], u + 1)
                        dve.transpose(dS[f][:, :, :], b_p[f][:, :, KQ:RO]).then_inc(s_dS[f], 1)
                        dve.wait_ge(s_dec[f], u + 1)
                        dve.wait_ge(s_dS[f], u + 1)
                        dve.tensor_tensor(S[:, ch, :], D[f][:, :, :], dS[f][:, :, :], ALU.add).then_inc(s_S[f], 1)
                dve.wait_ge(s_pad, 2)
                turn(0, 0)
                step(0, 0, False)
                step(1, 1, False)
                with dve.Fori(1, UN // 2 - 1) as j:
                    for b in range(2):
                        step(2 * j + b, b, False)
                tiles = range(NT) if nxt is not None else ()
                if nxt is not None:
                    dve.wait_ge(s_x1, 1)
                step(UN - 2, 0, False, tiles[:NT // 2])
                step(UN - 1, 1, True, tiles[NT // 2:])
                if nxt is not None:
                    dve.wait_ge(s_stat, NT)


def pool_dma_semaphores(nc, ctx, tag):
    return {n: ctx.enter_context(nc.semaphore(f"{tag}_{n}")) for n in ("scat", "out0", "out1")}


def macaron(nc, a, x, out):
    def scratch(name, shape):
        return nc.dram_tensor(name, shape, F32, kind="Internal").ap()

    with ExitStack() as ctx:
        pool_sems = [pool_dma_semaphores(nc, ctx, tag) for tag in ("pool1", "pool2")]
        x1, x2 = scratch("x1", [TOKENS, DIM]), scratch("x2", [TOKENS, DIM])
        xs, ys = scratch("xs", [XS_ROWS, XW]), scratch("ys", [YS_ROWS, DIM])
        ffn_first(nc, "ffn1", x, a, xs, ys, pool_sems[0])

        def sb(name, shape, dt=F32):
            return ctx.enter_context(nc.sbuf_tensor(f"table_{name}", shape, dt))

        table = Table(sb, lambda n: ctx.enter_context(nc.semaphore(f"table_{n}")))
        attn(nc, x, x1, x2, xs, ys, a, scratch("t", [CHAINS, 3 * HQ, PT]), scratch("f", [CHAINS, HQ, UN * FE]), table, pool_sems[1])
        ffn_second(nc, "ffn2", a, table, x2, out, xs, ys, pool_sems[1])


def layouts(i):
    def chunks(w):
        return w.reshape(KCH, P, -1).transpose(1, 0, 2)

    w = {n: i["L0_attn_" + n] for n in "Wq Wk Wv Wf1 Wf2 Wbeta Wog1 Wog2 norm_w Wo".split()}
    return {
        "x": i["L0_attn_x"].reshape(TOKENS, DIM),
        "wq": chunks(w["Wq"]), "wk": chunks(w["Wk"]), "wv": chunks(w["Wv"]), "wo": chunks(w["Wo"]),
        "wcat": chunks(np.concatenate([w["Wf1"], w["Wog1"], w["Wbeta"]], 1)),
        "wf2": w["Wf2"], "wog2": w["Wog2"], "nw": w["norm_w"].reshape(KCH, P).T,
        "w1t": i["L0_ffn_w1"].transpose(0, 2, 1).reshape(EXPERTS, KCH, P, 2 * INNER).transpose(0, 2, 1, 3),
        "w2t": i["L0_ffn_w2"].transpose(0, 2, 1).reshape(EXPERTS, ICH, P, DIM).transpose(0, 2, 1, 3),
        "rwt": i["L0_ffn_router_w"].T.reshape(KCH, P, EXPERTS).transpose(1, 0, 2),
        **ffn_constants(), **attn_constants(),
    }


def kernel(**inputs):
    import concourse.bacc as _bacc
    from concourse.bass_utils import run_bass_kernel_spmd as _run

    nc = _bacc.Bacc("TRN2", target_bir_lowering=False, num_devices=1)
    arrays, aps = {}, {}
    for name, a in layouts({k: np.asarray(v) for k, v in inputs.items()}).items():
        a = np.ascontiguousarray(a)
        arrays[f"in_{name}_dram"] = a
        aps[name] = nc.dram_tensor(f"in_{name}_dram", a.shape, mybir.dt.from_np(a.dtype), kind="ExternalInput").ap()
    out = nc.dram_tensor("out_0_dram", (TOKENS, DIM), F32, kind="ExternalOutput").ap()
    macaron(nc, aps, aps["x"], out)
    r = _run(nc, [arrays], core_ids=[0])
    return r.results[0]["out_0_dram"].reshape(BATCH, SEQ, DIM)
```
